# Optimizing a Trainium2 kernel written in Bass

```python
import numpy as np
import jax
import jax.numpy as jnp

def _softmax(x, axis=-1):
    return jax.nn.softmax(x, axis=axis)

def _gelu(x):
    return jax.nn.gelu(x, approximate=True)

def _silu(x):
    return jax.nn.silu(x)

def _sigmoid(x):
    return jax.nn.sigmoid(x)

def _layernorm(x, axis=-1, eps=1e-05):
    m = jnp.mean(x, axis=axis, keepdims=True)
    v = jnp.var(x, axis=axis, keepdims=True)
    return (x - m) / jnp.sqrt(v + eps)

def _scatter_add(tgt, idx, src, axis=0):
    return tgt.at[idx].add(src)

def _segment_sum(src, seg, n):
    return jax.ops.segment_sum(src, seg, n)
kernel_name = 'mk_conv_attn_hybrid_d4_conv_nchw128_r4_25f6aa'

def setup_inputs(seed: int=0):
    np.random.seed(seed)
    _w = jnp.asarray

    def _rec_inputs():
        import jax
        import jax.numpy as jnp
        _gk = jax.random.key(seed)
        x = 7.22e-05 + 1 * jax.random.normal(jax.random.fold_in(_gk, 1), (16, 32, 16, 16), jnp.float32)
        return x
    x = _rec_inputs()

    def _L0_conv_setup():
        import jax, jax.numpy as jnp
        import numpy as np
        B, C, H, W = (16, 32, 16, 16)

        def _pool2x2(t):
            b, c, h, w = t.shape
            return t.reshape(b, c, h // 2, 2, w // 2, 2).max(axis=(3, 5))
        key = jax.random.key(seed)
        ks = jax.random.split(key, 6)
        return {'x': jax.random.normal(ks[0], (B, C, H, W), dtype=jnp.float32), 'w_theta': jax.random.normal(ks[1], (C // 8, C), dtype=jnp.float32) * (1.0 / np.sqrt(C)), 'w_phi': jax.random.normal(ks[2], (C // 8, C), dtype=jnp.float32) * (1.0 / np.sqrt(C)), 'w_g': jax.random.normal(ks[3], (C // 2, C), dtype=jnp.float32) * (1.0 / np.sqrt(C)), 'w_o': jax.random.normal(ks[4], (C, C // 2), dtype=jnp.float32) * (1.0 / np.sqrt(C // 2)), 'gamma': jax.random.uniform(ks[5], (1,), dtype=jnp.float32)}
    _L0_conv_all = _L0_conv_setup()
    _L0_conv_in = {k: v for k, v in _L0_conv_all.items() if k in ('w_theta', 'w_phi', 'w_g', 'w_o', 'gamma')}
    del _L0_conv_all

    def _L1_conv_setup():
        import jax, jax.numpy as jnp
        import numpy as np
        D_CONV = 4
        D_STATE = 16
        GROUP = 8

        def _ln(x, g, b):
            mu = x.mean(-1, keepdims=True)
            v = ((x - mu) ** 2).mean(-1, keepdims=True)
            return (x - mu) * jax.lax.rsqrt(v + 1e-05) * g + b

        def _mamba(x, W_in, conv_w, conv_b, W_x, W_dt, b_dt, A_log, D_skip, W_out):
            B, L, Dm = x.shape
            d_inner = W_in.shape[0] // 2
            dt_rank = W_dt.shape[1]
            xz = x @ W_in.T
            xi, z = (xz[..., :d_inner], xz[..., d_inner:])
            xc = jax.lax.conv_general_dilated(xi.transpose(0, 2, 1), conv_w, (1,), [(D_CONV - 1, 0)], feature_group_count=d_inner, dimension_numbers=('NCH', 'OIH', 'NCH'))
            u = jax.nn.silu((xc + conv_b[:, None]).transpose(0, 2, 1))
            x_dbl = u @ W_x.T
            dt = jax.nn.softplus(x_dbl[..., :dt_rank] @ W_dt.T + b_dt)
            Bs = x_dbl[..., dt_rank:dt_rank + D_STATE]
            Cs = x_dbl[..., dt_rank + D_STATE:]
            A = -jnp.exp(A_log)

            def step(h, inp):
                dt_t, B_t, C_t, u_t = inp
                dA = jnp.exp(dt_t[..., None] * A)
                h = dA * h + (dt_t * u_t)[..., None] * B_t[:, None, :]
                return (h, jnp.einsum('bdn,bn->bd', h, C_t))
            h0 = jnp.zeros((B, d_inner, D_STATE), x.dtype)
            _, ys = jax.lax.scan(step, h0, (dt.transpose(1, 0, 2), Bs.transpose(1, 0, 2), Cs.transpose(1, 0, 2), u.transpose(1, 0, 2)))
            y = ys.transpose(1, 0, 2) + u * D_skip
            return y * jax.nn.silu(z) @ W_out.T
        key = jax.random.key(seed)
        ks = jax.random.split(key, 10)
        B, C, W, H = (4, 32, 16, 16)
        out_dim = 32
        d_inner = 2 * C
        dt_rank = (C + 15) // 16
        f = lambda k, s, sc=0.02: jax.random.normal(k, s, jnp.float32) * sc
        A_log = jnp.log(jnp.tile(jnp.arange(1, D_STATE + 1, dtype=jnp.float32), (d_inner, 1)))
        return dict(x=jax.random.normal(ks[0], (B, C, W, H), jnp.float32), gamma=jnp.ones((C,), jnp.float32), beta=jnp.zeros((C,), jnp.float32), W_in=f(ks[1], (2 * d_inner, C)), conv_w=f(ks[2], (d_inner, 1, D_CONV), 0.1), conv_b=jnp.zeros((d_inner,), jnp.float32), W_x=f(ks[3], (dt_rank + 2 * D_STATE, d_inner)), W_dt=f(ks[4], (d_inner, dt_rank), 0.1), b_dt=f(ks[5], (d_inner,), 0.5), A_log=A_log, D_skip=jnp.ones((d_inner,), jnp.float32), W_out=f(ks[6], (C, d_inner)), W_p=f(ks[7], (out_dim, C)), b_p=jnp.zeros((out_dim,), jnp.float32), s1=jnp.ones((1,), jnp.float32), s2=jnp.ones((1,), jnp.float32))
    _L1_conv_all = _L1_conv_setup()
    _L1_conv_in = {k: v for k, v in _L1_conv_all.items() if k in ('gamma', 'beta', 'W_in', 'conv_w', 'conv_b', 'W_x', 'W_dt', 'b_dt', 'A_log', 'D_skip', 'W_out', 'W_p', 'b_p', 's1', 's2')}
    del _L1_conv_all

    def _L2_attn_setup():
        import jax, jax.numpy as jnp
        import numpy as np
        EMB, HEADS, K = (32, 8, 32)
        key = jax.random.key(seed)
        ks = jax.random.split(key, 6)
        b, t, e, h = (2, 512, EMB, HEADS)
        s = 1.0 / np.sqrt(e).astype(np.float32)
        x = jax.random.normal(ks[0], (b, t, e), jnp.float32)
        Wq = jax.random.normal(ks[1], (e * h, e), jnp.float32) * s
        Wk = jax.random.normal(ks[2], (e * h, e), jnp.float32) * s
        Wv = jax.random.normal(ks[3], (e * h, e), jnp.float32) * s
        Wu = jax.random.normal(ks[4], (e, h * e), jnp.float32) * (1.0 / np.sqrt(h * e).astype(np.float32))
        bu = jnp.zeros((e,), jnp.float32)
        return {'x': x, 'Wq': Wq, 'Wk': Wk, 'Wv': Wv, 'Wu': Wu, 'bu': bu}
    _L2_attn_all = _L2_attn_setup()
    _L2_attn_in = {k: v for k, v in _L2_attn_all.items() if k in ('Wq', 'Wk', 'Wv', 'Wu', 'bu')}
    del _L2_attn_all

    def _L2_ffn_setup():
        import jax, jax.numpy as jnp
        import numpy as np
        B, N, D, C, E, K = (8, 2048, 32, 32, 8, 2)
        key = jax.random.key(seed)
        k0, k1, k2 = jax.random.split(key, 3)
        x = jax.random.normal(k0, (B, N, D), dtype=jnp.float32)
        router_w = jax.random.normal(k1, (D, E), dtype=jnp.float32) * 0.05
        router_b = jnp.zeros((E,), dtype=jnp.float32)
        expert_w = jax.random.normal(k2, (E, D, C), dtype=jnp.float32) * (1.0 / np.sqrt(D))
        expert_b = jnp.zeros((E, C), dtype=jnp.float32)
        return {'x': x, 'router_w': router_w, 'router_b': router_b, 'expert_w': expert_w, 'expert_b': expert_b}
    _L2_ffn_all = _L2_ffn_setup()
    _L2_ffn_in = {k: v for k, v in _L2_ffn_all.items() if k in ('router_w', 'router_b', 'expert_w', 'expert_b')}
    del _L2_ffn_all

    def _L3_attn_setup():
        import jax, jax.numpy as jnp
        import numpy as np
        BS = 32

        def _build_leaf_block_connectivity(edge_index, edge_values, positions, num_blocks, dtype):
            rows, cols = (edge_index[0], edge_index[1])
            br, bc = (rows // BS, cols // BS)
            in_blk = (br == bc) & (br < num_blocks)
            b_safe = jnp.where(in_blk, br, num_blocks)
            rl, cl = (rows % BS, cols % BS)
            dx = positions[cols] - positions[rows]
            ef_flat = jnp.concatenate([dx, edge_values[:, None]], axis=1).astype(dtype)
            diag = jnp.arange(BS)
            attn_mask = jnp.zeros((num_blocks + 1, BS, BS + 1), dtype)
            attn_mask = attn_mask.at[:, diag, diag].set(1.0)
            attn_mask = attn_mask.at[:, :, BS].set(1.0)
            attn_mask = attn_mask.at[b_safe, rl, cl].set(1.0)
            edge_feats = jnp.zeros((num_blocks + 1, BS, BS + 1, 4), dtype)
            edge_feats = edge_feats.at[b_safe, rl, cl].set(ef_flat)
            return (attn_mask[:num_blocks], edge_feats[:num_blocks])
        key = jax.random.key(seed)
        ks = jax.random.split(key, 10)
        N, C, E, H = (65536, 32, 1048576, 4)
        x = jax.random.normal(ks[0], (1, N, C), jnp.float32)
        rows = jax.random.randint(ks[1], (E,), 0, N, dtype=jnp.int32)
        offs = jax.random.randint(ks[2], (E,), -16, 16, dtype=jnp.int32)
        cols = jnp.clip(rows + offs, 0, N - 1)
        edge_index = jnp.stack([rows, cols], axis=0)
        edge_values = jax.random.normal(ks[3], (E,), jnp.float32)
        positions = jax.random.uniform(ks[4], (N, 3), jnp.float32)
        qkv_w = jax.random.normal(ks[5], (C, 3 * C), jnp.float32) * 0.02
        qkv_b = jnp.zeros((3 * C,), jnp.float32)
        proj_w = jax.random.normal(ks[6], (C, C), jnp.float32) * 0.02
        proj_b = jnp.zeros((C,), jnp.float32)
        gate_w = jax.random.normal(ks[7], (H, 1), jnp.float32) * 0.01
        gate_b = jnp.zeros((H,), jnp.float32)
        return {'x': x, 'edge_index': edge_index, 'edge_values': edge_values, 'positions': positions, 'qkv_w': qkv_w, 'qkv_b': qkv_b, 'proj_w': proj_w, 'proj_b': proj_b, 'gate_w': gate_w, 'gate_b': gate_b}
    _L3_attn_all = _L3_attn_setup()
    _L3_attn_in = {k: v for k, v in _L3_attn_all.items() if k in ('edge_index', 'edge_values', 'positions', 'qkv_w', 'qkv_b', 'proj_w', 'proj_b', 'gate_w', 'gate_b')}
    del _L3_attn_all

    def _L3_ffn_setup():
        import jax, jax.numpy as jnp
        import numpy as np
        NB, NOPS = (33, 19)
        D, H = (32, 128)
        B, S = (8, 256)
        CARRY_OPS = [0, 1, 2, 10, 11, 12, 13]

        def _build_masks():
            am = np.zeros((NB, NOPS), dtype=bool)
            fm = np.zeros((NB, NOPS), dtype=bool)
            fm[0, :] = True
            for b in range(1, 8):
                am[b, CARRY_OPS] = True
                fm[b, CARRY_OPS] = True
            am[8, [14, 15, 8, 9]] = True
            fm[8, [14, 15, 8, 9]] = True
            for b in range(16, 32):
                fm[b, [3, 4]] = True
            am[32, [10, 11, 12, 13]] = True
            fm[32, [5, 6, 7, 2, 4, 10, 11, 12, 13]] = True
            return (jnp.asarray(am), jnp.asarray(fm))
        key = jax.random.key(seed)
        ks = jax.random.split(key, 9)
        sd = 1.0 / np.sqrt(D)
        sh = 1.0 / np.sqrt(H)
        am, fm = _build_masks()
        return {'x': jax.random.normal(ks[0], (B, S, D), jnp.float32), 'ffn_w1': jax.random.normal(ks[1], (NB, NOPS, D, H), jnp.float32) * sd, 'ffn_b1': jnp.zeros((NB, NOPS, H), jnp.float32), 'ffn_w2': jax.random.normal(ks[2], (NB, NOPS, H, D), jnp.float32) * sh, 'ffn_b2': jnp.zeros((NB, NOPS, D), jnp.float32), 'wq': jax.random.normal(ks[3], (NB, NOPS, D, D), jnp.float32) * sd, 'wk': jax.random.normal(ks[4], (NB, NOPS, D, D), jnp.float32) * sd, 'wv': jax.random.normal(ks[5], (NB, NOPS, D, D), jnp.float32) * sd, 'wo': jax.random.normal(ks[6], (NB, NOPS, D, D), jnp.float32) * sd, 'attn_mask': am, 'ffn_mask': fm}
    _L3_ffn_all = _L3_ffn_setup()
    _L3_ffn_in = {k: v for k, v in _L3_ffn_all.items() if k in ('ffn_w1', 'ffn_b1', 'ffn_w2', 'ffn_b2', 'wq', 'wk', 'wv', 'wo', 'attn_mask', 'ffn_mask')}
    del _L3_ffn_all
    return {'x': x, 'L0_conv_w_theta': _L0_conv_in['w_theta'], 'L0_conv_w_phi': _L0_conv_in['w_phi'], 'L0_conv_w_g': _L0_conv_in['w_g'], 'L0_conv_w_o': _L0_conv_in['w_o'], 'L0_conv_gamma': _L0_conv_in['gamma'], 'L1_conv_gamma': _L1_conv_in['gamma'], 'L1_conv_beta': _L1_conv_in['beta'], 'L1_conv_W_in': _L1_conv_in['W_in'], 'L1_conv_conv_w': _L1_conv_in['conv_w'], 'L1_conv_conv_b': _L1_conv_in['conv_b'], 'L1_conv_W_x': _L1_conv_in['W_x'], 'L1_conv_W_dt': _L1_conv_in['W_dt'], 'L1_conv_b_dt': _L1_conv_in['b_dt'], 'L1_conv_A_log': _L1_conv_in['A_log'], 'L1_conv_D_skip': _L1_conv_in['D_skip'], 'L1_conv_W_out': _L1_conv_in['W_out'], 'L1_conv_W_p': _L1_conv_in['W_p'], 'L1_conv_b_p': _L1_conv_in['b_p'], 'L1_conv_s1': _L1_conv_in['s1'], 'L1_conv_s2': _L1_conv_in['s2'], 'L2_attn_Wq': _L2_attn_in['Wq'], 'L2_attn_Wk': _L2_attn_in['Wk'], 'L2_attn_Wv': _L2_attn_in['Wv'], 'L2_attn_Wu': _L2_attn_in['Wu'], 'L2_attn_bu': _L2_attn_in['bu'], 'L2_ffn_router_w': _L2_ffn_in['router_w'], 'L2_ffn_router_b': _L2_ffn_in['router_b'], 'L2_ffn_expert_w': _L2_ffn_in['expert_w'], 'L2_ffn_expert_b': _L2_ffn_in['expert_b'], 'L3_attn_edge_index': _L3_attn_in['edge_index'], 'L3_attn_edge_values': _L3_attn_in['edge_values'], 'L3_attn_positions': _L3_attn_in['positions'], 'L3_attn_qkv_w': _L3_attn_in['qkv_w'], 'L3_attn_qkv_b': _L3_attn_in['qkv_b'], 'L3_attn_proj_w': _L3_attn_in['proj_w'], 'L3_attn_proj_b': _L3_attn_in['proj_b'], 'L3_attn_gate_w': _L3_attn_in['gate_w'], 'L3_attn_gate_b': _L3_attn_in['gate_b'], 'L3_ffn_ffn_w1': _L3_ffn_in['ffn_w1'], 'L3_ffn_ffn_b1': _L3_ffn_in['ffn_b1'], 'L3_ffn_ffn_w2': _L3_ffn_in['ffn_w2'], 'L3_ffn_ffn_b2': _L3_ffn_in['ffn_b2'], 'L3_ffn_wq': _L3_ffn_in['wq'], 'L3_ffn_wk': _L3_ffn_in['wk'], 'L3_ffn_wv': _L3_ffn_in['wv'], 'L3_ffn_wo': _L3_ffn_in['wo'], 'L3_ffn_attn_mask': _L3_ffn_in['attn_mask'], 'L3_ffn_ffn_mask': _L3_ffn_in['ffn_mask']}

def reference(x, L0_conv_w_theta, L0_conv_w_phi, L0_conv_w_g, L0_conv_w_o, L0_conv_gamma, L1_conv_gamma, L1_conv_beta, L1_conv_W_in, L1_conv_conv_w, L1_conv_conv_b, L1_conv_W_x, L1_conv_W_dt, L1_conv_b_dt, L1_conv_A_log, L1_conv_D_skip, L1_conv_W_out, L1_conv_W_p, L1_conv_b_p, L1_conv_s1, L1_conv_s2, L2_attn_Wq, L2_attn_Wk, L2_attn_Wv, L2_attn_Wu, L2_attn_bu, L2_ffn_router_w, L2_ffn_router_b, L2_ffn_expert_w, L2_ffn_expert_b, L3_attn_edge_index, L3_attn_edge_values, L3_attn_positions, L3_attn_qkv_w, L3_attn_qkv_b, L3_attn_proj_w, L3_attn_proj_b, L3_attn_gate_w, L3_attn_gate_b, L3_ffn_ffn_w1, L3_ffn_ffn_b1, L3_ffn_ffn_w2, L3_ffn_ffn_b2, L3_ffn_wq, L3_ffn_wk, L3_ffn_wv, L3_ffn_wo, L3_ffn_attn_mask, L3_ffn_ffn_mask):
    import jax
    import jax.numpy as jnp

    def _L0_conv_ref(x, w_theta, w_phi, w_g, w_o, gamma):
        import jax, jax.numpy as jnp
        import numpy as np
        B, C, H, W = (16, 32, 16, 16)

        def _pool2x2(t):
            b, c, h, w = t.shape
            return t.reshape(b, c, h // 2, 2, w // 2, 2).max(axis=(3, 5))
        b, c, h, w = x.shape
        n = h * w
        m = n // 4
        theta = jnp.einsum('oc,bchw->bohw', w_theta, x).reshape(b, c // 8, n)
        phi = _pool2x2(jnp.einsum('oc,bchw->bohw', w_phi, x)).reshape(b, c // 8, m)
        g = _pool2x2(jnp.einsum('oc,bchw->bohw', w_g, x)).reshape(b, c // 2, m)
        attn = jax.nn.softmax(jnp.einsum('bcn,bcm->bnm', theta, phi), axis=-1)
        attn_g = jnp.einsum('bcm,bnm->bcn', g, attn).reshape(b, c // 2, h, w)
        o = jnp.einsum('oc,bchw->bohw', w_o, attn_g)
        return x + gamma[0] * o

    def _L1_conv_ref(x, gamma, beta, W_in, conv_w, conv_b, W_x, W_dt, b_dt, A_log, D_skip, W_out, W_p, b_p, s1, s2):
        import jax, jax.numpy as jnp
        import numpy as np
        D_CONV = 4
        D_STATE = 16
        GROUP = 8

        def _ln(x, g, b):
            mu = x.mean(-1, keepdims=True)
            v = ((x - mu) ** 2).mean(-1, keepdims=True)
            return (x - mu) * jax.lax.rsqrt(v + 1e-05) * g + b

        def _mamba(x, W_in, conv_w, conv_b, W_x, W_dt, b_dt, A_log, D_skip, W_out):
            B, L, Dm = x.shape
            d_inner = W_in.shape[0] // 2
            dt_rank = W_dt.shape[1]
            xz = x @ W_in.T
            xi, z = (xz[..., :d_inner], xz[..., d_inner:])
            xc = jax.lax.conv_general_dilated(xi.transpose(0, 2, 1), conv_w, (1,), [(D_CONV - 1, 0)], feature_group_count=d_inner, dimension_numbers=('NCH', 'OIH', 'NCH'))
            u = jax.nn.silu((xc + conv_b[:, None]).transpose(0, 2, 1))
            x_dbl = u @ W_x.T
            dt = jax.nn.softplus(x_dbl[..., :dt_rank] @ W_dt.T + b_dt)
            Bs = x_dbl[..., dt_rank:dt_rank + D_STATE]
            Cs = x_dbl[..., dt_rank + D_STATE:]
            A = -jnp.exp(A_log)

            def step(h, inp):
                dt_t, B_t, C_t, u_t = inp
                dA = jnp.exp(dt_t[..., None] * A)
                h = dA * h + (dt_t * u_t)[..., None] * B_t[:, None, :]
                return (h, jnp.einsum('bdn,bn->bd', h, C_t))
            h0 = jnp.zeros((B, d_inner, D_STATE), x.dtype)
            _, ys = jax.lax.scan(step, h0, (dt.transpose(1, 0, 2), Bs.transpose(1, 0, 2), Cs.transpose(1, 0, 2), u.transpose(1, 0, 2)))
            y = ys.transpose(1, 0, 2) + u * D_skip
            return y * jax.nn.silu(z) @ W_out.T
        B, C, W, H = x.shape
        L = W * H
        x_flat = x.reshape(B, C, L).transpose(0, 2, 1)
        x1 = _ln(x_flat, gamma, beta)
        cpg = C // GROUP
        x2 = x.reshape(B, GROUP, cpg, W, H).transpose(0, 2, 1, 3, 4).reshape(B, C, L).transpose(0, 2, 1)
        x2 = _ln(x2, gamma, beta)
        m = lambda t: _mamba(t, W_in, conv_w, conv_b, W_x, W_dt, b_dt, A_log, D_skip, W_out)
        xm = m(x1) + x1 * s1 + (m(x2) + x2 * s2)
        xm = _ln(xm, gamma, beta)
        out = xm @ W_p.T + b_p
        return out.transpose(0, 2, 1).reshape(B, -1, W, H)

    def _L2_attn_ref(x, Wq, Wk, Wv, Wu, bu):
        import jax, jax.numpy as jnp
        import numpy as np
        EMB, HEADS, K = (32, 8, 32)
        b, t, e = x.shape
        h, k = (HEADS, K)
        tp = t + k - 1
        scale = e ** 0.25
        xp = jnp.pad(x, ((0, 0), (k - 1, 0), (0, 0)))
        q = (x @ Wq.T).reshape(b, t, h, e) / scale
        kk = (xp @ Wk.T).reshape(b, tp, h, e) / scale
        v = (xp @ Wv.T).reshape(b, tp, h, e)
        idx = jnp.arange(t)[:, None] + jnp.arange(k)[None, :]
        kw = kk[:, idx]
        vw = v[:, idx]
        dot = jnp.einsum('bthe,btkhe->bthk', q, kw)
        attn = jax.nn.softmax(dot, axis=-1)
        out = jnp.einsum('bthk,btkhe->bthe', attn, vw)
        out = out.reshape(b, t, h * e)
        return out @ Wu.T + bu

    def _L2_ffn_ref(x, router_w, router_b, expert_w, expert_b):
        import jax, jax.numpy as jnp
        import numpy as np
        B, N, D, C, E, K = (8, 2048, 32, 32, 8, 2)
        router_probs = jax.nn.softmax(x @ router_w + router_b, axis=-1)
        top_p, top_i = jax.lax.top_k(router_probs, K)
        top_p = top_p / jnp.sum(top_p, axis=-1, keepdims=True)
        expert_out = jnp.einsum('bnd,edc->bnec', x, expert_w) + expert_b
        gathered = jnp.take_along_axis(expert_out, top_i[..., None], axis=2)
        return jnp.einsum('bnk,bnkc->bnc', top_p, gathered)

    def _L3_attn_ref(x, edge_index, edge_values, positions, qkv_w, qkv_b, proj_w, proj_b, gate_w, gate_b):
        import jax, jax.numpy as jnp
        import numpy as np
        BS = 32

        def _build_leaf_block_connectivity(edge_index, edge_values, positions, num_blocks, dtype):
            rows, cols = (edge_index[0], edge_index[1])
            br, bc = (rows // BS, cols // BS)
            in_blk = (br == bc) & (br < num_blocks)
            b_safe = jnp.where(in_blk, br, num_blocks)
            rl, cl = (rows % BS, cols % BS)
            dx = positions[cols] - positions[rows]
            ef_flat = jnp.concatenate([dx, edge_values[:, None]], axis=1).astype(dtype)
            diag = jnp.arange(BS)
            attn_mask = jnp.zeros((num_blocks + 1, BS, BS + 1), dtype)
            attn_mask = attn_mask.at[:, diag, diag].set(1.0)
            attn_mask = attn_mask.at[:, :, BS].set(1.0)
            attn_mask = attn_mask.at[b_safe, rl, cl].set(1.0)
            edge_feats = jnp.zeros((num_blocks + 1, BS, BS + 1, 4), dtype)
            edge_feats = edge_feats.at[b_safe, rl, cl].set(ef_flat)
            return (attn_mask[:num_blocks], edge_feats[:num_blocks])
        B, N, C = x.shape
        H = gate_b.shape[0]
        hd = C // H
        scale = hd ** (-0.5)
        nb = N // BS
        dtype = x.dtype
        attn_mask, edge_feats = _build_leaf_block_connectivity(edge_index, edge_values, positions, nb, dtype)
        x_blk = x.reshape(B, nb, BS, C)
        block_node = x_blk.mean(axis=2, keepdims=True)
        kv = jnp.concatenate([x_blk, block_node], axis=2)
        qkv_q = x_blk @ qkv_w + qkv_b
        qkv_kv = kv @ qkv_w + qkv_b
        q = qkv_q[..., :C].reshape(B, nb, BS, H, hd)
        k = qkv_kv[..., C:2 * C].reshape(B, nb, BS + 1, H, hd)
        v = qkv_kv[..., 2 * C:].reshape(B, nb, BS + 1, H, hd)
        scores = jnp.einsum('bnqhd,bnkhd->bnqkh', q, k) * scale
        diag = jnp.arange(BS)
        w_bias = edge_feats[..., 3]
        w_bias = w_bias.at[:, :, BS].set(1.0)
        w_bias = w_bias.at[:, diag, diag].set(1.0)
        scores = scores + w_bias[None, :, :, :, None]
        mask = attn_mask[None, :, :, :, None]
        neg = jnp.asarray(-1000000000.0, dtype)
        scores = jnp.where(mask == 0, neg, scores)
        attn_probs = jax.nn.softmax(scores, axis=3)
        gate = w_bias[..., None] * gate_w[:, 0] + gate_b
        gate = jnp.where(mask[0] == 0, 0.0, gate)[None]
        combined = attn_probs + gate
        out = jnp.einsum('bnqkh,bnkhd->bnqhd', combined, v).reshape(B, N, C)
        return out @ proj_w + proj_b

    def _L3_ffn_ref(x, ffn_w1, ffn_b1, ffn_w2, ffn_b2, wq, wk, wv, wo, attn_mask, ffn_mask):
        import jax, jax.numpy as jnp
        import numpy as np
        NB, NOPS = (33, 19)
        D, H = (32, 128)
        B, S = (8, 256)
        CARRY_OPS = [0, 1, 2, 10, 11, 12, 13]

        def _build_masks():
            am = np.zeros((NB, NOPS), dtype=bool)
            fm = np.zeros((NB, NOPS), dtype=bool)
            fm[0, :] = True
            for b in range(1, 8):
                am[b, CARRY_OPS] = True
                fm[b, CARRY_OPS] = True
            am[8, [14, 15, 8, 9]] = True
            fm[8, [14, 15, 8, 9]] = True
            for b in range(16, 32):
                fm[b, [3, 4]] = True
            am[32, [10, 11, 12, 13]] = True
            fm[32, [5, 6, 7, 2, 4, 10, 11, 12, 13]] = True
            return (jnp.asarray(am), jnp.asarray(fm))
        scale = jnp.asarray(1.0 / np.sqrt(D), x.dtype)

        def step(h, p):
            op = jnp.argmax(h[0, 0, :NOPS])
            q = h @ p['wq'][op]
            k = h @ p['wk'][op]
            v = h @ p['wv'][op]
            attn = jax.nn.softmax(jnp.einsum('bqd,bkd->bqk', q, k) * scale, axis=-1)
            y = jnp.einsum('bqk,bkd->bqd', attn, v) @ p['wo'][op]
            h = jnp.where(p['am'][op], y, h)
            z = jax.nn.relu(h @ p['w1'][op] + p['b1'][op]) @ p['w2'][op] + p['b2'][op]
            h = jnp.where(p['fm'][op], z, h)
            return (h, None)
        xs = {'w1': ffn_w1, 'b1': ffn_b1, 'w2': ffn_w2, 'b2': ffn_b2, 'wq': wq, 'wk': wk, 'wv': wv, 'wo': wo, 'am': attn_mask, 'fm': ffn_mask}
        out, _ = jax.lax.scan(step, x, xs)
        return out

    def _gn(v, G=32, eps=1e-05):
        B_, C_, H_, W_ = v.shape
        g = v.reshape(B_, G, C_ // G, H_, W_)
        m = jnp.mean(g, axis=(2, 3, 4), keepdims=True)
        s = jnp.var(g, axis=(2, 3, 4), keepdims=True)
        return ((g - m) / jnp.sqrt(s + eps)).reshape(v.shape)

    def _ln_c(v, eps=1e-06):
        m = jnp.mean(v, axis=1, keepdims=True)
        s = jnp.var(v, axis=1, keepdims=True)
        return (v - m) / jnp.sqrt(s + eps)

    def _ln_t(v, eps=1e-05):
        m = jnp.mean(v, axis=-1, keepdims=True)
        s = jnp.var(v, axis=-1, keepdims=True)
        return (v - m) / jnp.sqrt(s + eps)

    def _to_tokens(v):
        B_, C_, H_, W_ = v.shape
        return v.reshape(B_, C_, H_ * W_).transpose(0, 2, 1)

    def _from_tokens(t, like):
        B_, C_, H_, W_ = like.shape
        return t.transpose(0, 2, 1).reshape(B_, C_, H_, W_)
    x = _L0_conv_ref(x, L0_conv_w_theta, L0_conv_w_phi, L0_conv_w_g, L0_conv_w_o, L0_conv_gamma)
    x = x + _L1_conv_ref(_gn(x), L1_conv_gamma, L1_conv_beta, L1_conv_W_in, L1_conv_conv_w, L1_conv_conv_b, L1_conv_W_x, L1_conv_W_dt, L1_conv_b_dt, L1_conv_A_log, L1_conv_D_skip, L1_conv_W_out, L1_conv_W_p, L1_conv_b_p, L1_conv_s1, L1_conv_s2)
    t = _to_tokens(x)
    t = t + _L2_attn_ref(_ln_t(t), L2_attn_Wq, L2_attn_Wk, L2_attn_Wv, L2_attn_Wu, L2_attn_bu)
    t = t + _L2_ffn_ref(_ln_t(t), L2_ffn_router_w, L2_ffn_router_b, L2_ffn_expert_w, L2_ffn_expert_b)
    t = t + _L3_attn_ref(_ln_t(t), L3_attn_edge_index, L3_attn_edge_values, L3_attn_positions, L3_attn_qkv_w, L3_attn_qkv_b, L3_attn_proj_w, L3_attn_proj_b, L3_attn_gate_w, L3_attn_gate_b)
    t = t + _L3_ffn_ref(_ln_t(t), L3_ffn_ffn_w1, L3_ffn_ffn_b1, L3_ffn_ffn_w2, L3_ffn_ffn_b2, L3_ffn_wq, L3_ffn_wk, L3_ffn_wv, L3_ffn_wo, L3_ffn_attn_mask, L3_ffn_ffn_mask)
    x = _from_tokens(t, x)
    return x

_drawn_inputs = setup_inputs


def setup_inputs(seed=0):
    import zlib

    import numpy as np

    out = dict(_drawn_inputs(seed))
    spreads = {'L1_conv_gamma': (1.0, 0.2),
     'L1_conv_beta': (0.0, 0.1),
     'L1_conv_conv_b': (0.0, 0.8),
     'L1_conv_D_skip': (1.0, 0.6),
     'L1_conv_b_p': (0.0, 0.1),
     'L2_attn_bu': (0.0, 0.1),
     'L2_ffn_router_b': (0.0, 0.1),
     'L2_ffn_expert_b': (0.0, 0.1),
     'L3_attn_qkv_b': (0.0, 0.332),
     'L3_attn_proj_b': (0.0, 0.1),
     'L3_attn_gate_b': (0.0, 2.0),
     'L3_ffn_ffn_b1': (0.0, 0.1),
     'L3_ffn_ffn_b2': (0.0, 0.1)}
    factors = {'L1_conv_W_in': 8.0,
     'L1_conv_conv_w': 8.0,
     'L1_conv_W_x': 8.0,
     'L1_conv_W_dt': 8.0,
     'L1_conv_b_dt': 8.0,
     'L1_conv_A_log': 8.0,
     'L1_conv_W_out': 8.0,
     'L3_attn_edge_values': 30.838,
     'L3_attn_gate_w': 30.033,
     'L3_ffn_wq': 8.0,
     'L3_ffn_wk': 7.574}
    for name, (base, spread) in spreads.items():
        noise = np.random.default_rng([zlib.crc32(name.encode()), seed]).standard_normal(out[name].shape)
        drawn = base * np.exp(spread * noise) if base else spread * noise
        out[name] = jnp.asarray(drawn.astype(out[name].dtype))
    for name, factor in factors.items():
        out[name] = (out[name] * factor).astype(out[name].dtype)
    return out
```

```python
from contextlib import ExitStack

import concourse.bass as bass
from concourse import mybir

ALU = mybir.AluOpType
ACT = mybir.ActivationFunctionType
F32 = mybir.dt.float32
BF16 = mybir.dt.bfloat16
I32 = mybir.dt.int32
U32 = mybir.dt.uint32
U8 = mybir.dt.uint8
AX_X = mybir.AxisListType.X

P = 128
C = 32
G = P // C
J = 4
N = 256
NT = J * N
HALF = 512
B = G * J


def broadcast_rows(ap, rows):
    return bass.AP(ap.tensor, ap.offset, [[0, rows]] + [list(x) for x in ap.ap])


def hybrid_kernel(nc, a, out):
    with ExitStack() as ctx:
        def sb(name, shape, dt=F32):
            return ctx.enter_context(nc.sbuf_tensor(name, shape, dt))

        def sem(name):
            return ctx.enter_context(nc.semaphore(name))

        ps = ctx.enter_context(nc.psum_tensor("ps", [P, 8, HALF], F32))
        block = None

        def bank(k, n=1):
            return ps[:, k:k + n, :].rearrange("p a b -> p (a b)")

        ident = sb("ident", [P, P])
        averager = sb("averager", [P, P])
        centerer = sb("centerer", [P, P])
        permuter = sb("permuter", [P, P])
        half_mask = sb("half_mask", [P, P])
        one_row = sb("one_row", [1, P])
        one_col = sb("one_col", [P, 1])
        eps5 = sb("eps5", [P, 1])

        X = sb("X", [P, NT])
        xn = sb("xn", [P, NT])
        sq = sb("sq", [P, NT])
        rstd = sb("rstd", [P, NT])

        nat0 = sb("nat0", [P, 4, P])
        bd0 = sb("bd0", [P, 4, P])
        wo_nat = sb("wo_nat", [P, P])
        wo_bd = sb("wo_bd", [P, P])
        gamma0 = sb("gamma0", [P, 1])

        ln_g = sb("ln_g", [P, 1])
        ln_b = sb("ln_b", [P, 1])
        s1 = sb("s1", [P, 1])
        s2 = sb("s2", [P, 1])
        b_p = sb("b_p", [P, 1])
        win_nat = sb("win_nat", [P, 4, C])
        win_t = sb("win_t", [P, P])
        conv_w = sb("conv_w", [P, 4])
        conv_b = sb("conv_b", [P, 1])
        b_dt = sb("b_dt", [P, 1])
        d_skip = sb("d_skip", [P, 1])
        a_log = sb("a_log", [P, 16])
        a_neg = sb("a_neg", [P, 16])
        wx_t = sb("wx_t", [P, 34])
        wx_rows = sb("wx_rows", [2, 2, 64])
        wdt_t = sb("wdt_t", [2, 2, 64])
        w_dt = sb("w_dt", [P, P])
        w_bc = sb("w_bc", [P, 32, P])
        wout_nat = sb("wout_nat", [P, C])
        wout_t = sb("wout_t", [P, C])

        work = sb("work", [P, 23 * NT])

        def area(at, n):
            return work[:, at * NT:(at + n) * NT]

        theta = area(0, 1)
        pool_w = area(1, 1)
        phi_bd = area(2, 1).rearrange("p (j g m) -> p j g m", j=J, g=G)
        gp_bd = area(3, 1).rearrange("p (j g m) -> p j g m", j=J, g=G)
        att = area(4, 2)
        att_t = area(6, 2)
        vb = area(8, 1)
        mx0 = sb("mx0", [P, 32])
        sm0 = sb("sm0", [P, 32])
        rs0 = sb("rs0", [P, 32])
        xi_pad = work[:, 0:16 * 259].rearrange("p (b t) -> p b t", b=B)
        u_act = area(5, 4)
        z_act = area(9, 4)
        dt_act = area(13, 4)
        dtu = area(17, 4)
        tmp_a = area(21, 1)
        tmp_b = area(22, 1)
        x1 = sb("x1", [P, NT])
        x2 = sb("x2", [P, NT])
        dA = sb("dA", [P, 2, NT])
        dBu = sb("dBu", [P, 2, NT])
        hst = sb("hst", [P, 2, NT])
        hC = sb("hC", [P, 2, NT])
        yacc = sb("yacc", [P, 2, NT])
        bn6 = sb("bn6", [P, J, 6])
        bn2 = sb("bn2", [P, J, 2])
        rs4 = sb("rs4", [P, J])

        H2 = 8
        WT = N // C
        wq2 = sb("wq2", [C, H2, C])
        wk2 = sb("wk2", [C, H2, C])
        wv2 = sb("wv2", [C, H2, C])
        wu_nat = sb("wu_nat", [C, H2 * C])
        wu_t = sb("wu_t", [C, H2 * C])
        w_km = sb("w_km", [P, H2, P])
        w_vu = sb("w_vu", [P, H2 * C])
        b_u = sb("b_u", [P, 1])
        win_mask = sb("win_mask", [P, 2 * C])
        mask_bf = sb("mask_bf", [P, WT, 2 * C], BF16)
        ident_bf = sb("ident_bf", [P, P], BF16)
        zero_bf = sb("zero_bf", [P, P], BF16)
        km = area(0, 8).rearrange("p (t h k) -> p t h k", h=H2, k=C)
        s2_buf = [area(8 + k, 1) for k in range(2)]
        pt_buf = [area(10 + k, 1) for k in range(2)]
        vm_buf = [area(12, 1)[:, k * HALF:(k + 1) * HALF] for k in range(2)]
        mx2 = sb("mx2", [P, 2, 16])
        sm2 = sb("sm2", [P, 2, 16])

        E2 = 8
        r_bd = sb("r_bd", [P, G, E2])
        e_bd = x1[:, :].rearrange("p (g e) -> p g e", g=G)
        rb_row = sb("rb_row", [1, G, E2])
        eb_row = x2[0:1, :].rearrange("p (g e) -> p g e", g=G)
        rank = sb("rank", [P, E2])
        TT = 2 * J
        lg = area(16, 1)[:, 0 * N:1 * N].rearrange("p (t e) -> p t e", e=E2)
        sel_a = area(16, 1)[:, 1 * N:2 * N].rearrange("p (t e) -> p t e", e=E2)
        sel_b = area(16, 1)[:, 2 * N:3 * N].rearrange("p (t e) -> p t e", e=E2)
        gate = area(16, 1)[:, 3 * N:4 * N].rearrange("p (t e) -> p t e", e=E2)
        top1 = sb("top1", [P, TT * G])
        top2 = sb("top2", [P, TT * G])
        mix = [area(14 + k, 1) for k in range(2)]

        EDGES = a["L3_attn_edge_values"].shape[0]
        EF = EDGES // P
        EC = NT
        NCH = EF // EC
        SEG = 256
        SLOTS = 48
        CELLS = N * C
        CHUNK = 16
        GW = CHUNK
        SYMBOL = 6
        SPACE = SYMBOL + 1
        PLANES = 4
        e_row = dA[:, :, :].bitcast(I32)
        e_col = dBu[:, :, :].bitcast(I32)
        e_x = hst[:, 0, :].bitcast(I32)
        e_u = hst[:, 1, :]
        e_key = hC[:, 0, :]
        cand = hC[:, 1, 0:SEG]
        k_a = hC[:, 1, SEG:2 * SEG].bitcast(I32)
        k_b = hC[:, 1, 2 * SEG:3 * SEG].bitcast(I32)
        k_key = hC[:, 1, 3 * SEG:4 * SEG].bitcast(I32)
        seg_place = sb("seg_place", [P, SEG])
        seg_bits = yacc[:, 1, 0:SEG].bitcast(I32)
        top48 = yacc[:, 1, SEG:SEG + SLOTS]
        d_a = yacc[:, 1, 320:320 + SLOTS].bitcast(I32)
        d_b = yacc[:, 1, 384:384 + SLOTS].bitcast(I32)
        d_f = yacc[:, 1, 448:448 + SLOTS]
        d_idx = yacc[:, 1, 512:512 + SLOTS]
        d_ev = yacc[:, 1, 576:576 + SLOTS]
        d_ok = yacc[:, 1, 640:640 + SLOTS]
        d_c = yacc[:, 1, 448:448 + SLOTS].bitcast(I32)
        d_row = yacc[:, 1, 512:512 + SLOTS].bitcast(I32)
        d_col = yacc[:, 1, 576:576 + SLOTS].bitcast(I32)
        d_ok = yacc[:, 1, 640:640 + SLOTS]
        d_new = yacc[:, 1, 704:704 + SLOTS]
        d_at = yacc[:, 1, 960:960 + SLOTS]
        weighed = yacc[:, 1, 768:768 + PLANES * SLOTS].rearrange("p (s k) -> p s k", k=PLANES)
        rows_at = sb("rows_at", [P, N], BF16)
        weight = sb("weight", [P, 1], I32)
        p_base = sb("p_base", [P, 2], I32)
        g_base = sb("g_base", [P, 2, G])
        halves = lambda t: t.bitcast(BF16).rearrange("p a b -> p (a b)")
        row_hot = [halves(t[:, :, :]).rearrange("p (s r) -> p s r", r=N) for t in (dA, dBu)]
        col_hot = hC[:, 0, 0:SLOTS * C // 2].bitcast(BF16).rearrange("p (s c) -> p s c", c=C)
        plane_hot = [hst[:, k, :].bitcast(BF16).rearrange("p (s k c) -> p s k c", k=PLANES, c=C)
                     for k in range(2)]
        inv_i = hC[:, 1, 0:G * 2 * C].rearrange("p (g c) -> p g c", g=G).bitcast(I32)
        symbols = hC[:, 1, G * 2 * C:G * 2 * C * PLANES].rearrange("p (g k c) -> p g k c", g=G, c=2 * C)
        g_row = dBu[:, 0, 0:GW].bitcast(I32)
        g_col = dBu[:, 1, 0:GW].bitcast(I32)
        g_x = hC[:, 0, SLOTS * C // 2:SLOTS * C // 2 + GW].bitcast(I32)
        g_u = hC[:, 0, SLOTS * C // 2 + GW:SLOTS * C // 2 + 2 * GW]
        over = sb("over", [P, 2])
        over_i = sb("over_i", [1, 1], I32)
        tab = sb("tab", [P, 2 * C])
        tab_new = sb("tab_new", [P, 2 * C])
        tab_i = sb("tab_i", [P, 2 * C], U32)
        hit = sb("hit", [P, 2, 2, C])
        bias_dram = nc.dram_tensor("cell_bias", [2, CELLS], F32, kind="Internal").ap()

        H3 = 4
        KN = C + 1
        BL = N // C
        w_q3 = nat0[:, 0, :]
        w_k3 = nat0[:, 1, :]
        w_p3 = nat0[:, 2, :]
        w_v3 = nat0[:, 3, :].rearrange("p (h c) -> p h c", c=C)
        b_q3 = sb("b_q3", [P, 1])
        b_k3 = sb("b_k3", [P, 1])
        b_v3 = sb("b_v3", [P, 1])
        b_p3 = sb("b_p3", [P, 1])
        gate_w3 = sb("gate_w3", [P, 1])
        gate_b3 = sb("gate_b3", [P, 1])
        head_scale = sb("head_scale", [P, H3])
        b_qh = sb("b_qh", [P, H3])
        diag = sb("diag", [P, C])
        wgt = w_bc[:, 0:3, :].rearrange("p a b -> p (a b)")[:, 0:BL * KN].rearrange("p (b k) -> p b k", k=KN)
        msk = w_bc[:, 3:6, :].rearrange("p a b -> p (a b)")[:, 0:BL * KN].rearrange("p (b k) -> p b k", k=KN)
        gate3 = w_bc[:, 6:8, :].rearrange("p a b -> p (a b)").rearrange("p (b k) -> p b k", k=C)
        node_gate = sb("node_gate", [P, BL])
        k3 = work[:, 0:J * BL * KN].rearrange("p (s k) -> p s k", k=KN)
        q3 = area(2, 4).rearrange("p (s h q) -> p s h q", h=H3, q=C)
        v3 = area(6, 4)
        vm3 = area(10, 4)
        s3 = [work[:, (14 + 2 * k) * NT:(14 + 2 * k) * NT + G * BL * KN] for k in range(2)]
        a3 = [area(18 + k, 1) for k in range(2)]
        at3 = [area(20 + k, 1) for k in range(2)]
        o3 = area(22, 1)
        mx3 = sb("mx3", [P, 2, 32])
        sm3 = sb("sm3", [P, 2, 32])

        NB, NOPS = a["L3_ffn_attn_mask"].shape
        STEPS = NB * NOPS
        F = a["L3_ffn_ffn_w1"].shape[-1]
        NONE = 64
        h4 = area(0, 1)
        hid = area(1, 4)
        q4 = area(5, 1)
        k4 = area(6, 1)
        v4 = area(7, 1)
        p4 = area(8, 1)[:, 0:HALF]
        pt4 = area(9, 1)[:, 0:HALF]
        y4 = area(10, 1)
        w4 = area(11, 1)[:, 0:4 * C].rearrange("p (k c) -> p k c", c=C)
        w1_4 = area(11, 1)[:, HALF:HALF + F]
        w2_4 = area(11, 1)[:, HALF + F:HALF + F + C]
        b1_4 = area(11, 1)[:, HALF + F + C:HALF + F + C + 1]
        b2_4 = area(11, 1)[:, HALF + F + C + 8:HALF + F + C + 9]
        h_t = area(12, 1)[0:C, 0:C]
        mx4 = area(12, 1)[:, 64:66]
        nm4 = area(12, 1)[:, 72:74]
        sm4 = area(12, 1)[:, 80:82]
        flat_bc = w_bc[:, :, :].rearrange("p a b -> p (a b)")
        steps_u8 = flat_bc[0:1, 1024:1024 + 320].bitcast(U8)[:, 0:2 * STEPS]
        steps_f = flat_bc[0:1, 1408:1408 + 2 * STEPS].rearrange("p (t o) -> p t o", o=NOPS)
        picked = flat_bc[0:1, 2688:2688 + 2 * STEPS].rearrange("p (t o) -> p t o", o=NOPS)
        ops_at = sb("ops_at", [1, NB])
        ops_back = sb("ops_back", [1, NB])
        best8 = sb("best8", [1, 8])
        best8_i = sb("best8_i", [1, 8], U32)
        op_f = sb("op_f", [1, 1])
        one_hot = sb("one_hot", [1, NB])
        flags = sb("flags", [1, 2, NB])
        open_ = sb("open_", [1, NB])
        from_block = sb("from_block", [1, 1])
        found = sb("found", [1, 1])
        next_block = sb("next_block", [1, 1])
        ctrl_f = sb("ctrl_f", [1, 4])
        ctrl = sb("ctrl", [1, 4], I32)

        dma_fa = sem("dma_fa")
        dma_f = sem("dma_f")
        dma_m = sem("dma_m")
        ctrl_ready = sem("ctrl_ready")
        loop_passed = sem("loop_passed")
        step_chain = sem("step_chain")
        attn_chain = sem("attn_chain")
        ffn_pe = sem("ffn_pe")
        ffn_act = sem("ffn_act")
        attn_pe = sem("attn_pe")
        attn_act = sem("attn_act")
        attn_dve = sem("attn_dve")
        dma_e = [sem(f"dma_e{k}") for k in range(2)]
        e_used = sem("e_used")
        cols_sb = sem("cols_sb")
        rows_sb = sem("rows_sb")
        hot_sb = sem("hot_sb")
        hot_used = sem("hot_used")
        planes_ps = sem("planes_ps")
        over_sb = sem("over_sb")
        tab_dve = sem("tab_dve")
        gathered = sem("gathered")
        hit_sb = sem("hit_sb")
        bias_out = sem("bias_out")
        bias_in = sem("bias_in")
        gen_in = sem("gen_in")
        gen_slots = sem("gen_slots")
        gen_ps = sem("gen_ps")
        gen_done = sem("gen_done")
        gen_chain = sem("gen_chain")
        gen_frame = sem("gen_frame")
        gen_passed = sem("gen_passed")
        dma_w3 = sem("dma_w3")
        w3_zero = sem("w3_zero")
        qkv3_ps = sem("qkv3_ps")
        q3_sb = sem("q3_sb")
        k3_sb = sem("k3_sb")
        v3_ps = sem("v3_ps")
        v3_sb = sem("v3_sb")
        k3_node = sem("k3_node")
        vm3_sb = sem("vm3_sb")
        s3_ps = sem("s3_ps")
        s3_read = sem("s3_read")
        s3_shift = sem("s3_shift")
        s3_exp = sem("s3_exp")
        at3_sb = sem("at3_sb")
        o3_ps = sem("o3_ps")
        o3_sb = sem("o3_sb")
        p3_ps = sem("p3_ps")
        dma_w2 = sem("dma_w2")
        dma_ex = sem("dma_ex")
        ex_zero = sem("ex_zero")
        w2_zero = sem("w2_zero")
        w2_mask = sem("w2_mask")
        wu_ready = sem("wu_ready")
        w2_ps = sem("w2_ps")
        w2_sb = sem("w2_sb")
        km_ps = sem("km_ps")
        km_sb = sem("km_sb")
        s2_ps = sem("s2_ps")
        v2_ps = sem("v2_ps")
        s2_read = sem("s2_read")
        v2_sb = sem("v2_sb")
        s2_shifted = sem("s2_shifted")
        s2_exp = sem("s2_exp")
        s2_scale = sem("s2_scale")
        s2_prob = sem("s2_prob")
        p2_sb = sem("p2_sb")
        o2_ps = sem("o2_ps")
        lg_ps = sem("lg_ps")
        lg_shifted = sem("lg_shifted")
        lg_exp = sem("lg_exp")
        ex_ps = sem("ex_ps")
        ex_sb = sem("ex_sb")
        y2_part = sem("y2_part")
        dma_x = sem("dma_x")
        dma_w0 = sem("dma_w0")
        dma_w1 = sem("dma_w1")
        zeroed = sem("zeroed")
        consts = sem("consts")
        pool_chain = sem("pool_chain")
        dve_chain = sem("dve_chain")
        act_chain = sem("act_chain")
        bd0_ready = sem("bd0_ready")
        proj0 = sem("proj0")
        theta_sb = sem("theta_sb")
        pooled = sem("pooled")
        logits0 = sem("logits0")
        vb_ps = sem("vb_ps")
        vb_sb = sem("vb_sb")
        shifted0 = sem("shifted0")
        exp0 = sem("exp0")
        prob0 = sem("prob0")
        attT_ps = sem("attT_ps")
        attT_sb = sem("attT_sb")
        o0_ps = sem("o0_ps")
        norm_in = sem("norm_in")
        centred = sem("centred")
        squared = sem("squared")
        variance = sem("variance")
        rstd_sb = sem("rstd_sb")
        bn_sb = sem("bn_sb")
        rs4_sb = sem("rs4_sb")
        normed = sem("normed")
        w1_pool = sem("w1_pool")
        w1_dve = sem("w1_dve")
        w1_act = sem("w1_act")
        wdt_ps = sem("wdt_ps")
        x1_sb = sem("x1_sb")
        x2_ps = sem("x2_ps")
        x12 = sem("x12")
        xz_ps = sem("xz_ps")
        xi_used = sem("xi_used")
        z_used = sem("z_used")
        conv0 = sem("conv0")
        conv_done = sem("conv_done")
        u_sb = sem("u_sb")
        dt_ps = sem("dt_ps")
        dt_parts = sem("dt_parts")
        dt_sb = sem("dt_sb")
        dA_zero = sem("dA_zero")
        bc_ps = sem("bc_ps")
        dA_sb = sem("dA_sb")
        dbu_done = sem("dbu_done")
        scan_done = sem("scan_done")
        hc_done = sem("hc_done")
        y_init = sem("y_init")
        y_added = sem("y_added")
        gated = sem("gated")
        mo_ps = sem("mo_ps")
        wp_ps = sem("wp_ps")
        x_new = sem("x_new")
        stored = sem("stored")

        S = 16

        block = ctx.enter_context(nc.Block())

        W0_DMAS = 0
        W1_DMAS = 0

        def load_w0():
            for g in range(G):
                r = slice(C * g, C * g + C)
                yield nat0[C * g:C * g + 4, 0, r], a["L0_conv_w_theta"]
                yield nat0[C * g:C * g + 4, 1, r], a["L0_conv_w_phi"]
                yield nat0[C * g:C * g + 16, 2, r], a["L0_conv_w_g"]
                yield nat0[r, 3, r], a["L1_conv_W_p"]
                yield wo_nat[r, C * g:C * g + 16], a["L0_conv_w_o"]
            yield gamma0[:, :], broadcast_rows(a["L0_conv_gamma"], P)

        def load_w1():
            col = lambda v: v.rearrange("(c o) -> c o", o=1)
            for g in range(G):
                r = slice(C * g, C * g + C)
                yield ln_g[r, :], col(a["L1_conv_gamma"])
                yield ln_b[r, :], col(a["L1_conv_beta"])
                yield b_p[r, :], col(a["L1_conv_b_p"])
                yield win_nat[r, :, :], a["L1_conv_W_in"].rearrange("(r e) c -> e r c", e=C)
                k = g % 2
                yield wout_nat[r, :], a["L1_conv_W_out"][:, C * k:C * k + C]
            yield s1[:, :], broadcast_rows(a["L1_conv_s1"], P)
            yield s2[:, :], broadcast_rows(a["L1_conv_s2"], P)
            for v in range(2):
                r = slice(64 * v, 64 * v + 64)
                yield conv_w[r, :], a["L1_conv_conv_w"].rearrange("d o k -> d (o k)")
                yield conv_b[r, :], col(a["L1_conv_conv_b"])
                yield b_dt[r, :], col(a["L1_conv_b_dt"])
                yield d_skip[r, :], col(a["L1_conv_D_skip"])
                yield a_log[r, :], a["L1_conv_A_log"]
                yield wx_t[r, :], a["L1_conv_W_x"].rearrange("n d -> d n")
                yield wx_rows[:, v, :], a["L1_conv_W_x"][0:2, :]
                yield wdt_t[:, v, :], a["L1_conv_W_dt"].rearrange("d r -> r d")

        def load_w2():
            col = lambda v: v.rearrange("(c o) -> c o", o=1)
            for dst, name in ((wq2, "Wq"), (wk2, "Wk"), (wv2, "Wv")):
                yield dst[:, :, :], a["L2_attn_" + name].rearrange("(h e) c -> e h c", e=C)
            yield wu_nat[:, :], a["L2_attn_Wu"]
            for g in range(G):
                r = slice(C * g, C * g + C)
                yield b_u[r, :], col(a["L2_attn_bu"])
                yield r_bd[r, g, :], a["L2_ffn_router_w"]
                yield rb_row[0:1, g, :], a["L2_ffn_router_b"].rearrange("(o e) -> o e", o=1)

        def load_experts():
            for g in range(G):
                yield e_bd[C * g:C * g + C, g, :].rearrange("p (e c) -> p e c", e=E2), \
                    a["L2_ffn_expert_w"].rearrange("e d c -> d e c")
                yield eb_row[0:1, g, :], a["L2_ffn_expert_b"].rearrange("(o e) c -> o (e c)", o=1)

        n_ex = 16 * len(list(load_experts()))

        def load_w3():
            col = lambda v: v.rearrange("(c o) -> c o", o=1)
            qkv, qkv_b = a["L3_attn_qkv_w"], a["L3_attn_qkv_b"]
            hd = C // H3
            for g in range(G):
                r = slice(C * g, C * g + C)
                yield w_q3[r, r], qkv[:, 0:C]
                yield w_k3[r, r], qkv[:, C:2 * C]
                yield w_p3[r, r], a["L3_attn_proj_w"]
                yield b_q3[r, :], col(qkv_b)[0:C, :]
                yield b_k3[r, :], col(qkv_b)[C:2 * C, :]
                yield b_p3[r, :], col(a["L3_attn_proj_b"])
                for h in range(H3):
                    c = slice(2 * C + hd * h, 2 * C + hd * h + hd)
                    yield w_v3[r, h, hd * h:hd * h + hd], qkv[:, c]
                h, c = g, slice(2 * C + hd * g, 2 * C + hd * g + hd)
                yield b_v3[C * h + hd * h:C * h + hd * h + hd, :], col(qkv_b)[c, :]
                yield gate_w3[r, :], broadcast_rows(a["L3_attn_gate_w"][h, :], C)
                yield gate_b3[r, :], broadcast_rows(a["L3_attn_gate_b"][h:h + 1], C)

        n_w3 = 16 * len(list(load_w3()))
        n_w2 = 16 * len(list(load_w2()))
        n_w0 = 16 * len(list(load_w0()))
        n_w1 = 16 * len(list(load_w1()))

        def step_weights(at, names, vectors):
            for dst, name in names:
                src = a["L3_ffn_" + name].rearrange("b o x y -> (b o) x y")[bass.ds(at, 1), :, :] \
                    .rearrange("o x y -> (o x) y")
                yield dst, src if src.shape[0] == P else broadcast_rows(src, G)
            for dst, name in vectors:
                src = a["L3_ffn_" + name].rearrange("b o x -> (b o) x")[bass.ds(at, 1), :] \
                    .rearrange("o x -> x o")
                yield dst, src if src.shape[0] == P else broadcast_rows(src, G)

        def load_attention_step(at):
            return step_weights(at, [(w4[:, k, :], name) for k, name in enumerate(("wq", "wk", "wv", "wo"))], [])

        def load_feeding_step(at):
            return step_weights(at, [(w1_4, "ffn_w1"), (w2_4, "ffn_w2")], [(b1_4, "ffn_b1"), (b2_4, "ffn_b2")])

        N_STEP = 16 * 4
        ATTN_PE = 3 + 3 * B
        ATTN_ACT = 3 + B
        ATTN_DVE = 2 + 3 * B
        FFN_PE = G + 1

        def hold(eng, s_, value):
            eng.wait_ge(s_, value)
            eng.sem_inc(loop_passed, 1)

        def chained(eng, chain):
            count = [0]

            def link(ins):
                count[0] += 1
                ins.then_inc(chain, 1)
                eng.wait_ge(chain, count[0])
            return link

        def weigh_planes(eng, k, q):
            r = slice(CHUNK * q, CHUNK * (q + 1))
            return eng.tensor_tensor(plane_hot[k],
                                     col_hot[:, r, :].unsqueeze(2).to_broadcast([P, CHUNK, PLANES, C]),
                                     weighed[:, r, :].unsqueeze(3).to_broadcast([P, CHUNK, PLANES, C]),
                                     ALU.mult)

        @block.sync
        def _(sp):
            sp.dma_start(X[:, :].rearrange("p (j n) -> p j n", j=J),
                         a["x"].rearrange("(j g) c h w -> (g c) j (h w)", g=G)).then_inc(dma_x, 16)
            sp.wait_ge(zeroed, 2)
            for dst, src in load_w0():
                sp.dma_start(dst, src).then_inc(dma_w0, 16)
            with nc.allow_non_contiguous_dma("small transposed weights"):
                for dst, src in load_w1():
                    sp.dma_start(dst, src).then_inc(dma_w1, 16)
            for c in range(NCH):
                if c >= 2:
                    sp.wait_ge(e_used, c - 1)
                for k, dst in ((0, e_row), (1, e_col)):
                    src = a["L3_attn_edge_index"][k, :].rearrange("(p f) -> p f", p=P)
                    sp.dma_start(dst[:, c % 2, :], src[:, c * EC:(c + 1) * EC]).then_inc(dma_e[c % 2], 16)
            sp.wait_ge(w2_zero, 1)
            with nc.allow_non_contiguous_dma("small biases"):
                for dst, src in load_w2():
                    sp.dma_start(dst, src).then_inc(dma_w2, 16)
            sp.wait_ge(w3_zero, 1)
            with nc.allow_non_contiguous_dma("small biases and column slices"):
                for dst, src in load_w3():
                    sp.dma_start(dst, src).then_inc(dma_w3, 16)
            sp.wait_ge(ex_zero, 1)
            for dst, src in load_experts():
                sp.dma_start(dst, src).then_inc(dma_ex, 16)
            for k, name in enumerate(("attn_mask", "ffn_mask")):
                sp.dma_start(steps_u8[:, k * STEPS:(k + 1) * STEPS],
                             a["L3_ffn_" + name].rearrange("(o b) n -> o (b n)", o=1)).then_inc(dma_m, 16)
            active = sp.alloc_register("sp_active")
            hold(sp, ctrl_ready, 1)
            sp.reg_load(active, ctrl[0:1, 0:1])
            with sp.Fori(0, NB) as i:
                with sp.If_ne(active, 0):
                    attends = sp.value_load(ctrl[0:1, 1:2], min_val=0, max_val=1)
                    feeds = sp.value_load(ctrl[0:1, 2:3], min_val=0, max_val=1)
                    at = sp.value_load(ctrl[0:1, 3:4], min_val=0, max_val=STEPS - 1)
                    with nc.allow_non_contiguous_dma("small biases"):
                        with sp.If(attends > 0):
                            for dst, src in load_attention_step(at):
                                sp.dma_start(dst, src).then_inc(dma_fa, 16)
                        with sp.Else():
                            sp.sem_inc(dma_fa, N_STEP)
                        with sp.If(feeds > 0):
                            for dst, src in load_feeding_step(at):
                                sp.dma_start(dst, src).then_inc(dma_f, 16)
                        with sp.Else():
                            sp.sem_inc(dma_f, N_STEP)
                    hold(sp, ctrl_ready, i + 2)
                    sp.reg_load(active, ctrl[0:1, 0:1])
            sp.wait_ge(x_new, 6)
            sp.dma_start(out.rearrange("(j g) c h w -> (g c) j (h w)", g=G),
                         X[:, :].rearrange("p (j n) -> p j n", j=J)).then_inc(stored, 16)
            sp.wait_ge(stored, 16)

        @block.gpsimd
        def _(pool):
            link = chained(pool, pool_chain)
            nc.gpsimd.memset(nat0[:, :, :], 0.0).then_inc(zeroed, 1)
            nc.gpsimd.memset(wo_nat[:, :], 0.0).then_inc(zeroed, 1)
            link(nc.gpsimd.memset(ident[:, :], 0.0))
            link(nc.gpsimd.affine_select(out=ident[:, :], in_=ident[:, :], compare_op=ALU.not_equal,
                                         fill=1.0, base=0, pattern=[[-1, P]], channel_multiplier=1))
            link(nc.gpsimd.memset(averager[:, :], 0.0))
            for g in range(G):
                link(nc.gpsimd.memset(averager[C * g:C * g + C, C * g:C * g + C], 1.0 / C))
            link(nc.gpsimd.memset(eps5[:, :], 1e-5))
            link(nc.gpsimd.iota(ops_at[:, :], pattern=[[1, NB]], base=0, channel_multiplier=0,
                                allow_small_or_imprecise_dtypes=True))
            link(nc.gpsimd.iota(ops_back[:, :], pattern=[[-1, NB]], base=NONE, channel_multiplier=0,
                                allow_small_or_imprecise_dtypes=True))
            link(nc.gpsimd.memset(from_block[:, :], 0.0))
            link(nc.gpsimd.iota(seg_place[:, :], pattern=[[8192, SEG]], base=1, channel_multiplier=0,
                                allow_small_or_imprecise_dtypes=True))
            link(nc.gpsimd.iota(seg_bits, pattern=[[256, SEG // 8], [0, 8]], base=1 << 30,
                                channel_multiplier=0))
            link(nc.gpsimd.iota(rows_at[:, :], pattern=[[1, N]], base=0, channel_multiplier=0,
                                allow_small_or_imprecise_dtypes=True))
            ones = sum(1 << SYMBOL * k for k in range(PLANES - 1))
            for k, width in ((0, EF), (1, GW)):
                for g in range(G):
                    nc.gpsimd.memset(g_base[:, k, g:g + 1], float(C * width * g + 1 - ones))
            for g in range(G):
                r = slice(C * g, C * g + C)
                link(nc.gpsimd.iota(weight[r, :], pattern=[[0, 1]], base=127 + 2 - 16 * SPACE,
                                    channel_multiplier=SPACE))
                for k, width in ((0, EF), (1, GW)):
                    link(nc.gpsimd.iota(p_base[r, k:k + 1], pattern=[[0, 1]], base=0,
                                        channel_multiplier=width))
            link(nc.gpsimd.memset(one_col[:, :], 1.0))
            link(nc.gpsimd.memset(one_row[:, :], 1.0))
            link(nc.gpsimd.tensor_tensor(centerer[:, :], ident[:, :], averager[:, :], ALU.subtract))
            for g in range(G):
                nc.gpsimd.tensor_copy(
                    permuter[:, C * g:C * g + C].rearrange("p (k i) -> p k i", i=8),
                    ident[:, C * g:C * g + C].rearrange("p (i k) -> p k i", k=4))
            nc.gpsimd.memset(half_mask[:, :], 0.0).then_inc(consts, 1)
            pool.wait_ge(consts, 1)
            for v in range(2):
                link(nc.gpsimd.memset(half_mask[64 * v:64 * v + 64, 64 * v:64 * v + 64], 1.0))
            link(nc.gpsimd.memset(diag[:, :], 0.0))
            for h in range(G):
                r = slice(C * h, C * h + C)
                link(nc.gpsimd.affine_select(out=diag[r, :], in_=diag[r, :], compare_op=ALU.not_equal,
                                             fill=1.0, base=0, pattern=[[-1, C]], channel_multiplier=1))
            nc.gpsimd.memset(zero_bf[:, :], 0.0).then_inc(consts, 1)
            pool.wait_ge(consts, 2)
            pool.wait_ge(dma_w1, n_w1)
            for n in range(2 * S):
                last = nc.gpsimd.tensor_scalar(w_bc[:, n, :], half_mask[:, :], wx_t[:, 2 + n:3 + n], None,
                                               ALU.mult)
            last.then_inc(w1_pool, 1)

            for t in (w_km, r_bd):
                link(nc.gpsimd.memset(t[:, :, :], 0.0))
            nc.gpsimd.tensor_copy(ident_bf[:, :], ident[:, :]).then_inc(w2_zero, 1)
            link(nc.gpsimd.memset(win_mask[:, :], 0.0))
            for h in range(G):
                r = slice(C * h, C * h + C)
                link(nc.gpsimd.affine_select(out=win_mask[r, 0:C], in_=win_mask[r, 0:C], compare_op=ALU.is_gt,
                                             fill=-1e30, base=0, pattern=[[-1, C]], channel_multiplier=1))
                link(nc.gpsimd.affine_select(out=win_mask[r, C:2 * C], in_=win_mask[r, C:2 * C],
                                             compare_op=ALU.is_ge, fill=-1e30, base=0, pattern=[[1, C]],
                                             channel_multiplier=-1))
            pool.wait_ge(bd0_ready, 1)
            for t in (w_q3, w_k3, w_p3):
                link(nc.gpsimd.memset(t[:, :], 0.0))
            link(nc.gpsimd.memset(w_v3, 0.0))
            link(nc.gpsimd.memset(head_scale[:, :], float(C // H3) ** -0.5))
            for g in range(G):
                r = slice(C * g, C * g + C)
                link(nc.gpsimd.affine_select(out=head_scale[r, :], in_=head_scale[r, :],
                                             compare_op=ALU.is_ge, fill=0.0, base=0,
                                             pattern=[[-8, H3]], channel_multiplier=1))
                link(nc.gpsimd.affine_select(out=head_scale[r, :], in_=head_scale[r, :],
                                             compare_op=ALU.is_ge, fill=0.0, base=7,
                                             pattern=[[8, H3]], channel_multiplier=-1))
            nc.gpsimd.memset(b_v3[:, :], 0.0).then_inc(w3_zero, 1)
            pool.wait_ge(w3_zero, 1)
            for i in range(WT):
                nc.gpsimd.tensor_copy(mask_bf[:, i, :], win_mask[:, :])
            nc.gpsimd.iota(rank[:, :], pattern=[[-1, E2]], base=E2, channel_multiplier=0,
                           allow_small_or_imprecise_dtypes=True).then_inc(w2_mask, 1)

            pool.wait_ge(cols_sb, 1)
            for q in range(SLOTS // CHUNK):
                if q >= 2:
                    pool.wait_ge(hot_used, q - 1)
                weigh_planes(nc.gpsimd, q % 2, q).then_inc(hot_sb, 1)

            def gather(i):
                nc.gpsimd.indirect_dma_start(
                    out=hit[:, i // C, 0, i % C:i % C + 1], out_offset=None,
                    in_=a["L3_attn_edge_values"].rearrange("(e o) -> e o", o=1),
                    in_offset=bass.IndirectOffsetOnAxis(ap=tab_i[:, i:i + 1], axis=0)).then_inc(gathered, 16)

            for j in range(J):
                if j >= 2:
                    pool.wait_ge(gated, j - 1)
                pool.wait_ge(u_sb, j + 1)
                nc.gpsimd.tensor_scalar(yacc[:, j % 2, :], u_act[:, j * NT:(j + 1) * NT],
                                        d_skip[:, :], None, ALU.mult).then_inc(y_added, 1)
                for n in range(S):
                    i = S * j + n
                    if i == 0:
                        pool.wait_ge(tab_dve, 1)
                    gather(i)
                    pool.wait_ge(hc_done, i + 1)
                    pool.wait_ge(y_added, (S + 1) * j + n + 1)
                    nc.gpsimd.tensor_tensor(yacc[:, j % 2, :], yacc[:, j % 2, :], hC[:, i % 2, :],
                                            ALU.add).then_inc(y_added, 1)

            pool.wait_ge(x_new, 2)
            nc.gpsimd.memset(e_bd, 0.0).then_inc(ex_zero, 1)

            pool.wait_ge(over_sb, 1)
            more = pool.value_load(over_i[0:1, 0:1], min_val=0, max_val=P)
            pool.wait_ge(gathered, 16 * 2 * C)
            with pool.If(more > 0):
                with pool.Fori(0, EDGES // (P * GW)) as t:
                    for k, dst in ((0, g_row), (1, g_col)):
                        src = a["L3_attn_edge_index"][k, :].rearrange("(t p f) -> t p f", p=P, f=GW)
                        nc.gpsimd.dma_start(dst, src[bass.ds(t, 1), :, :].rearrange(
                            "o p f -> (o p) f")).then_inc(gen_in, 16)
                    pool.wait_ge(gen_done, t + 1)
                    pool.sem_inc(gen_passed, 1)
                pool.wait_ge(tab_dve, 2)
                for i in range(2 * C):
                    gather(i)
                pool.wait_ge(gathered, 2 * 16 * 2 * C)
            nc.gpsimd.tensor_tensor(hit[:, :, 0, :], hit[:, :, 0, :], hit[:, :, 1, :],
                                    ALU.mult).then_inc(hit_sb, 1)
            pool.wait_ge(hit_sb, 1)
            for k in range(2):
                nc.gpsimd.dma_start(bias_dram[k, :].rearrange("(s p c) -> p s c", s=2, c=C),
                                    hit[:, :, k, :]).then_inc(bias_out, 16)
            pool.wait_ge(bias_out, 32)
            for h in range(H3):
                for k, dst in ((0, wgt), (1, msk)):
                    nc.gpsimd.dma_start(dst[C * h:C * h + C, :, 0:C],
                                        bias_dram[k, :].rearrange("(b q c) -> q b c", b=BL, c=C)
                                        ).then_inc(bias_in, 16)
            for u in range(16):
                pool.wait_ge(s2_scale, u + 1)
                nc.gpsimd.tensor_tensor(
                    s2_buf[u % 2].rearrange("p (s k) -> p s k", k=2 * C),
                    s2_buf[u % 2].rearrange("p (s k) -> p s k", k=2 * C),
                    sm2[:, u % 2, :].unsqueeze(2).to_broadcast([P, 16, 2 * C]), ALU.mult).then_inc(s2_prob, 1)

        @block.scalar
        def _(act):
            act.wait_ge(proj0, 1)
            nc.scalar.activation(theta, bank(0, 2), ACT.Copy).then_inc(theta_sb, 1)
            act.wait_ge(vb_ps, 1)
            nc.scalar.activation(vb, bank(0, 2), ACT.Copy).then_inc(vb_sb, 1)
            act.wait_ge(shifted0, 1)
            nc.scalar.activation(att, att, ACT.Exp).then_inc(exp0, 1)
            act.wait_ge(attT_ps, 1)
            nc.scalar.activation(att_t, bank(0, 4), ACT.Copy).then_inc(attT_sb, 1)

            n_act = [0]

            def link(ins):
                n_act[0] += 1
                ins.then_inc(act_chain, 1)
                act.wait_ge(act_chain, n_act[0])

            def inverse_root(dst, src, eps):
                link(nc.scalar.activation(dst, src, ACT.Ln, bias=eps[:, :]))
                return nc.scalar.activation(dst, dst, ACT.Exp, scale=-0.5)

            def norm_steps(k, eps):
                act.wait_ge(centred, k)
                nc.scalar.activation(sq[:, :], bank(0, 2), ACT.Square).then_inc(squared, 1)
                act.wait_ge(variance, k)
                inverse_root(rstd[:, :], bank(2, 2), eps).then_inc(rstd_sb, 1)

            act.wait_ge(consts, 2)
            act.wait_ge(bn_sb, 1)
            inverse_root(rs4[:, :], bn2[:, :, 1], eps5).then_inc(rs4_sb, 1)

            act.wait_ge(dma_w1, n_w1)
            link(nc.scalar.activation(a_neg[:, :], a_log[:, :], ACT.Exp))
            nc.scalar.mul(a_neg[:, :], a_neg[:, :], -1.0).then_inc(w1_act, 1)
            norm_steps(1, eps5)
            for i in range(8):
                g, jp = i // 2, i % 2
                act.wait_ge(xz_ps, 2 * i + 1)
                k = 4 * (i % 2)
                dst = xi_pad[:, g + 8 * jp:g + 8 * jp + 5:4, 3:259]
                nc.scalar.activation(dst, bank(k).rearrange("p (j n) -> p j n", n=N),
                                     ACT.Copy).then_inc(xi_used, 1)
                act.wait_ge(xz_ps, 2 * i + 2)
                nc.scalar.activation(z_act.rearrange("p (b n) -> p b n", n=N)
                                     [:, g + 8 * jp:g + 8 * jp + 5:4, :],
                                     bank(k + 1).rearrange("p (j n) -> p j n", n=N),
                                     ACT.Silu).then_inc(z_used, 1)
            act.wait_ge(conv0, 1)
            act.wait_ge(xi_used, 8)
            nc.scalar.activation(u_act.rearrange("p (b t) -> p b t", b=B), xi_pad[:, :, 0:N],
                                 ACT.Identity, bias=conv_b[:, :],
                                 scale=conv_w[:, 0:1]).then_inc(conv0, 1)
            for j in range(J):
                act.wait_ge(conv_done, j + 1)
                r = slice(j * NT, (j + 1) * NT)
                nc.scalar.activation(u_act[:, r], u_act[:, r], ACT.Silu).then_inc(u_sb, 1)
            for j in range(J):
                r = slice(j * NT, (j + 1) * NT)
                act.wait_ge(dt_ps, j + 1)
                pre = bank(2 * (j % 2), 2)
                link(nc.scalar.activation(tmp_a, pre, ACT.Abs, bias=b_dt[:, :]))
                link(nc.scalar.activation(tmp_a, tmp_a, ACT.Exp, scale=-1.0))
                if j > 0:
                    act.wait_ge(dt_sb, j)
                link(nc.scalar.activation(tmp_b, tmp_a, ACT.Ln, bias=1.0))
                nc.scalar.activation(dt_act[:, r], pre, ACT.Relu, bias=b_dt[:, :]).then_inc(dt_parts, 1)
            for i in range(J * S):
                j, n = i // S, i % S
                if i >= 2:
                    act.wait_ge(scan_done, i - 1)
                if i == 0:
                    act.wait_ge(dA_zero, 1)
                if n == 0:
                    act.wait_ge(dt_sb, j + 1)
                src = dt_act[:, j * NT:(j + 1) * NT].rearrange("p (b t) -> p b t", t=N)
                dst = dA[:, i % 2, :].rearrange("p (b t) -> p b t", t=N)
                nc.scalar.activation(dst[:, :, 1:], src[:, :, 1:], ACT.Exp,
                                     scale=a_neg[:, n:n + 1]).then_inc(dA_sb, 1)
            norm_steps(2, eps5)

            act.wait_ge(w2_ps, 1)
            act.wait_ge(w2_zero, 1)
            for g in range(G):
                r = slice(C * g, C * g + C)
                nc.scalar.activation(w_km[r, :, r], bank(6)[r, 0:H2 * C].rearrange("p (h c) -> p h c", c=C),
                                     ACT.Copy, scale=float(C) ** -0.5)
            nc.scalar.activation(w_vu[:, :], bank(7)[:, 0:H2 * C], ACT.Copy).then_inc(w2_sb, 1)
            norm_steps(3, eps5)
            for h in range(H2):
                act.wait_ge(km_ps, h + 1)
                nc.scalar.activation(km[:, :, h, :], bank(2 * (h % 4), 2).rearrange("p (t k) -> p t k", k=C),
                                     ACT.Copy).then_inc(km_sb, 1)
            for u in range(16):
                act.wait_ge(s2_shifted, u + 1)
                nc.scalar.activation(s2_buf[u % 2], s2_buf[u % 2], ACT.Exp).then_inc(s2_exp, 1)
            norm_steps(4, eps5)
            act.wait_ge(lg_shifted, 1)
            nc.scalar.activation(gate[:, :, :], gate[:, :, :], ACT.Exp).then_inc(lg_exp, 1)

            norm_steps(5, eps5)
            act.wait_ge(dma_w3, n_w3)
            link(nc.scalar.activation(b_qh[:, :], head_scale[:, :], ACT.Copy, scale=b_q3[:, :]))
            act.wait_ge(qkv3_ps, 1)
            for h in range(H3):
                last = nc.scalar.activation(q3[:, :, h, :], bank(4, 2).rearrange("p (s q) -> p s q", q=C),
                                            ACT.Identity, bias=b_qh[:, h:h + 1],
                                            scale=head_scale[:, h:h + 1])
            last.then_inc(q3_sb, 1)
            nc.scalar.activation(k3[:, :, 0:C], bank(6, 2).rearrange("p (s k) -> p s k", k=C),
                                 ACT.Identity, bias=b_k3[:, :]).then_inc(k3_sb, 1)
            for jp in range(2):
                act.wait_ge(v3_ps, jp + 1)
                dst = v3.rearrange("p (g j n) -> p g j n", g=G, j=J)[:, :, 2 * jp:2 * jp + 2, :]
                nc.scalar.activation(dst.rearrange("p g j n -> p g (j n)"),
                                     bank(4 * jp, 4).rearrange("p (g n) -> p g n", g=G),
                                     ACT.Identity, bias=b_v3[:, :]).then_inc(v3_sb, 1)
            for j in range(J):
                act.wait_ge(s3_shift, j + 1)
                nc.scalar.activation(s3[j % 2], s3[j % 2], ACT.Exp).then_inc(s3_exp, 1)
                if j >= 1:
                    act.wait_ge(o3_ps, j)
                    nc.scalar.activation(o3[:, (j - 1) * N:j * N], bank(4 * ((j - 1) % 2))[:, 0:N],
                                         ACT.Copy).then_inc(o3_sb, 1)
            act.wait_ge(o3_ps, J)
            nc.scalar.activation(o3[:, (J - 1) * N:J * N], bank(4 * ((J - 1) % 2))[:, 0:N],
                                 ACT.Copy).then_inc(o3_sb, 1)

            norm_steps(6, eps5)
            active = act.alloc_register("act_active")
            hold(act, ctrl_ready, 1)
            act.reg_load(active, ctrl[0:1, 0:1])
            with act.Fori(0, NB) as i:
                with act.If_ne(active, 0):
                    attends = act.value_load(ctrl[0:1, 1:2], min_val=0, max_val=1)
                    feeds = act.value_load(ctrl[0:1, 2:3], min_val=0, max_val=1)
                    with act.If(attends > 0):
                        hold(act, attn_pe, ATTN_PE * i + 1)
                        nc.scalar.activation(q4, bank(0, 2), ACT.Copy).then_inc(attn_act, 1)
                        hold(act, attn_pe, ATTN_PE * i + 2)
                        nc.scalar.activation(v4.rearrange("p (g t) -> p g t", g=G), ps[:, 4:8, 0:N],
                                             ACT.Copy).then_inc(attn_act, 1)
                        for b in range(B):
                            hold(act, attn_dve, ATTN_DVE * i + 2 + 3 * b)
                            for h in range(2):
                                last = nc.scalar.activation(p4[:, h * N:(h + 1) * N],
                                                            bank(0)[:, h * N:(h + 1) * N], ACT.Exp,
                                                            bias=nm4[:, h:h + 1], scale=float(C) ** -0.5,
                                                            accum_out=sm4[:, h:h + 1])
                            last.then_inc(attn_act, 1)
                        hold(act, attn_pe, ATTN_PE * i + 2 + 3 * B)
                        nc.scalar.activation(y4, bank(2, 2), ACT.Copy).then_inc(attn_act, 1)
                    with act.Else():
                        act.sem_inc(attn_act, ATTN_ACT)
                    with act.If(feeds > 0):
                        hold(act, dma_f, N_STEP * i + N_STEP)
                        for g in range(G):
                            hold(act, ffn_pe, FFN_PE * i + g + 1)
                            nc.scalar.activation(hid[:, g * NT:(g + 1) * NT], bank(2 * g, 2), ACT.Relu,
                                                 bias=b1_4).then_inc(ffn_act, 1)
                    with act.Else():
                        act.sem_inc(ffn_act, G)
                    hold(act, ctrl_ready, i + 2)
                    act.reg_load(active, ctrl[0:1, 0:1])

        @block.vector
        def _(dve):
            link = chained(dve, dve_chain)
            V = nc.vector
            dve.wait_ge(dma_w0, n_w0)
            link(V.memset(phi_bd, 0.0))
            link(V.memset(gp_bd, 0.0))
            V.transpose(bd0[:, :, :].rearrange("p a b -> p (a b)"),
                        nat0[:, :, :].rearrange("p a b -> p (a b)"))
            V.transpose(wo_bd[:, :], wo_nat[:, :]).then_inc(bd0_ready, 1)
            for k, dst in ((1, phi_bd), (2, gp_bd)):
                dve.wait_ge(proj0, k + 1)
                link(V.tensor_reduce(pool_w[:, 0:NT // 2],
                                     bank(2 * k, 2).rearrange("p (m b) -> p m b", b=2), AX_X, ALU.max))
                src = pool_w[:, 0:NT // 2].rearrange("p (m a w) -> p m w a", a=2, w=8)
                for g in range(G):
                    r = slice(C * g, C * g + C)
                    last = V.tensor_reduce(
                        dst[r, :, g, :].rearrange("p j (h w) -> p j h w", w=8),
                        pool_w[r, 0:NT // 2].rearrange("p (j h a w) -> p j h w a", j=J, a=2, w=8),
                        AX_X, ALU.max)
                last.then_inc(pooled, 1)
                dve.wait_ge(pooled, k)
            seg = lambda t: t.rearrange("p (s m) -> p s m", m=64)
            wide = lambda t: t[:, :].unsqueeze(2).to_broadcast([P, 32, 64])
            dve.wait_ge(logits0, 1)
            link(V.tensor_reduce(mx0[:, :], seg(bank(4, 4)), AX_X, ALU.max))
            V.tensor_tensor(seg(att), seg(bank(4, 4)), wide(mx0), ALU.subtract).then_inc(shifted0, 1)
            dve.wait_ge(exp0, 1)
            link(V.tensor_reduce(sm0[:, :], seg(att), AX_X, ALU.add))
            link(V.reciprocal(rs0[:, :], sm0[:, :]))
            V.tensor_tensor(seg(att), seg(att), wide(rs0), ALU.mult).then_inc(prob0, 1)
            dve.wait_ge(o0_ps, 1)
            dve.wait_ge(dma_x, 16)
            V.scalar_tensor_tensor(X[:, :], bank(4, 2), gamma0[:, :], X[:, :], ALU.mult,
                                   ALU.add).then_inc(x_new, 1)
            dve.wait_ge(x_new, 1)

            for j in range(J):
                last = V.bn_stats(bn6[:, j, :], X[:, j * N:(j + 1) * N])
            link(last)
            for j in range(J):
                last = V.bn_aggr(bn2[:, j, :], bn6[:, j, :])
            last.then_inc(bn_sb, 1)
            dve.wait_ge(rs4_sb, 1)
            for j in range(J):
                last = V.tensor_scalar(xn[:, j * N:(j + 1) * N], X[:, j * N:(j + 1) * N],
                                       bn2[:, j, 0:1], rs4[:, j:j + 1], ALU.subtract, ALU.mult)
            last.then_inc(norm_in, 1)

            def finish_norm(k, dst):
                dve.wait_ge(rstd_sb, k)
                link(V.tensor_tensor(dst, bank(0, 2), rstd[:, :], ALU.mult))

            dve.wait_ge(dma_w1, n_w1)
            V.transpose(win_t[:, :], win_nat[:, :, :].rearrange("p a b -> p (a b)"))
            V.transpose(wout_t[:, :], wout_nat[:, :])
            V.memset(xi_pad[:, :, 0:3], 0.0).then_inc(conv0, 1)
            dve.wait_ge(wdt_ps, 1)
            dve.wait_ge(w1_pool, 1)
            V.tensor_tensor(w_dt[:, :], bank(7)[:, 0:P], half_mask[:, :], ALU.mult).then_inc(w1_dve, 1)
            finish_norm(1, xn[:, :])
            V.tensor_scalar(x1[:, :], xn[:, :], ln_g[:, :], ln_b[:, :], ALU.mult, ALU.add).then_inc(x1_sb, 1)
            dve.wait_ge(x2_ps, 1)
            V.tensor_scalar(x2[:, :], bank(4, 2), ln_g[:, :], ln_b[:, :], ALU.mult,
                            ALU.add).then_inc(x12, 1)
            for c in range(NCH):
                dve.wait_ge(dma_e[c % 2], 32 * (c // 2 + 1))
                r_, c_ = e_row[:, c % 2, :], e_col[:, c % 2, :]
                link(V.tensor_tensor(e_x, r_, c_, ALU.bitwise_xor))
                V.scalar_tensor_tensor(e_u, e_x, 8.0, r_, ALU.mult, ALU.max)
                V.scalar_tensor_tensor(e_key, r_, float(C), e_x, ALU.mult, ALU.add).then_inc(e_used, 1)
                dve.wait_ge(e_used, c + 1)
                per = lambda t: t.rearrange("p (s f) -> p s f", f=SEG)
                link(V.tensor_tensor(per(e_key), per(e_key),
                                     seg_place[:, :].unsqueeze(1).to_broadcast([P, EC // SEG, SEG]), ALU.add))
                link(V.scalar_tensor_tensor(e_key, e_u, float(N), e_key, ALU.is_lt, ALU.mult))
                for q in range(EC // SEG):
                    at = 8 * (c * (EC // SEG) + q)
                    last = V.max(cand[:, at:at + 8], e_key[:, q * SEG:(q + 1) * SEG])
            link(last)
            link(V.tensor_scalar(k_a, cand, -1.0, None, ALU.add))
            link(V.tensor_scalar(k_b, k_a, CELLS - 1, 13, ALU.bitwise_and, ALU.logical_shift_left))
            link(V.tensor_scalar(k_a, k_a, 13, None, ALU.logical_shift_right))
            link(V.tensor_tensor(k_b, k_b, k_a, ALU.bitwise_or))
            link(V.tensor_tensor(k_b, k_b, seg_bits, ALU.bitwise_or))
            link(V.tensor_scalar(k_a, cand, 0.0, -1.0, ALU.is_gt, ALU.mult))
            link(V.tensor_tensor(k_key, k_b, k_a, ALU.bitwise_and))

            def sort_slots(keys, rounds, link):
                for q in range(rounds):
                    link(V.max(top48[:, 8 * q:8 * q + 8], keys))
                    link(V.match_replace(keys, top48[:, 8 * q:8 * q + 8], keys, 0.0))

            def slot_fields(slots, base, link):
                n = slice(0, slots)
                t = top48[:, n].bitcast(I32)
                link(V.tensor_scalar(d_a[:, n], t, 13, CELLS - 1, ALU.logical_shift_right, ALU.bitwise_and))
                link(V.tensor_scalar(d_b[:, n], t, 8191, None, ALU.bitwise_and))
                link(V.tensor_tensor(d_b[:, n], d_b[:, n], base.to_broadcast([P, slots]), ALU.bitwise_or))
                link(V.tensor_scalar(d_ok[:, n], top48[:, n], 0.0, weight[:, :].bitcast(F32), ALU.is_gt,
                                     ALU.mult))
                link(V.tensor_tensor(d_new[:, 1:slots], d_a[:, 1:slots], d_a[:, 0:slots - 1], ALU.not_equal))
                link(V.tensor_tensor(d_ok[:, 1:slots], d_ok[:, 1:slots], d_new[:, 1:slots], ALU.mult))
                link(V.tensor_copy(weighed[:, n, 0], d_ok[:, n]))
                for k in range(1, PLANES):
                    link(V.tensor_scalar(d_c[:, n], d_b[:, n], SYMBOL * (k - 1), (1 << SYMBOL) - 1,
                                         ALU.logical_shift_right, ALU.bitwise_and))
                    link(V.scalar_tensor_tensor(weighed[:, n, k], d_c[:, n], 1.0, d_ok[:, n], ALU.add, ALU.mult))
                link(V.tensor_scalar(d_row[:, n], d_a[:, n], 5, None, ALU.logical_shift_right))
                link(V.tensor_tensor(d_c[:, n], d_a[:, n], d_row[:, n], ALU.bitwise_xor))
                link(V.tensor_scalar(d_col[:, n], d_c[:, n], C - 1, None, ALU.bitwise_and))
                link(V.tensor_copy(d_at[:, n], d_row[:, n]))
                return V.tensor_tensor(col_hot[:, n, :],
                                       rows_at[:, 0:C].unsqueeze(1).to_broadcast([P, slots, C]),
                                       d_col[:, n].unsqueeze(2).to_broadcast([P, slots, C]), ALU.is_equal)

            def hot_rows(k, q):
                for s_ in range(CHUNK):
                    at = CHUNK * q + s_
                    last = V.tensor_scalar(row_hot[k][:, s_, :], rows_at[:, :], d_at[:, at:at + 1], None,
                                           ALU.is_equal)
                return last

            def table_indices(link):
                link(V.tensor_scalar(tab_i[:, :], tab[:, :], -1.0, 0.0, ALU.add, ALU.max))
                return V.tensor_scalar(hit[:, :, 1, :], tab[:, :].rearrange("p (s c) -> p s c", c=C), 0.0, None,
                                       ALU.is_gt)

            def planes_to_table(dst, base, link):
                weights = ps[:, 4:8, 0:2 * C]
                shares = ps[:, 4:8, 2 * C:2 * C * PLANES].rearrange("p g (k c) -> p g k c", c=2 * C)
                k3_ = PLANES - 1
                link(V.tensor_scalar(inv_i, weights.bitcast(I32), 23, None, ALU.logical_shift_right))
                link(V.tensor_scalar(inv_i, inv_i, -1, 254, ALU.mult, ALU.add))
                link(V.tensor_scalar(inv_i, inv_i, 23, None, ALU.logical_shift_left))
                link(V.tensor_tensor(symbols, shares, inv_i.bitcast(F32).unsqueeze(2)
                                     .to_broadcast([P, G, k3_, 2 * C]), ALU.mult))
                link(V.tensor_scalar(symbols, symbols, -0.25, float(1 << 23), ALU.add, ALU.add))
                link(V.tensor_scalar(symbols, symbols, -float(1 << 23), None, ALU.add))
                number = symbols[:, :, k3_ - 1, :]
                for k in range(k3_ - 2, -1, -1):
                    link(V.scalar_tensor_tensor(number, number, float(1 << SYMBOL), symbols[:, :, k, :],
                                                ALU.mult, ALU.add))
                link(V.tensor_tensor(number, number, base.unsqueeze(2).to_broadcast([P, G, 2 * C]), ALU.add))
                link(V.scalar_tensor_tensor(number, weights, 0.0, number, ALU.is_gt, ALU.mult))
                return V.tensor_reduce(dst, number.rearrange("p g c -> p c g"), AX_X, ALU.max)

            sort_slots(k_key.bitcast(F32), SLOTS // 8, link)
            link(V.tensor_reduce(over[:, 0:1], cand.rearrange("p (s e) -> p s e", e=8)[:, :, 7:8]
                                 .rearrange("p s e -> p (s e)"), AX_X, ALU.max))
            link(V.tensor_reduce(over[:, 1:2], k_key.bitcast(F32), AX_X, ALU.max))
            link(V.tensor_tensor(over[:, 0:1], over[:, 0:1], over[:, 1:2], ALU.max))
            link(V.tensor_scalar(over[:, 0:1], over[:, 0:1], 0.0, None, ALU.is_gt))
            link(V.tensor_scalar(weight[:, :], weight[:, :], 23, None, ALU.logical_shift_left))
            slot_fields(SLOTS, p_base[:, 0:1], link).then_inc(cols_sb, 1)
            dve.wait_ge(cols_sb, 1)
            for q in range(2):
                hot_rows(q, q).then_inc(rows_sb, 1)
            dve.wait_ge(conv0, 2)
            for j in range(J):
                r = slice(j * NT, (j + 1) * NT)
                uj = u_act[:, r].rearrange("p (b t) -> p b t", t=N)
                for k in range(1, 4):
                    ins = V.scalar_tensor_tensor(uj, xi_pad[:, 4 * j:4 * j + 4, k:k + N],
                                                 conv_w[:, k:k + 1], uj, ALU.mult, ALU.add)
                    if k < 3:
                        link(ins)
                ins.then_inc(conv_done, 1)
            dve.wait_ge(hot_used, 1)
            hot_rows(0, 2).then_inc(rows_sb, 1)
            for j in range(J):
                r = slice(j * NT, (j + 1) * NT)
                dve.wait_ge(dt_parts, j + 1)
                V.tensor_tensor(dt_act[:, r], dt_act[:, r], tmp_b, ALU.add).then_inc(dt_sb, 1)
                dve.wait_ge(dt_sb, j + 1)
                last = V.tensor_tensor(dtu[:, r], dt_act[:, r], u_act[:, r], ALU.mult)
            link(last)
            dve.wait_ge(planes_ps, 1)
            V.tensor_copy(over_i[:, :], bank(4)[0:1, HALF - 1:HALF]).then_inc(over_sb, 1)
            link(planes_to_table(tab[:, :], g_base[:, 0, :], link))
            table_indices(link).then_inc(tab_dve, 1)
            V.memset(dA[:, :, 0:NT:N], 0.0).then_inc(dA_zero, 1)
            for i in range(J * S):
                j, n = i // S, i % S
                k = i % 2
                dve.wait_ge(bc_ps, 2 * i + 1)
                V.tensor_tensor(dBu[:, k, :], dtu[:, j * NT:(j + 1) * NT], bank(4 * k, 2),
                                ALU.mult).then_inc(dbu_done, 1)
                dve.wait_ge(dbu_done, i + 1)
                dve.wait_ge(dA_sb, i + 1)
                V.tensor_tensor_scan(hst[:, k, :], dA[:, k, :], dBu[:, k, :], 0.0, ALU.mult,
                                     ALU.add).then_inc(scan_done, 1)
                dve.wait_ge(scan_done, i + 1)
                dve.wait_ge(bc_ps, 2 * i + 2)
                if i >= 2:
                    dve.wait_ge(y_added, (S + 1) * ((i - 2) // S) + (i - 2) % S + 2)
                V.tensor_tensor(hC[:, k, :], hst[:, k, :], bank(4 * k + 2, 2), ALU.mult).then_inc(hc_done, 1)
                if n == S - 1:
                    dve.wait_ge(y_added, (S + 1) * (j + 1))
                    r = slice(j * NT, (j + 1) * NT)
                    V.tensor_tensor(z_act[:, r], z_act[:, r], yacc[:, j % 2, :], ALU.mult).then_inc(gated, 1)
            dve.wait_ge(mo_ps, 1)
            link(V.scalar_tensor_tensor(xn[:, :], x1[:, :], s1[:, :], bank(0, 2), ALU.mult, ALU.add))
            V.scalar_tensor_tensor(xn[:, :], x2[:, :], s2[:, :], xn[:, :], ALU.mult,
                                   ALU.add).then_inc(norm_in, 1)
            finish_norm(2, xn[:, :])
            V.tensor_scalar(xn[:, :], xn[:, :], ln_g[:, :], ln_b[:, :], ALU.mult, ALU.add).then_inc(normed, 1)
            dve.wait_ge(wp_ps, 1)
            V.scalar_tensor_tensor(X[:, :], bank(4, 2), b_p[:, :], X[:, :], ALU.add,
                                   ALU.add).then_inc(x_new, 1)

            more = dve.value_load(over_i[0:1, 0:1], min_val=0, max_val=P)
            with dve.If(more > 0):
                flink = chained(dve, gen_frame)
                dve.wait_ge(gathered, 16 * 2 * C)
                flink(V.memset(tab[:, :], 0.0))
                GEN = 44
                with dve.Fori(0, EDGES // (P * GW)) as t:
                    inside = [0]

                    def glink(ins):
                        inside[0] += 1
                        ins.then_inc(gen_chain, 1)
                        dve.wait_ge(gen_chain, GEN * t + inside[0])
                        dve.sem_inc(gen_passed, 1)

                    dve.wait_ge(gen_in, 32 * t + 32)
                    glink(V.tensor_tensor(g_x, g_row, g_col, ALU.bitwise_xor))
                    glink(V.scalar_tensor_tensor(g_u, g_x, 8.0, g_row, ALU.mult, ALU.max))
                    glink(V.scalar_tensor_tensor(k_b[:, 0:GW], g_row, float(C), g_x, ALU.mult, ALU.add))
                    glink(V.tensor_scalar(k_b[:, 0:GW], k_b[:, 0:GW], CELLS - 1, 13, ALU.bitwise_and,
                                          ALU.logical_shift_left))
                    glink(V.tensor_copy(k_a[:, 0:GW], rows_at[:, 0:GW]))
                    glink(V.tensor_tensor(k_b[:, 0:GW], k_b[:, 0:GW], k_a[:, 0:GW], ALU.bitwise_or))
                    glink(V.tensor_scalar(k_a[:, 0:GW], g_u, float(N), -1.0, ALU.is_lt, ALU.mult))
                    glink(V.tensor_scalar(k_b[:, 0:GW], k_b[:, 0:GW], 1 << 30, None, ALU.bitwise_or))
                    glink(V.tensor_tensor(k_key[:, 0:GW], k_b[:, 0:GW], k_a[:, 0:GW], ALU.bitwise_and))
                    sort_slots(k_key[:, 0:GW].bitcast(F32), GW // 8, glink)
                    glink(slot_fields(GW, p_base[:, 1:2], glink))
                    hot_rows(0, 0)
                    weigh_planes(V, 0, 0).then_inc(gen_slots, 1)
                    dve.wait_ge(gen_ps, t + 1)
                    glink(planes_to_table(tab_new[:, :], g_base[:, 1, :], glink))
                    glink(V.tensor_tensor(tab[:, :], tab[:, :], tab_new[:, :], ALU.max))
                    glink(V.tensor_scalar(g_base[:, 1, :], g_base[:, 1, :], float(P * GW), None, ALU.add))
                    dve.sem_inc(gen_done, 1)
                    assert inside[0] == GEN, inside[0]
                table_indices(flink).then_inc(tab_dve, 1)

            dve.wait_ge(dma_w2, n_w2)
            V.transpose(wu_t[:, :], wu_nat[:, :]).then_inc(wu_ready, 1)

            def norm(k):
                dve.wait_ge(rstd_sb, k)
                V.tensor_tensor(xn[:, :], bank(0, 2), rstd[:, :], ALU.mult).then_inc(normed, 1)

            norm(3)

            def window_scores(u):
                k = u % 2
                s = s2_buf[k]
                seg = s.rearrange("p (s k) -> p s k", k=2 * C)
                dve.wait_ge(s2_ps, u + 1)
                if u >= 2:
                    dve.wait_ge(p2_sb, u - 1)
                V.transpose(s, bank(2 * k, 2)).then_inc(s2_read, 1)
                dve.wait_ge(s2_read, u + 1)
                link(V.tensor_reduce(mx2[:, k, :], seg, AX_X, ALU.max))
                V.tensor_tensor(seg, seg, mx2[:, k, :].unsqueeze(2).to_broadcast([P, 16, 2 * C]),
                                ALU.subtract).then_inc(s2_shifted, 1)
                dve.wait_ge(v2_ps, u + 1)
                if u >= 2:
                    dve.wait_ge(o2_ps, u - 1)
                V.transpose(vm_buf[k], bank(4 + k)).then_inc(v2_sb, 1)

            def window_sums(u):
                k = u % 2
                dve.wait_ge(s2_exp, u + 1)
                link(V.tensor_reduce(sm2[:, k, :], s2_buf[k].rearrange("p (s k) -> p s k", k=2 * C),
                                     AX_X, ALU.add))
                V.reciprocal(sm2[:, k, :], sm2[:, k, :]).then_inc(s2_scale, 1)

            def window_probs(u):
                k = u % 2
                dve.wait_ge(s2_prob, u + 1)
                if u >= 2:
                    dve.wait_ge(o2_ps, u - 1)
                V.transpose(pt_buf[k], s2_buf[k]).then_inc(p2_sb, 1)

            window_scores(0)
            for u in range(1, 16):
                window_sums(u - 1)
                if u >= 2:
                    window_probs(u - 2)
                window_scores(u)
            window_sums(15)
            window_probs(14)
            window_probs(15)
            dve.wait_ge(o2_ps, 16)
            V.scalar_tensor_tensor(X[:, :], bank(6, 2), b_u[:, :], X[:, :], ALU.add,
                                   ALU.add).then_inc(x_new, 1)

            norm(4)
            wide8 = lambda t: t[:, :].unsqueeze(2).to_broadcast([P, TT * G, E2])
            ranks = rank[:, :].unsqueeze(1).to_broadcast([P, TT * G, E2])
            dve.wait_ge(lg_ps, 1)
            dve.wait_ge(w2_mask, 1)
            lps = bank(4)[:, 0:TT * G * E2].rearrange("p (t e) -> p t e", e=E2)
            link(V.tensor_copy(lg[:, :, :], lps))

            def pick(sel, values, top):
                link(V.tensor_reduce(top[:, :], values, AX_X, ALU.max))
                link(V.tensor_tensor(sel[:, :, :], values, wide8(top), ALU.is_equal))
                link(V.tensor_tensor(sel[:, :, :], sel[:, :, :], ranks, ALU.mult))
                link(V.tensor_reduce(top2[:, :], sel[:, :, :], AX_X, ALU.max))
                link(V.tensor_tensor(sel[:, :, :], sel[:, :, :], wide8(top2), ALU.is_equal))

            pick(sel_a, lg[:, :, :], top1)
            V.tensor_tensor(gate[:, :, :], lg[:, :, :], wide8(top1), ALU.subtract).then_inc(lg_shifted, 1)
            dve.wait_ge(lg_exp, 1)
            link(V.scalar_tensor_tensor(lg[:, :, :], sel_a[:, :, :], -3e38, lg[:, :, :], ALU.mult, ALU.add))
            pick(sel_b, lg[:, :, :], top1)
            link(V.tensor_tensor(sel_a[:, :, :], sel_a[:, :, :], sel_b[:, :, :], ALU.add))
            link(V.tensor_tensor(gate[:, :, :], gate[:, :, :], sel_a[:, :, :], ALU.mult))
            link(V.tensor_reduce(top1[:, :], gate[:, :, :], AX_X, ALU.add))
            link(V.reciprocal(top1[:, :], top1[:, :]))
            link(V.tensor_tensor(gate[:, :, :], gate[:, :, :], wide8(top1), ALU.mult))
            for t in range(TT):
                dve.wait_ge(ex_ps, t + 1)
                if t >= 2:
                    dve.wait_ge(y2_part, t - 1)
                w = gate[:, G * t:G * t + G, :].unsqueeze(3)
                V.tensor_tensor(mix[t % 2].rearrange("p (e g c) -> p g e c", e=E2, g=G),
                                bank(4 + 2 * (t % 2), 2).rearrange("p (g e c) -> p g e c", g=G, c=C),
                                w.to_broadcast([P, G, E2, C]), ALU.mult).then_inc(ex_sb, 1)
            dve.wait_ge(y2_part, TT)
            V.tensor_tensor(X[:, :], X[:, :], bank(2, 2), ALU.add).then_inc(x_new, 1)

            norm(5)
            dve.wait_ge(k3_sb, 1)
            link(V.tensor_reduce(mx3[:, 0, :], k3[:, :, 0:C], AX_X, ALU.add))
            V.tensor_scalar(k3[:, :, C:KN].rearrange("p s k -> p (s k)"), mx3[:, 0, :], 1.0 / C, None,
                            ALU.mult).then_inc(k3_node, 1)
            dve.wait_ge(bias_in, 16 * 2 * H3)
            dg = diag[:, :].unsqueeze(1).to_broadcast([P, BL, C])
            link(V.memset(wgt[:, :, C:KN], 1.0))
            link(V.memset(msk[:, :, C:KN], 1.0))
            link(V.tensor_tensor(gate3[:, :, :], wgt[:, :, 0:C], dg, ALU.mult))
            link(V.tensor_tensor(wgt[:, :, 0:C], wgt[:, :, 0:C], gate3[:, :, :], ALU.subtract))
            link(V.tensor_tensor(wgt[:, :, 0:C], wgt[:, :, 0:C], dg, ALU.add))
            link(V.tensor_tensor(msk[:, :, 0:C], msk[:, :, 0:C], dg, ALU.max))
            flat3 = lambda t: t[:, :, :].rearrange("p b k -> p (b k)")
            dve.wait_ge(dma_w3, n_w3)
            link(V.tensor_scalar(gate3[:, :, :], wgt[:, :, 0:C], gate_w3[:, :], gate_b3[:, :], ALU.mult,
                                 ALU.add))
            link(V.tensor_tensor(gate3[:, :, :], gate3[:, :, :], msk[:, :, 0:C], ALU.mult))
            link(V.tensor_tensor(node_gate[:, 0:1], gate_w3[:, :], gate_b3[:, :], ALU.add))
            link(V.tensor_scalar(node_gate[:, 0:1], node_gate[:, 0:1], 1.0 / C, None, ALU.mult))
            link(V.tensor_scalar(gate3[:, :, :], gate3[:, :, :], node_gate[:, 0:1], None, ALU.add))
            link(V.tensor_scalar(flat3(msk), flat3(msk), -1.0, 1e30, ALU.add, ALU.mult))
            link(V.tensor_tensor(flat3(msk), flat3(msk), flat3(wgt), ALU.add))
            for jp in range(2):
                dve.wait_ge(v3_sb, jp + 1)
                for g in range(G):
                    r = slice((g * J + 2 * jp) * N, (g * J + 2 * jp + 2) * N)
                    last = V.transpose(vm3[:, r], v3[:, r])
            last.then_inc(vm3_sb, 1)

            def block_scores(j):
                k = j % 2
                seg = s3[k].rearrange("p (g t) -> p g t", g=G)
                keys = s3[k].rearrange("p (s k) -> p s k", k=KN)
                dve.wait_ge(s3_ps, j + 1)
                V.tensor_tensor(seg, ps[:, 4 * k:4 * k + 4, 0:BL * KN],
                                flat3(msk).unsqueeze(1).to_broadcast([P, G, BL * KN]),
                                ALU.add).then_inc(s3_read, 1)
                dve.wait_ge(s3_read, j + 1)
                link(V.tensor_reduce(mx3[:, k, :], keys, AX_X, ALU.max))
                V.tensor_tensor(keys, keys, mx3[:, k, :].unsqueeze(2).to_broadcast([P, G * BL, KN]),
                                ALU.subtract).then_inc(s3_shift, 1)

            def block_probs(j):
                k = j % 2
                keys = s3[k].rearrange("p (s k) -> p s k", k=KN)
                a_ = a3[k].rearrange("p (s k) -> p s k", k=C)
                dve.wait_ge(s3_exp, j + 1)
                link(V.tensor_reduce(sm3[:, k, :], keys, AX_X, ALU.add))
                link(V.reciprocal(sm3[:, k, :], sm3[:, k, :]))
                link(V.tensor_scalar(mx3[:, k, :], keys[:, :, C:KN].rearrange("p s k -> p (s k)"), 1.0 / C, None,
                                     ALU.mult))
                link(V.tensor_tensor(a_, keys[:, :, 0:C], mx3[:, k, :].unsqueeze(2)
                                     .to_broadcast([P, G * BL, C]), ALU.add))
                link(V.tensor_tensor(a_, a_, sm3[:, k, :].unsqueeze(2).to_broadcast([P, G * BL, C]), ALU.mult))
                link(V.tensor_tensor(a3[k].rearrange("p (g t) -> p g t", g=G),
                                     a3[k].rearrange("p (g t) -> p g t", g=G),
                                     flat3(gate3).unsqueeze(1).to_broadcast([P, G, BL * C]), ALU.add))
                if j >= 2:
                    dve.wait_ge(o3_ps, j - 1)
                V.transpose(at3[k], a3[k]).then_inc(at3_sb, 1)

            block_scores(0)
            for j in range(1, J):
                block_scores(j)
                block_probs(j - 1)
            block_probs(J - 1)
            dve.wait_ge(p3_ps, 1)
            V.scalar_tensor_tensor(X[:, :], bank(2, 2), b_p3[:, :], X[:, :], ALU.add,
                                   ALU.add).then_inc(x_new, 1)

            dve.wait_ge(rstd_sb, 6)
            link(V.tensor_tensor(h4, bank(0, 2), rstd[:, :], ALU.mult))
            dve.wait_ge(dma_m, 32)
            link(V.tensor_copy(steps_f.rearrange("p t o -> p (t o)"), steps_u8))

            def find_step(link):
                link(V.transpose(h_t, h4[0:C, 0:C]))
                link(V.max(best8[:, :], h_t[0:1, 0:NOPS]))
                link(V.max_index(best8_i[:, :], best8[:, :], h_t[0:1, 0:NOPS]))
                link(V.tensor_copy(op_f[:, :], best8_i[:, 0:1]))
                link(V.tensor_scalar(one_hot[:, :], ops_at[:, :], op_f[:, :], None, ALU.is_equal))
                link(V.tensor_tensor(picked, steps_f, one_hot[:, 0:NOPS].unsqueeze(1)
                                     .to_broadcast([1, 2 * NB, NOPS]), ALU.mult))
                link(V.tensor_reduce(flags[:, :, :].rearrange("p k b -> p (k b)"), picked, AX_X, ALU.max))
                link(V.tensor_tensor(open_[:, :], flags[:, 0, :], flags[:, 1, :], ALU.max))
                link(V.tensor_scalar(one_hot[:, :], ops_at[:, :], from_block[:, :], None, ALU.is_ge))
                link(V.tensor_tensor(open_[:, :], open_[:, :], one_hot[:, :], ALU.mult))
                link(V.tensor_tensor(open_[:, :], open_[:, :], ops_back[:, :], ALU.mult))
                link(V.tensor_reduce(found[:, :], open_[:, :], AX_X, ALU.max))
                link(V.tensor_scalar(next_block[:, :], found[:, :], -1.0, float(NONE), ALU.mult, ALU.add))
                link(V.tensor_scalar(one_hot[:, :], ops_at[:, :], next_block[:, :], None, ALU.is_equal))
                link(V.tensor_tensor(flags[:, :, :], flags[:, :, :], one_hot[:, :].unsqueeze(1)
                                     .to_broadcast([1, 2, NB]), ALU.mult))
                link(V.tensor_reduce(ctrl_f[:, 1:3], flags[:, :, :], AX_X, ALU.max))
                link(V.tensor_scalar(ctrl_f[:, 0:1], found[:, :], 0.0, None, ALU.is_gt))
                link(V.scalar_tensor_tensor(ctrl_f[:, 3:4], next_block[:, :], float(NOPS), op_f[:, :],
                                            ALU.mult, ALU.add))
                link(V.tensor_scalar(ctrl_f[:, 3:4], ctrl_f[:, 3:4], float(STEPS - 1), None, ALU.min))
                link(V.tensor_scalar(from_block[:, :], next_block[:, :], 1.0, None, ALU.add))
                return V.tensor_copy(ctrl[:, :], ctrl_f[:, :])

            FIND = 20
            find_step(link).then_inc(ctrl_ready, 1)

            def counted(chain, base, done):
                def link_(ins):
                    done[0] += 1
                    ins.then_inc(chain, 1)
                    hold(dve, chain, base + done[0])
                return link_

            active = dve.alloc_register("dve_active")
            hold(dve, ctrl_ready, 1)
            dve.reg_load(active, ctrl[0:1, 0:1])
            with dve.Fori(0, NB) as i:
                with dve.If_ne(active, 0):
                    attends = dve.value_load(ctrl[0:1, 1:2], min_val=0, max_val=1)
                    feeds = dve.value_load(ctrl[0:1, 2:3], min_val=0, max_val=1)
                    ATTN_LINKS = 3 * B + 1
                    with dve.If(attends > 0):
                        done = [0]
                        alink = counted(attn_chain, ATTN_LINKS * i, done)
                        hold(dve, attn_pe, ATTN_PE * i + 1)
                        V.tensor_copy(k4, bank(2, 2)).then_inc(attn_dve, 1)
                        for b in range(B):
                            hold(dve, attn_pe, ATTN_PE * i + 3 + 3 * b)
                            alink(V.tensor_reduce(mx4, bank(0).rearrange("p (h k) -> p h k", h=2), AX_X,
                                                  ALU.max))
                            V.tensor_scalar(nm4, mx4, -float(C) ** -0.5, None, ALU.mult).then_inc(attn_dve, 1)
                            hold(dve, attn_act, ATTN_ACT * i + 3 + b)
                            alink(V.reciprocal(mx4, sm4))
                            V.tensor_tensor(p4.rearrange("p (h k) -> p h k", h=2),
                                            p4.rearrange("p (h k) -> p h k", h=2),
                                            mx4.unsqueeze(2).to_broadcast([P, 2, N]),
                                            ALU.mult).then_inc(attn_dve, 1)
                            hold(dve, attn_pe, ATTN_PE * i + 4 + 3 * b)
                            alink(V.tensor_copy(pt4, bank(1)))
                            dve.sem_inc(attn_dve, 1)
                        hold(dve, attn_pe, ATTN_PE * i + 3 + 3 * B)
                        V.tensor_copy(h4, bank(0, 2)).then_inc(attn_dve, 1)
                        hold(dve, attn_dve, ATTN_DVE * i + 2 + 3 * B)
                        V.tensor_copy(mx4, nm4).then_inc(attn_chain, 1)
                        assert done[0] + 1 == ATTN_LINKS
                    with dve.Else():
                        dve.sem_inc(attn_dve, ATTN_DVE)
                        dve.sem_inc(attn_chain, ATTN_LINKS)
                    done = [1]
                    slink = counted(step_chain, (FIND + 1) * i, done)
                    with dve.If(feeds > 0):
                        hold(dve, dma_f, N_STEP * i + N_STEP)
                        hold(dve, ffn_pe, FFN_PE * i + G + 1)
                        V.tensor_scalar(h4, bank(0, 2), b2_4, None, ALU.add).then_inc(step_chain, 1)
                    with dve.Else():
                        dve.sem_inc(step_chain, 1)
                    hold(dve, step_chain, (FIND + 1) * i + 1)
                    find_step(slink).then_inc(ctrl_ready, 1)
                    assert done[0] == FIND + 1, done[0]
                    hold(dve, ctrl_ready, i + 2)
                    dve.reg_load(active, ctrl[0:1, 0:1])
            V.tensor_tensor(X[:, :], X[:, :], h4, ALU.add).then_inc(x_new, 1)

        @block.tensor
        def _(pe):
            T = nc.tensor

            def both_halves(k, weight, src):
                for h in range(2):
                    last = T.matmul(bank(k + h), weight, src[:, h * HALF:(h + 1) * HALF],
                                    start=True, stop=True)
                return last

            pe.wait_ge(bd0_ready, 1)
            pe.wait_ge(dma_x, 16)
            for k in range(3):
                both_halves(2 * k, bd0[:, k, :], X).then_inc(proj0, 1)
            pe.wait_ge(theta_sb, 1)
            pe.wait_ge(pooled, 2)
            for j in range(J):
                for h in range(2):
                    t = 2 * j + h
                    last = T.matmul(bank(4 + t // 2)[:, N * (t % 2):N * (t % 2) + N],
                                    theta[:, j * N + h * P:j * N + h * P + P],
                                    phi_bd[:, j, :, :].rearrange("p g m -> p (g m)"), start=True, stop=True)
            last.then_inc(logits0, 1)
            for j in range(J):
                for q in range(2):
                    t = 2 * j + q
                    last = T.matmul(bank(t // 4)[:, P * (t % 4):P * (t % 4) + P],
                                    gp_bd[:, j, 2 * q:2 * q + 2, :].rearrange("p g m -> p (g m)"),
                                    wo_bd[:, :], start=True, stop=True)
            last.then_inc(vb_ps, 1)
            pe.wait_ge(prob0, 1)
            pe.wait_ge(vb_sb, 1)
            pe.wait_ge(consts, 2)
            for j in range(J):
                for h in range(2):
                    for q in range(2):
                        at = (2 * j + h) * N + q * P
                        last = T.transpose(bank(j)[:, q * N + h * P:q * N + h * P + P], att[:, at:at + P],
                                           ident[:, :])
            last.then_inc(attT_ps, 1)
            pe.wait_ge(attT_sb, 1)
            for j in range(J):
                for q in range(2):
                    last = T.matmul(bank(4 + j // 2)[:, N * (j % 2):N * (j % 2) + N],
                                    vb[:, (2 * j + q) * P:(2 * j + q + 1) * P],
                                    att_t[:, (2 * j + q) * N:(2 * j + q + 1) * N],
                                    start=(q == 0), stop=(q == 1))
            last.then_inc(o0_ps, 1)

            def channel_norm(k, src):
                pe.wait_ge(norm_in, k)
                both_halves(0, centerer[:, :], src).then_inc(centred, 1)
                pe.wait_ge(squared, k)
                both_halves(2, averager[:, :], sq).then_inc(variance, 1)

            pe.wait_ge(dma_w1, n_w1)
            flat = lambda t: t[:, :, :].rearrange("p a b -> p (a b)")
            T.matmul(bank(7)[:, 0:P], flat(wx_rows), flat(wdt_t), start=True, stop=True).then_inc(wdt_ps, 1)
            channel_norm(1, xn)
            pe.wait_ge(x1_sb, 1)
            both_halves(4, permuter[:, :], xn).then_inc(x2_ps, 1)
            pe.wait_ge(x12, 1)
            pe.wait_ge(w1_dve, 1)
            for i in range(8):
                g, jp = i // 2, i % 2
                k = 4 * (i % 2)
                r = slice(C * g, C * g + C)
                if i >= 2:
                    pe.wait_ge(xi_used, i - 1)
                    pe.wait_ge(z_used, i - 1)
                for part in range(2):
                    for v, src in ((0, x1), (1, x2)):
                        last = T.matmul(bank(k + part)[64 * v:64 * v + 64, :],
                                        win_t[r, 64 * part:64 * part + 64],
                                        src[r, jp * HALF:(jp + 1) * HALF], start=True, stop=True)
                    last.then_inc(xz_ps, 1)

            def clear_planes():
                for g in range(G):
                    r = slice(C * g, C * g + C)
                    last = T.matmul(bank(4 + g)[:, 0:2 * P], zero_bf[r, :],
                                    zero_bf[r, :].unsqueeze(1).to_broadcast([C, 2, P]), start=True,
                                    stop=False, skip_group_check=True)
                return last

            def put_chunk(k, ends):
                for s_ in range(CHUNK):
                    for h in range(2):
                        for g in range(G):
                            r = slice(C * g, C * g + C)
                            last = T.matmul(
                                bank(4 + g)[:, 0:2 * P].rearrange("p (k h c) -> p k h c", h=2, c=C)[:, :, h, :],
                                row_hot[k][r, s_, h * P:(h + 1) * P],
                                plane_hot[k][r, s_, :, :], start=False, stop=(ends and s_ == CHUNK - 1),
                                skip_group_check=True)
                return last

            pe.wait_ge(xi_used, 8)
            pe.wait_ge(z_used, 8)
            pe.wait_ge(consts, 2)
            clear_planes()
            pe.wait_ge(cols_sb, 1)
            T.matmul(bank(4)[0:1, HALF - 1:HALF], over[:, 0:1], one_col[:, :], start=True, stop=True,
                     skip_group_check=True)
            for q in range(SLOTS // CHUNK):
                pe.wait_ge(rows_sb, q + 1)
                pe.wait_ge(hot_sb, q + 1)
                ins = put_chunk(q % 2, q == SLOTS // CHUNK - 1)
                ins.then_inc(hot_used if q < SLOTS // CHUNK - 1 else planes_ps, 1)
            pe.wait_ge(u_sb, J)
            pe.wait_ge(xi_used, 8)
            pe.wait_ge(z_used, 8)
            pe.wait_ge(u_sb, J)
            for j in range(J):
                if j >= 2:
                    pe.wait_ge(dt_parts, j - 1)
                both_halves(2 * (j % 2), w_dt[:, :], u_act[:, j * NT:(j + 1) * NT]).then_inc(dt_ps, 1)
            pe.wait_ge(w1_pool, 1)
            pe.wait_ge(dt_parts, J)
            for i in range(J * S):
                j, n = i // S, i % S
                if i == 1:
                    pe.wait_ge(tab_dve, 1)
                if i >= 2:
                    pe.wait_ge(dbu_done, i - 1)
                both_halves(4 * (i % 2), w_bc[:, n, :], u_act[:, j * NT:(j + 1) * NT]).then_inc(bc_ps, 1)
                if i >= 2:
                    pe.wait_ge(hc_done, i - 1)
                both_halves(4 * (i % 2) + 2, w_bc[:, S + n, :],
                            u_act[:, j * NT:(j + 1) * NT]).then_inc(bc_ps, 1)
            pe.wait_ge(gated, J)
            for b in range(B):
                j, g = b // G, b % G
                last = T.matmul(bank(j // 2)[C * g:C * g + C, N * (j % 2):N * (j % 2) + N], wout_t[:, :],
                                z_act[:, b * N:(b + 1) * N], start=True, stop=True)
            last.then_inc(mo_ps, 1)
            channel_norm(2, xn)
            pe.wait_ge(normed, 1)
            both_halves(4, bd0[:, 3, :], xn).then_inc(wp_ps, 1)

            def stream_norm(k, news):
                pe.wait_ge(x_new, news)
                both_halves(0, centerer[:, :], X).then_inc(centred, 1)
                pe.wait_ge(squared, k)
                both_halves(2, averager[:, :], sq).then_inc(variance, 1)

            pe.wait_ge(over_sb, 1)
            more = pe.value_load(over_i[0:1, 0:1], min_val=0, max_val=P)
            with pe.If(more > 0):
                with pe.Fori(0, EDGES // (P * GW)) as t:
                    pe.wait_ge(gen_slots, t + 1)
                    pe.sem_inc(gen_passed, 1)
                    clear_planes()
                    put_chunk(0, True).then_inc(gen_ps, 1)
            pe.wait_ge(dma_w2, n_w2)
            pe.wait_ge(wu_ready, 1)
            for h in range(H2):
                for g in range(G):
                    r = slice(C * g, C * g + C)
                    T.matmul(bank(6)[r, C * h:C * h + C], wk2[:, h, :], wq2[:, h, :], start=True, stop=True)
                    last = T.matmul(bank(7)[r, C * h:C * h + C], wv2[:, h, :], wu_t[:, C * h:C * h + C],
                                    start=True, stop=True)
            last.then_inc(w2_ps, 1)
            stream_norm(3, 2)
            pe.wait_ge(normed, 2)
            pe.wait_ge(w2_sb, 1)
            for h in range(H2):
                if h >= 4:
                    pe.wait_ge(km_sb, h - 3)
                both_halves(2 * (h % 4), w_km[:, h, :], xn).then_inc(km_ps, 1)
            pe.wait_ge(km_sb, H2)
            pe.wait_ge(w2_mask, 1)
            for k in range(2):
                T.matmul(bank(6 + k), zero_bf[:, :], mask_bf[:, :, :].rearrange("p i t -> p (i t)"),
                         start=True, stop=False, skip_group_check=True)

            def unit(u):
                return u // 4, u // 2 % 2, u % 2

            def unit_scores(u):
                g, jp, hg = unit(u)
                r = slice(C * g, C * g + C)
                k = u % 2
                if u >= 2:
                    pe.wait_ge(s2_read, u - 1)
                for d in range(2):
                    j = 2 * jp + d
                    sb_ = bank(2 * k + d)
                    T.matmul(sb_, ident_bf[:, :], mask_bf[:, :, :].rearrange("p i t -> p (i t)"),
                             start=True, stop=False, skip_group_check=True)
                    for m in range(WT):
                        width = 2 * C if m < WT - 1 else C
                        q0 = j * N + m * C
                        last = T.matmul(sb_[:, 2 * C * m + C:2 * C * m + C + width],
                                        km[r, j * WT + m, 4 * hg:4 * hg + 4, :].rearrange("p h k -> p (h k)"), xn[r, q0:q0 + width],
                                        start=False, stop=(m == WT - 1), skip_group_check=True)
                last.then_inc(s2_ps, 1)
                if u >= 2:
                    pe.wait_ge(v2_sb, u - 1)
                T.matmul(bank(4 + k), w_vu[r, 4 * hg * C:4 * (hg + 1) * C],
                         xn[r, jp * HALF:(jp + 1) * HALF], start=True, stop=True).then_inc(v2_ps, 1)

            def unit_output(u):
                g, jp, hg = unit(u)
                r = slice(C * g, C * g + C)
                k = u % 2
                pe.wait_ge(p2_sb, u + 1)
                pe.wait_ge(v2_sb, u + 1)
                for d in range(2):
                    for m in range(WT):
                        width = 2 * C if m < WT - 1 else C
                        q0 = d * N + m * C
                        p0 = d * HALF + 2 * C * m + C
                        last = T.matmul(bank(6 + jp)[r, q0:q0 + width],
                                        vm_buf[k][:, d * N + m * C:d * N + m * C + C],
                                        pt_buf[k][:, p0:p0 + width], start=False,
                                        stop=(u == 15 and m == WT - 1), skip_group_check=True)
                last.then_inc(o2_ps, 1)

            for u in range(16):
                unit_scores(u)
                if u >= 2:
                    unit_output(u - 2)
            unit_output(14)
            unit_output(15)

            stream_norm(4, 3)
            pe.wait_ge(normed, 3)
            rb = rb_row[:, :, :].rearrange("p g e -> p (g e)")
            eb = eb_row[:, :, :].rearrange("p g e -> p (g e)")
            pe.wait_ge(dma_ex, n_ex)
            ebd = e_bd[:, :, :].rearrange("p g e -> p (g e)")
            for t in range(TT):
                o = bank(4)[:, t * G * E2:(t + 1) * G * E2]
                T.matmul(o, one_row[:, :], rb, start=True, stop=False)
                last = T.matmul(o, xn[:, t * P:t * P + P], r_bd[:, :, :].rearrange("p g e -> p (g e)"),
                                start=False, stop=True)
            last.then_inc(lg_ps, 1)

            def combine(t):
                pe.wait_ge(ex_sb, t + 1)
                for e in range(E2):
                    last = T.matmul(bank(2 + t // 4)[:, P * (t % 4):P * (t % 4) + P], mix[t % 2][:, P * e:P * e + P],
                                    ident[:, :], start=(e == 0), stop=(e == E2 - 1))
                last.then_inc(y2_part, 1)

            for t in range(TT):
                if t == 0:
                    pe.wait_ge(lg_shifted, 1)
                if t >= 2:
                    pe.wait_ge(ex_sb, t - 1)
                for k in range(2):
                    o = bank(4 + 2 * (t % 2) + k)
                    T.matmul(o, one_row[:, :], eb[:, k * HALF:(k + 1) * HALF], start=True, stop=False)
                    last = T.matmul(o, xn[:, t * P:t * P + P], ebd[:, k * HALF:(k + 1) * HALF], start=False,
                                    stop=True)
                last.then_inc(ex_ps, 1)
                if t >= 1:
                    combine(t - 1)
            combine(TT - 1)

            stream_norm(5, 4)
            pe.wait_ge(normed, 4)
            pe.wait_ge(dma_w3, n_w3)
            both_halves(4, w_q3[:, :], xn)
            both_halves(6, w_k3[:, :], xn).then_inc(qkv3_ps, 1)
            for jp in range(2):
                if jp == 1:
                    pe.wait_ge(q3_sb, 1)
                    pe.wait_ge(k3_sb, 1)
                for g in range(G):
                    last = T.matmul(bank(4 * jp + g), w_v3[C * g:C * g + C, :, :].rearrange("p h c -> p (h c)"),
                                    xn[C * g:C * g + C, jp * HALF:(jp + 1) * HALF], start=True, stop=True)
                last.then_inc(v3_ps, 1)

            def block_scores(j):
                k = j % 2
                for g in range(G):
                    r = slice(C * g, C * g + C)
                    for b in range(BL):
                        last = T.matmul(bank(4 * k + g)[:, b * KN:(b + 1) * KN],
                                        q3[r, j * BL + b, :, :].rearrange("p h q -> p (h q)"),
                                        k3[r, j * BL + b, :], start=True, stop=True)
                last.then_inc(s3_ps, 1)

            def block_output(j):
                k = j % 2
                pe.wait_ge(at3_sb, j + 1)
                for g in range(G):
                    for b in range(BL):
                        v0 = (g * J + j) * N + b * C
                        last = T.matmul(bank(4 * k)[C * g:C * g + C, b * C:b * C + C],
                                        vm3[:, v0:v0 + C], at3[k][:, (g * BL + b) * C:(g * BL + b + 1) * C],
                                        start=True, stop=True)
                last.then_inc(o3_ps, 1)

            pe.wait_ge(k3_node, 1)
            for j in range(J):
                if j < 2:
                    pe.wait_ge(v3_sb, j + 1)
                if j >= 2:
                    pe.wait_ge(o3_sb, j - 1)
                block_scores(j)
                if j == 0:
                    pe.wait_ge(vm3_sb, 1)
                if j >= 1:
                    block_output(j - 1)
            block_output(J - 1)
            pe.wait_ge(o3_sb, J)
            both_halves(2, w_p3[:, :], o3).then_inc(p3_ps, 1)

            stream_norm(6, 5)

            def per_batch(k, weight, src):
                for g in range(G):
                    r = slice(C * g, C * g + C)
                    for h in range(2):
                        last = T.matmul(bank(k + h)[r, :], weight[r, :], src[r, h * HALF:(h + 1) * HALF],
                                        start=True, stop=True)
                return last

            active = pe.alloc_register("pe_active")
            hold(pe, ctrl_ready, 1)
            pe.reg_load(active, ctrl[0:1, 0:1])
            with pe.Fori(0, NB) as i:
                with pe.If_ne(active, 0):
                    attends = pe.value_load(ctrl[0:1, 1:2], min_val=0, max_val=1)
                    feeds = pe.value_load(ctrl[0:1, 2:3], min_val=0, max_val=1)
                    with pe.If(attends > 0):
                        hold(pe, dma_fa, N_STEP * i + N_STEP)
                        per_batch(0, w4[:, 0, :], h4)
                        per_batch(2, w4[:, 1, :], h4).then_inc(attn_pe, 1)
                        for g in range(G):
                            r = slice(C * g, C * g + C)
                            for t in range(TT):
                                last = T.matmul(bank(4 + g)[:, t * C:(t + 1) * C], h4[r, t * P:(t + 1) * P],
                                                w4[r, 2, :], start=True, stop=True)
                        last.then_inc(attn_pe, 1)
                        hold(pe, attn_act, ATTN_ACT * i + 2)
                        hold(pe, attn_dve, ATTN_DVE * i + 1)
                        for b in range(B):
                            g, j = b // J, b % J
                            r = slice(C * g, C * g + C)
                            for h in range(2):
                                q0 = j * N + h * P
                                last = T.matmul(bank(0)[:, h * N:(h + 1) * N], q4[r, q0:q0 + P],
                                                k4[r, j * N:(j + 1) * N], start=True, stop=True)
                            last.then_inc(attn_pe, 1)
                            hold(pe, attn_dve, ATTN_DVE * i + 3 + 3 * b)
                            for kh in range(2):
                                for qh in range(2):
                                    last = T.transpose(bank(1)[:, kh * N + qh * P:kh * N + qh * P + P],
                                                       p4[:, qh * N + kh * P:qh * N + kh * P + P],
                                                       ident[:, :])
                            last.then_inc(attn_pe, 1)
                            hold(pe, attn_dve, ATTN_DVE * i + 4 + 3 * b)
                            for kh in range(2):
                                v0 = ((g * J + j) * 2 + kh) * C
                                last = T.matmul(bank(2 + j // 2)[r, (j % 2) * N:(j % 2) * N + N],
                                                v4[:, v0:v0 + C], pt4[:, kh * N:(kh + 1) * N],
                                                start=(kh == 0), stop=(kh == 1))
                            last.then_inc(attn_pe, 1)
                        hold(pe, attn_act, ATTN_ACT * i + 3 + B)
                        per_batch(0, w4[:, 3, :], y4).then_inc(attn_pe, 1)
                    with pe.Else():
                        pe.sem_inc(attn_pe, ATTN_PE)
                    with pe.If(feeds > 0):
                        hold(pe, dma_f, N_STEP * i + N_STEP)
                        hold(pe, attn_dve, ATTN_DVE * i + ATTN_DVE)
                        for g in range(G):
                            r = slice(C * g, C * g + C)
                            for h in range(2):
                                last = T.matmul(bank(2 * g + h), w1_4[r, :], h4[r, h * HALF:(h + 1) * HALF],
                                                start=True, stop=True)
                            last.then_inc(ffn_pe, 1)
                        for g in range(G):
                            hold(pe, ffn_act, G * i + g + 1)
                            for h in range(2):
                                last = T.matmul(bank(h)[C * g:C * g + C, :], w2_4,
                                                hid[:, g * NT + h * HALF:g * NT + (h + 1) * HALF],
                                                start=True, stop=True)
                        last.then_inc(ffn_pe, 1)
                    with pe.Else():
                        pe.sem_inc(ffn_pe, FFN_PE)
                    hold(pe, ctrl_ready, i + 2)
                    pe.reg_load(active, ctrl[0:1, 0:1])


_INS = [
    'x', 'L0_conv_w_theta', 'L0_conv_w_phi', 'L0_conv_w_g',
    'L0_conv_w_o', 'L0_conv_gamma', 'L1_conv_gamma', 'L1_conv_beta',
    'L1_conv_W_in', 'L1_conv_conv_w', 'L1_conv_conv_b', 'L1_conv_W_x',
    'L1_conv_W_dt', 'L1_conv_b_dt', 'L1_conv_A_log', 'L1_conv_D_skip',
    'L1_conv_W_out', 'L1_conv_W_p', 'L1_conv_b_p', 'L1_conv_s1',
    'L1_conv_s2', 'L2_attn_Wq', 'L2_attn_Wk', 'L2_attn_Wv',
    'L2_attn_Wu', 'L2_attn_bu', 'L2_ffn_router_w', 'L2_ffn_router_b',
    'L2_ffn_expert_w', 'L2_ffn_expert_b', 'L3_attn_edge_index', 'L3_attn_edge_values',
    'L3_attn_qkv_w', 'L3_attn_qkv_b', 'L3_attn_proj_w', 'L3_attn_proj_b',
    'L3_attn_gate_w', 'L3_attn_gate_b', 'L3_ffn_ffn_w1', 'L3_ffn_ffn_b1',
    'L3_ffn_ffn_w2', 'L3_ffn_ffn_b2', 'L3_ffn_wq', 'L3_ffn_wk',
    'L3_ffn_wv', 'L3_ffn_wo', 'L3_ffn_attn_mask', 'L3_ffn_ffn_mask']
_OUT = (16, 32, 16, 16)


def kernel(**inputs):
    import numpy as _np
    import concourse.bacc as _bacc
    from concourse import mybir as _mybir
    from concourse.bass_utils import run_bass_kernel_spmd as _run

    nc = _bacc.Bacc("TRN2", target_bir_lowering=False, num_devices=1)
    arrays, aps = {}, {}
    for name in _INS:
        a = _np.ascontiguousarray(inputs[name])
        arrays[f"in_{name}"] = a
        aps[name] = nc.dram_tensor(f"in_{name}", a.shape, _mybir.dt.from_np(a.dtype), kind="ExternalInput").ap()
    out = nc.dram_tensor("out_0", _OUT, _mybir.dt.float32, kind="ExternalOutput").ap()
    hybrid_kernel(nc, aps, out)
    r = _run(nc, [arrays], core_ids=[0])
    return r.results[0]["out_0"]
```

```python
from contextlib import ExitStack

import concourse.bass as bass
from concourse import mybir

ALU = mybir.AluOpType
ACT = mybir.ActivationFunctionType
F32 = mybir.dt.float32
BF16 = mybir.dt.bfloat16
I32 = mybir.dt.int32
U32 = mybir.dt.uint32
U8 = mybir.dt.uint8
AX_X = mybir.AxisListType.X

P = 128
C = 32
G = P // C
J = 4
N = 256
NT = J * N
HALF = 512
B = G * J


def broadcast_rows(ap, rows):
    return bass.AP(ap.tensor, ap.offset, [[0, rows]] + [list(x) for x in ap.ap])


def hybrid_kernel(nc, a, out):
    with ExitStack() as ctx:
        def sb(name, shape, dt=F32):
            return ctx.enter_context(nc.sbuf_tensor(name, shape, dt))

        def sem(name):
            return ctx.enter_context(nc.semaphore(name))

        ps = ctx.enter_context(nc.psum_tensor("ps", [P, 8, HALF], F32))

        def bank(k, n=1):
            return ps[:, k:k + n, :].rearrange("p a b -> p (a b)")

        ident = sb("ident", [P, P])
        averager = sb("averager", [P, P])
        centerer = sb("centerer", [P, P])
        permuter = sb("permuter", [P, P])
        half_mask = sb("half_mask", [P, P])
        one_row = sb("one_row", [1, P])
        one_col = sb("one_col", [P, 1])
        eps5 = sb("eps5", [P, 1])

        X = sb("X", [P, NT])
        xn = sb("xn", [P, NT])
        sq = sb("sq", [P, NT])
        rstd = sb("rstd", [P, NT])

        nat0 = sb("nat0", [P, 4, P])
        bd0 = sb("bd0", [P, 4, P])
        wo_nat = sb("wo_nat", [P, P])
        wo_bd = sb("wo_bd", [P, P])
        gamma0 = sb("gamma0", [P, 1])

        ln_g = sb("ln_g", [P, 1])
        ln_b = sb("ln_b", [P, 1])
        s1 = sb("s1", [P, 1])
        s2 = sb("s2", [P, 1])
        b_p = sb("b_p", [P, 1])
        win_nat = sb("win_nat", [P, 4, C])
        win_t = sb("win_t", [P, P])
        conv_w = sb("conv_w", [P, 4])
        conv_b = sb("conv_b", [P, 1])
        b_dt = sb("b_dt", [P, 1])
        d_skip = sb("d_skip", [P, 1])
        a_log = sb("a_log", [P, 16])
        a_neg = sb("a_neg", [P, 16])
        wx_t = sb("wx_t", [P, 34])
        wx_rows = sb("wx_rows", [2, 2, 64])
        wdt_t = sb("wdt_t", [2, 2, 64])
        w_dt = sb("w_dt", [P, P])
        S = 16
        PARTS = 3
        BC = PARTS * 2 * S
        w_rows = sb("w_rows", [P, 2, PARTS, 2, S])
        pick_state = sb("pick_state", [BC, S, 2, 64], BF16)
        less_1 = sb("less_1", [BC, 1])
        less_2 = sb("less_2", [BC, 1])
        skip_diag = sb("skip_diag", [P, P])
        late = sb("late", [P, 32 * P])
        parts = late[0:BC, :].bitcast(BF16).rearrange("p (k t) -> p k t", k=2)
        wout_nat = sb("wout_nat", [P, C])
        wout_t = sb("wout_t", [P, C])

        work = sb("work", [P, 23 * NT])

        def area(at, n):
            return work[:, at * NT:(at + n) * NT]

        theta = area(0, 1)
        pool_w = area(1, 1)
        phi_bd = area(2, 1).rearrange("p (j g m) -> p j g m", j=J, g=G)
        gp_bd = area(3, 1).rearrange("p (j g m) -> p j g m", j=J, g=G)
        att = area(4, 2)
        att_t = area(6, 2)
        vb = area(8, 1)
        mx0 = sb("mx0", [P, 32])
        sm0 = sb("sm0", [P, 32])
        rs0 = sb("rs0", [P, 32])
        xi_pad = work[:, 0:16 * 259].rearrange("p (b t) -> p b t", b=B)
        u_act = area(5, 4)
        z_act = area(9, 4)
        dt_act = area(13, 4)
        dtu = area(17, 4)
        rounded = [area(21, 1)[0:BC, k * HALF:(k + 1) * HALF].bitcast(BF16) for k in range(2)]
        rest = [area(k, 1)[0:BC, :] for k in range(2)]
        x1 = sb("x1", [P, NT])
        x2 = sb("x2", [P, NT])
        dA = sb("dA", [P, 2, NT])
        dBu = sb("dBu", [P, 2, NT])
        hst = sb("hst", [P, 2, NT])
        h_buf = [hst[:, 0, :], hst[:, 1, :], area(22, 1)]
        hC = sb("hC", [P, 2, NT])
        b_sb = sb("b_sb", [P, 2, NT])
        bn6 = sb("bn6", [P, J, 6])
        bn2 = sb("bn2", [P, J, 2])
        rs4 = sb("rs4", [P, J])

        H2 = 8
        WT = N // C
        wq2 = sb("wq2", [C, H2, C])
        wk2 = sb("wk2", [C, H2, C])
        wv2 = sb("wv2", [C, H2, C])
        wu_nat = sb("wu_nat", [C, H2 * C])
        wu_t = sb("wu_t", [C, H2 * C])
        w_km = sb("w_km", [P, H2, P])
        w_vu = sb("w_vu", [P, H2 * C])
        b_u = sb("b_u", [P, 1])
        win_mask = sb("win_mask", [P, 2 * C])
        mask_bf = sb("mask_bf", [P, WT, 2 * C], BF16)
        ident_bf = sb("ident_bf", [P, P], BF16)
        zero_bf = sb("zero_bf", [P, P], BF16)
        km = area(0, 8).rearrange("p (t h k) -> p t h k", h=H2, k=C)
        s2_buf = [area(8 + k, 1) for k in range(2)]
        pt_buf = [area(10 + k, 1) for k in range(2)]
        vm_buf = [area(12, 1)[:, k * HALF:(k + 1) * HALF] for k in range(2)]
        alone = area(17, 4).rearrange("p (g n) -> p g n", g=G)
        mx2 = sb("mx2", [P, 2, 16])
        sm2 = sb("sm2", [P, 2, 16])

        E2 = 8
        r_bd = sb("r_bd", [P, G, E2])
        e_bd = x1[:, :].rearrange("p (g e) -> p g e", g=G)
        rb_row = sb("rb_row", [1, G, E2])
        eb_bd = x2[0:G * E2, 0:P]
        gate_t = area(13, 1)[0:G * E2, :]
        rank = sb("rank", [P, E2])
        TT = 2 * J
        lg = area(16, 1)[:, 0 * N:1 * N].rearrange("p (t e) -> p t e", e=E2)
        sel_a = area(16, 1)[:, 1 * N:2 * N].rearrange("p (t e) -> p t e", e=E2)
        sel_b = area(16, 1)[:, 2 * N:3 * N].rearrange("p (t e) -> p t e", e=E2)
        gate = area(16, 1)[:, 3 * N:4 * N].rearrange("p (t e) -> p t e", e=E2)
        top1 = sb("top1", [P, TT * G])
        top2 = sb("top2", [P, TT * G])
        mix = [area(14 + k, 1) for k in range(2)]

        EDGES = a["L3_attn_edge_values"].shape[0]
        EF = EDGES // P
        EC = NT
        NCH = EF // EC
        SEG = 256
        SLOTS = 48
        CELLS = N * C
        UNDER_SCAN = 16
        EARLY = 32
        CHUNK = 16
        GW = CHUNK
        SYMBOL = 6
        SPACE = SYMBOL + 1
        PLANES = 4
        e_row = dA[:, :, :].bitcast(I32)
        e_col = dBu[:, :, :].bitcast(I32)
        e_x = hst[:, 0, :].bitcast(I32)
        e_u = hst[:, 1, :]
        e_key = hC[:, 0, :]
        cand = hC[:, 1, 0:SEG]
        k_a = hC[:, 1, SEG:2 * SEG].bitcast(I32)
        k_b = hC[:, 1, 2 * SEG:3 * SEG].bitcast(I32)
        k_key = hC[:, 1, 3 * SEG:4 * SEG].bitcast(I32)
        seg_place = sb("seg_place", [P, SEG])
        seg_bits = b_sb[:, 1, 0:SEG].bitcast(I32)
        top48 = b_sb[:, 1, SEG:SEG + SLOTS]
        d_a = b_sb[:, 1, 320:320 + SLOTS].bitcast(I32)
        d_b = b_sb[:, 1, 384:384 + SLOTS].bitcast(I32)
        d_c = b_sb[:, 1, 448:448 + SLOTS].bitcast(I32)
        d_row = b_sb[:, 1, 512:512 + SLOTS].bitcast(I32)
        d_col = b_sb[:, 1, 576:576 + SLOTS].bitcast(I32)
        d_ok = b_sb[:, 1, 640:640 + SLOTS]
        d_new = b_sb[:, 1, 704:704 + SLOTS]
        d_at = b_sb[:, 1, 960:960 + SLOTS]
        weighed = b_sb[:, 1, 768:768 + PLANES * SLOTS].rearrange("p (s k) -> p s k", k=PLANES)
        rows_at = sb("rows_at", [P, N], BF16)
        weight = sb("weight", [P, 1], I32)
        p_base = sb("p_base", [P, 2], I32)
        g_base = sb("g_base", [P, 2, G])
        halves = lambda t: t.bitcast(BF16).rearrange("p a b -> p (a b)")
        row_hot = [halves(t[:, :, :]).rearrange("p (s r) -> p s r", r=N) for t in (dA, dBu)]
        col_hot = hC[:, 0, 0:SLOTS * C // 2].bitcast(BF16).rearrange("p (s c) -> p s c", c=C)
        plane_hot = [hst[:, k, :].bitcast(BF16).rearrange("p (s k c) -> p s k c", k=PLANES, c=C)
                     for k in range(2)]
        planes = area(22, 1).rearrange("p (g r) -> p g r", g=G)
        inv_i = hC[:, 1, 0:G * 2 * C].rearrange("p (g c) -> p g c", g=G).bitcast(I32)
        symbols = hC[:, 1, G * 2 * C:G * 2 * C * PLANES].rearrange("p (g k c) -> p g k c", g=G, c=2 * C)
        g_row = dBu[:, 0, 0:GW].bitcast(I32)
        g_col = dBu[:, 1, 0:GW].bitcast(I32)
        g_x = hC[:, 0, SLOTS * C // 2:SLOTS * C // 2 + GW].bitcast(I32)
        g_u = hC[:, 0, SLOTS * C // 2 + GW:SLOTS * C // 2 + 2 * GW]
        over = sb("over", [P, 2])
        over_i = sb("over_i", [1, 1], I32)
        tab = sb("tab", [P, 2 * C])
        tab_new = sb("tab_new", [P, 2 * C])
        tab_i = sb("tab_i", [P, 2 * C], U32)
        hit = sb("hit", [P, 2, 2, C])
        bias_dram = nc.dram_tensor("cell_bias", [2, CELLS], F32, kind="Internal").ap()

        H3 = 4
        KN = C + 1
        BL = N // C
        w_q3, w_k3, w_p3 = nat0[:, 0, :], nat0[:, 1, :], nat0[:, 2, :]
        w_v3 = nat0[:, 3, :].rearrange("p (h c) -> p h c", c=C)
        b_q3 = sb("b_q3", [P, 1])
        b_k3 = sb("b_k3", [P, 1])
        b_v3 = sb("b_v3", [P, 1])
        b_p3 = sb("b_p3", [P, 1])
        gate_w3 = sb("gate_w3", [P, 1])
        gate_b3 = sb("gate_b3", [P, 1])
        head_scale = sb("head_scale", [P, H3])
        b_qh = sb("b_qh", [P, H3])
        diag = sb("diag", [P, C])
        wgt = late[:, 0:BL * KN].rearrange("p (b k) -> p b k", k=KN)
        msk = late[:, 3 * P:3 * P + BL * KN].rearrange("p (b k) -> p b k", k=KN)
        gate3 = late[:, 6 * P:8 * P].rearrange("p (b k) -> p b k", k=C)
        node_gate = sb("node_gate", [P, BL])
        added = work[:, 0:BL * G * KN].rearrange("p (b g k) -> p b g k", g=G, k=KN)
        k3 = work[:, 6 * NT:6 * NT + J * BL * G * KN].rearrange("p (s g k) -> p s g k", g=G, k=KN)
        q3 = area(2, 4).rearrange("p (s h q) -> p s h q", h=H3, q=C)
        flat2 = lambda t: t[:, :, :].rearrange("p a b -> p (a b)")
        v3 = [flat2(dA), flat2(dBu)]
        vm3 = [flat2(hst), flat2(hC)]
        s3 = [work[:, (14 + 2 * k) * NT:(14 + 2 * k) * NT + G * BL * KN] for k in range(2)]
        a3 = [area(18 + k, 1) for k in range(2)]
        at3 = [area(20 + k, 1) for k in range(2)]
        o3 = area(22, 1)
        mx3 = sb("mx3", [P, 2, 32])
        sm3 = sb("sm3", [P, 2, 32])

        NB, NOPS = a["L3_ffn_attn_mask"].shape
        STEPS = NB * NOPS
        F = a["L3_ffn_ffn_w1"].shape[-1]
        ROUNDS = 6
        assert ROUNDS * ROUNDS >= NB
        NONE = 64
        h4 = area(0, 1)
        hid = area(1, 4)
        q4 = area(5, 1)
        k4 = area(6, 1)
        v4 = area(7, 1)
        p4 = area(8, 1)[:, 0:HALF]
        pt4 = area(9, 1)[:, 0:HALF]
        y4 = area(10, 1)
        w4 = area(11, 1)[:, 0:4 * C].rearrange("p (k c) -> p k c", c=C)
        w1_4 = area(11, 1)[:, HALF:HALF + F]
        w2_4 = area(11, 1)[:, HALF + F:HALF + F + C]
        b1_4 = area(11, 1)[:, HALF + F + C:HALF + F + C + 1]
        b2_4 = area(11, 1)[:, HALF + F + C + 8:HALF + F + C + 9]
        h_t = area(12, 1)[0:C, 0:C]
        mx4 = area(12, 1)[:, 64:66]
        nm4 = area(12, 1)[:, 72:74]
        sm4 = area(12, 1)[:, 80:82]
        steps_u8 = late[0:1, 1024:1024 + 320].bitcast(U8)[:, 0:2 * STEPS]
        steps_f = late[0:1, 1408:1408 + 2 * STEPS].rearrange("p (t o) -> p t o", o=NOPS)
        picked = late[0:1, 2688:2688 + 2 * STEPS].rearrange("p (t o) -> p t o", o=NOPS)
        ops_at = sb("ops_at", [1, NB])
        ops_back = sb("ops_back", [1, NB])
        best8 = sb("best8", [1, 8])
        best8_i = sb("best8_i", [1, 8], U32)
        op_f = sb("op_f", [1, 1])
        one_hot = sb("one_hot", [1, NB])
        flags = sb("flags", [1, 2, NB])
        open_ = sb("open_", [1, NB])
        from_block = sb("from_block", [1, 1])
        found = sb("found", [1, 1])
        next_block = sb("next_block", [1, 1])
        ctrl_f = sb("ctrl_f", [1, 4])
        ctrl = sb("ctrl", [1, 4], I32)

        dma_fa = sem("dma_fa")
        dma_f = sem("dma_f")
        dma_m = sem("dma_m")
        ctrl_ready = sem("ctrl_ready")
        loop_passed = sem("loop_passed")
        step_chain = sem("step_chain")
        attn_chain = sem("attn_chain")
        ffn_pe = sem("ffn_pe")
        ffn_act = sem("ffn_act")
        attn_pe = sem("attn_pe")
        attn_act = sem("attn_act")
        attn_dve = sem("attn_dve")
        dma_e = [sem(f"dma_e{k}") for k in range(2)]
        e_used = sem("e_used")
        place_sb = sem("place_sb")
        cols_sb = sem("cols_sb")
        rows_sb = sem("rows_sb")
        hot_sb = sem("hot_sb")
        hot_used = sem("hot_used")
        planes_ps = sem("planes_ps")
        planes_sb = sem("planes_sb")
        planes_t = sem("planes_t")
        gen_sb = sem("gen_sb")
        gen_t = sem("gen_t")
        over_sb = sem("over_sb")
        tab_dve = sem("tab_dve")
        gathered = sem("gathered")
        gathered_again = sem("gathered_again")
        hit_sb = sem("hit_sb")
        bias_out = sem("bias_out")
        bias_in = sem("bias_in")
        gen_in = sem("gen_in")
        gen_slots = sem("gen_slots")
        gen_ps = sem("gen_ps")
        gen_done = sem("gen_done")
        gen_chain = sem("gen_chain")
        gen_frame = sem("gen_frame")
        gen_passed = sem("gen_passed")
        dma_w3 = sem("dma_w3")
        w3_zero = sem("w3_zero")
        qkv3_ps = sem("qkv3_ps")
        q3_sb = sem("q3_sb")
        k3_zero = sem("k3_zero")
        v3_ps = sem("v3_ps")
        v3_sb = sem("v3_sb")
        k3_node = sem("k3_node")
        vm3_sb = sem("vm3_sb")
        s3_ps = sem("s3_ps")
        s3_read = sem("s3_read")
        s3_shift = sem("s3_shift")
        s3_exp = sem("s3_exp")
        at3_sb = sem("at3_sb")
        o3_ps = sem("o3_ps")
        o3_sb = sem("o3_sb")
        p3_ps = sem("p3_ps")
        dma_w2 = sem("dma_w2")
        dma_ex = sem("dma_ex")
        ex_zero = sem("ex_zero")
        w2_zero = sem("w2_zero")
        w2_mask = sem("w2_mask")
        wu_ready = sem("wu_ready")
        w2_ps = sem("w2_ps")
        w2_sb = sem("w2_sb")
        alone_zero = sem("alone_zero")
        alone_sb = sem("alone_sb")
        km_ps = sem("km_ps")
        km_sb = sem("km_sb")
        s2_ps = sem("s2_ps")
        v2_ps = sem("v2_ps")
        s2_read = sem("s2_read")
        v2_sb = sem("v2_sb")
        s2_shifted = sem("s2_shifted")
        s2_exp = sem("s2_exp")
        s2_scale = sem("s2_scale")
        s2_prob = sem("s2_prob")
        p2_sb = sem("p2_sb")
        o2_ps = sem("o2_ps")
        lg_ps = sem("lg_ps")
        lg_shifted = sem("lg_shifted")
        lg_exp = sem("lg_exp")
        gate_sb = sem("gate_sb")
        gate_ps = sem("gate_ps")
        gate_copied = sem("gate_copied")
        ex_ps = sem("ex_ps")
        ex_sb = sem("ex_sb")
        y2_part = sem("y2_part")
        dma_x = sem("dma_x")
        dma_w0 = sem("dma_w0")
        dma_w1 = sem("dma_w1")
        zeroed = sem("zeroed")
        consts = sem("consts")
        pool_chain = sem("pool_chain")
        dve_chain = sem("dve_chain")
        act_chain = sem("act_chain")
        bd0_ready = sem("bd0_ready")
        proj0 = sem("proj0")
        theta_sb = sem("theta_sb")
        pooled = sem("pooled")
        logits0 = sem("logits0")
        vb_ps = sem("vb_ps")
        vb_sb = sem("vb_sb")
        shifted0 = sem("shifted0")
        exp0 = sem("exp0")
        prob0 = sem("prob0")
        attT_ps = sem("attT_ps")
        attT_sb = sem("attT_sb")
        o0_ps = sem("o0_ps")
        norm_in = sem("norm_in")
        centred = sem("centred")
        squared = sem("squared")
        variance = sem("variance")
        rstd_sb = sem("rstd_sb")
        bn_sb = sem("bn_sb")
        rs4_sb = sem("rs4_sb")
        normed = sem("normed")

        w1_dve = sem("w1_dve")

        wdt_ps = sem("wdt_ps")
        x1_sb = sem("x1_sb")
        x2_ps = sem("x2_ps")
        x12 = sem("x12")
        xz_ps = sem("xz_ps")
        xi_used = sem("xi_used")
        z_used = sem("z_used")
        conv0 = sem("conv0")
        conv_done = sem("conv_done")
        u_sb = sem("u_sb")
        dt_ps = sem("dt_ps")

        dt_parts = sem("dt_parts")
        dt_log = sem("dt_log")
        dt_sb = sem("dt_sb")
        dtu_sb = sem("dtu_sb")
        w_rows_sb = sem("w_rows_sb")
        skip_sb = sem("skip_sb")
        compact_ps = sem("compact_ps")
        round_1 = sem("round_1")
        rest_1 = sem("rest_1")
        round_2 = sem("round_2")
        parts_sb = sem("parts_sb")
        b_ps = sem("b_ps")
        b_copied = sem("b_copied")
        c_ps = sem("c_ps")
        y_ps = sem("y_ps")
        dA_zero = sem("dA_zero")

        dA_sb = sem("dA_sb")
        dbu_done = sem("dbu_done")
        scan_done = sem("scan_done")
        hc_done = sem("hc_done")


        gated = sem("gated")
        mo_ps = sem("mo_ps")
        wp_ps = sem("wp_ps")
        x_new = sem("x_new")
        stored = sem("stored")

        block = ctx.enter_context(nc.Block())

        def load_w0():
            for g in range(G):
                r = slice(C * g, C * g + C)
                yield nat0[C * g:C * g + 4, 0, r], a["L0_conv_w_theta"]
                yield nat0[C * g:C * g + 4, 1, r], a["L0_conv_w_phi"]
                yield nat0[C * g:C * g + 16, 2, r], a["L0_conv_w_g"]
                yield nat0[r, 3, r], a["L1_conv_W_p"]
                yield wo_nat[r, C * g:C * g + 16], a["L0_conv_w_o"]
            yield gamma0[:, :], broadcast_rows(a["L0_conv_gamma"], P)

        def load_w1():
            col = lambda v: v.rearrange("(c o) -> c o", o=1)
            for g in range(G):
                r = slice(C * g, C * g + C)
                yield ln_g[r, :], col(a["L1_conv_gamma"])
                yield ln_b[r, :], col(a["L1_conv_beta"])
                yield b_p[r, :], col(a["L1_conv_b_p"])
                yield win_nat[r, :, :], a["L1_conv_W_in"].rearrange("(r e) c -> e r c", e=C)
                k = g % 2
                yield wout_nat[r, :], a["L1_conv_W_out"][:, C * k:C * k + C]
            yield s1[:, :], broadcast_rows(a["L1_conv_s1"], P)
            yield s2[:, :], broadcast_rows(a["L1_conv_s2"], P)
            for v in range(2):
                r = slice(64 * v, 64 * v + 64)
                yield conv_w[r, :], a["L1_conv_conv_w"].rearrange("d o k -> d (o k)")
                yield conv_b[r, :], col(a["L1_conv_conv_b"])
                yield b_dt[r, :], col(a["L1_conv_b_dt"])
                yield d_skip[r, :], col(a["L1_conv_D_skip"])
                yield a_log[r, :], a["L1_conv_A_log"]
                yield wx_t[r, :], a["L1_conv_W_x"].rearrange("n d -> d n")
                yield wx_rows[:, v, :], a["L1_conv_W_x"][0:2, :]
                yield wdt_t[:, v, :], a["L1_conv_W_dt"].rearrange("d r -> r d")

        def load_w2():
            col = lambda v: v.rearrange("(c o) -> c o", o=1)
            for dst, name in ((wq2, "Wq"), (wk2, "Wk"), (wv2, "Wv")):
                yield dst[:, :, :], a["L2_attn_" + name].rearrange("(h e) c -> e h c", e=C)
            yield wu_nat[:, :], a["L2_attn_Wu"]
            for g in range(G):
                r = slice(C * g, C * g + C)
                yield b_u[r, :], col(a["L2_attn_bu"])
                yield r_bd[r, g, :], a["L2_ffn_router_w"]
                yield rb_row[0:1, g, :], a["L2_ffn_router_b"].rearrange("(o e) -> o e", o=1)

        def load_experts():
            for g in range(G):
                yield e_bd[C * g:C * g + C, g, :].rearrange("p (e c) -> p e c", e=E2), \
                    a["L2_ffn_expert_w"].rearrange("e d c -> d e c")
                yield eb_bd[E2 * g:E2 * g + E2, C * g:C * g + C], a["L2_ffn_expert_b"]

        n_ex = 16 * len(list(load_experts()))

        def load_w3():
            col = lambda v: v.rearrange("(c o) -> c o", o=1)
            qkv, qkv_b = a["L3_attn_qkv_w"], a["L3_attn_qkv_b"]
            hd = C // H3
            for g in range(G):
                r = slice(C * g, C * g + C)
                yield w_q3[r, r], qkv[:, 0:C]
                yield w_k3[r, r], qkv[:, C:2 * C]
                yield w_p3[r, r], a["L3_attn_proj_w"]
                yield b_q3[r, :], col(qkv_b)[0:C, :]
                yield b_k3[r, :], col(qkv_b)[C:2 * C, :]
                yield b_p3[r, :], col(a["L3_attn_proj_b"])
                for h in range(H3):
                    c = slice(2 * C + hd * h, 2 * C + hd * h + hd)
                    yield w_v3[r, h, hd * h:hd * h + hd], qkv[:, c]
                h, c = g, slice(2 * C + hd * g, 2 * C + hd * g + hd)
                yield b_v3[C * h + hd * h:C * h + hd * h + hd, :], col(qkv_b)[c, :]
                yield gate_w3[r, :], broadcast_rows(a["L3_attn_gate_w"][h, :], C)
                yield gate_b3[r, :], broadcast_rows(a["L3_attn_gate_b"][h:h + 1], C)

        n_w3 = 16 * len(list(load_w3()))
        n_w2 = 16 * len(list(load_w2()))
        n_w0 = 16 * len(list(load_w0()))
        n_w1 = 16 * len(list(load_w1()))

        def step_weights(at, names, vectors):
            for dst, name in names:
                src = a["L3_ffn_" + name].rearrange("b o x y -> (b o) x y")[bass.ds(at, 1), :, :] \
                    .rearrange("o x y -> (o x) y")
                yield dst, src if src.shape[0] == P else broadcast_rows(src, G)
            for dst, name in vectors:
                src = a["L3_ffn_" + name].rearrange("b o x -> (b o) x")[bass.ds(at, 1), :] \
                    .rearrange("o x -> x o")
                yield dst, src if src.shape[0] == P else broadcast_rows(src, G)

        def load_attention_step(at):
            return step_weights(at, [(w4[:, k, :], name) for k, name in enumerate(("wq", "wk", "wv", "wo"))], [])

        def load_feeding_step(at):
            return step_weights(at, [(w1_4, "ffn_w1"), (w2_4, "ffn_w2")], [(b1_4, "ffn_b1"), (b2_4, "ffn_b2")])

        N_STEP = 16 * 4
        ATTN_PE = 3 + 3 * B
        ATTN_ACT = 3 + B
        ATTN_DVE = 2 + 3 * B
        FFN_PE = G + 1

        def hold(eng, s_, value):
            eng.wait_ge(s_, value)
            eng.sem_inc(loop_passed, 1)

        def chained(eng, chain):
            count = [0]

            def link(ins):
                count[0] += 1
                ins.then_inc(chain, 1)
                eng.wait_ge(chain, count[0])
            return link

        def weigh_planes(eng, k, q):
            r = slice(CHUNK * q, CHUNK * (q + 1))
            return eng.tensor_tensor(plane_hot[k],
                                     col_hot[:, r, :].unsqueeze(2).to_broadcast([P, CHUNK, PLANES, C]),
                                     weighed[:, r, :].unsqueeze(3).to_broadcast([P, CHUNK, PLANES, C]),
                                     ALU.mult)

        SPLIT = (1, 8)
        ROUND_1, REST_1, ROUND_2, REST_2 = 3, 2, 6, 5

        @block.sync
        def _(sp):
            sp.dma_start(X[:, :].rearrange("p (j n) -> p j n", j=J),
                         a["x"].rearrange("(j g) c h w -> (g c) j (h w)", g=G)).then_inc(dma_x, 16)
            def load_edges(first, end):
                for c in range(first, end):
                    if c >= 2:
                        sp.wait_ge(e_used, 2 * (c - 1))
                    for k, dst in ((0, e_row), (1, e_col)):
                        src = a["L3_attn_edge_index"][k, :].rearrange("(p f) -> p f", p=P)
                        sp.dma_start(dst[:, c % 2, :], src[:, c * EC:(c + 1) * EC]).then_inc(dma_e[c % 2], 16)

            load_edges(0, 2)
            sp.wait_ge(zeroed, 2)
            for dst, src in load_w0():
                sp.dma_start(dst, src).then_inc(dma_w0, 16)
            with nc.allow_non_contiguous_dma("small transposed weights"):
                for dst, src in load_w1():
                    sp.dma_start(dst, src).then_inc(dma_w1, 16)
            load_edges(2, NCH)
            sp.wait_ge(w2_zero, 1)
            with nc.allow_non_contiguous_dma("small biases"):
                for dst, src in load_w2():
                    sp.dma_start(dst, src).then_inc(dma_w2, 16)
            sp.wait_ge(w3_zero, 1)
            with nc.allow_non_contiguous_dma("small biases and column slices"):
                for dst, src in load_w3():
                    sp.dma_start(dst, src).then_inc(dma_w3, 16)
            sp.wait_ge(ex_zero, 1)
            for dst, src in load_experts():
                sp.dma_start(dst, src).then_inc(dma_ex, 16)
            for k, name in enumerate(("attn_mask", "ffn_mask")):
                sp.dma_start(steps_u8[:, k * STEPS:(k + 1) * STEPS],
                             a["L3_ffn_" + name].rearrange("(o b) n -> o (b n)", o=1)).then_inc(dma_m, 16)
            active = sp.alloc_register("sp_active")
            hold(sp, ctrl_ready, 1)
            sp.reg_load(active, ctrl[0:1, 0:1])
            with sp.Fori(0, ROUNDS) as outer:
                with sp.If_ne(active, 0):
                    with sp.Fori(0, ROUNDS) as inner:
                        i = outer * ROUNDS + inner
                        with sp.If_ne(active, 0):
                            attends = sp.value_load(ctrl[0:1, 1:2], min_val=0, max_val=1)
                            feeds = sp.value_load(ctrl[0:1, 2:3], min_val=0, max_val=1)
                            at = sp.value_load(ctrl[0:1, 3:4], min_val=0, max_val=STEPS - 1)
                            with nc.allow_non_contiguous_dma("small biases"):
                                with sp.If(attends > 0):
                                    for dst, src in load_attention_step(at):
                                        sp.dma_start(dst, src).then_inc(dma_fa, 16)
                                with sp.Else():
                                    sp.sem_inc(dma_fa, N_STEP)
                                with sp.If(feeds > 0):
                                    for dst, src in load_feeding_step(at):
                                        sp.dma_start(dst, src).then_inc(dma_f, 16)
                                with sp.Else():
                                    sp.sem_inc(dma_f, N_STEP)
                            hold(sp, ctrl_ready, i + 2)
                            sp.reg_load(active, ctrl[0:1, 0:1])
            sp.wait_ge(x_new, 6)
            sp.dma_start(out.rearrange("(j g) c h w -> (g c) j (h w)", g=G),
                         X[:, :].rearrange("p (j n) -> p j n", j=J)).then_inc(stored, 16)
            sp.wait_ge(stored, 16)

        @block.gpsimd
        def _(pool):
            link = chained(pool, pool_chain)
            nc.gpsimd.memset(nat0[:, :, :], 0.0).then_inc(zeroed, 1)
            nc.gpsimd.memset(wo_nat[:, :], 0.0).then_inc(zeroed, 1)
            nc.gpsimd.iota(seg_place[:, :], pattern=[[8192, SEG]], base=1, channel_multiplier=0,
                           allow_small_or_imprecise_dtypes=True).then_inc(place_sb, 1)
            link(nc.gpsimd.memset(ident[:, :], 0.0))
            link(nc.gpsimd.affine_select(out=ident[:, :], in_=ident[:, :], compare_op=ALU.not_equal,
                                         fill=1.0, base=0, pattern=[[-1, P]], channel_multiplier=1))
            link(nc.gpsimd.memset(averager[:, :], 0.0))
            for g in range(G):
                link(nc.gpsimd.memset(averager[C * g:C * g + C, C * g:C * g + C], 1.0 / C))
            link(nc.gpsimd.memset(eps5[:, :], 1e-5))
            link(nc.gpsimd.iota(ops_at[:, :], pattern=[[1, NB]], base=0, channel_multiplier=0,
                                allow_small_or_imprecise_dtypes=True))
            link(nc.gpsimd.iota(ops_back[:, :], pattern=[[-1, NB]], base=NONE, channel_multiplier=0,
                                allow_small_or_imprecise_dtypes=True))
            link(nc.gpsimd.memset(from_block[:, :], 0.0))
            link(nc.gpsimd.iota(seg_bits, pattern=[[256, SEG // 8], [0, 8]], base=1 << 30,
                                channel_multiplier=0))
            link(nc.gpsimd.iota(rows_at[:, :], pattern=[[1, N]], base=0, channel_multiplier=0,
                                allow_small_or_imprecise_dtypes=True))
            ones = sum(1 << SYMBOL * k for k in range(PLANES - 1))
            for k, width in ((0, EF), (1, GW)):
                for g in range(G):
                    nc.gpsimd.memset(g_base[:, k, g:g + 1], float(C * width * g + 1 - ones))
            for g in range(G):
                r = slice(C * g, C * g + C)
                link(nc.gpsimd.iota(weight[r, :], pattern=[[0, 1]], base=127 + 2 - 16 * SPACE,
                                    channel_multiplier=SPACE))
                for k, width in ((0, EF), (1, GW)):
                    link(nc.gpsimd.iota(p_base[r, k:k + 1], pattern=[[0, 1]], base=0,
                                        channel_multiplier=width))
            link(nc.gpsimd.memset(one_col[:, :], 1.0))
            link(nc.gpsimd.memset(one_row[:, :], 1.0))
            link(nc.gpsimd.tensor_tensor(centerer[:, :], ident[:, :], averager[:, :], ALU.subtract))
            for g in range(G):
                nc.gpsimd.tensor_copy(
                    permuter[:, C * g:C * g + C].rearrange("p (k i) -> p k i", i=8),
                    ident[:, C * g:C * g + C].rearrange("p (i k) -> p k i", k=4))
            nc.gpsimd.memset(half_mask[:, :], 0.0).then_inc(consts, 1)
            pool.wait_ge(consts, 1)
            for v in range(2):
                link(nc.gpsimd.memset(half_mask[64 * v:64 * v + 64, 64 * v:64 * v + 64], 1.0))
            link(nc.gpsimd.memset(diag[:, :], 0.0))
            for h in range(G):
                r = slice(C * h, C * h + C)
                link(nc.gpsimd.affine_select(out=diag[r, :], in_=diag[r, :], compare_op=ALU.not_equal,
                                             fill=1.0, base=0, pattern=[[-1, C]], channel_multiplier=1))
            nc.gpsimd.memset(zero_bf[:, :], 0.0).then_inc(consts, 1)
            pool.wait_ge(consts, 2)
            pool.wait_ge(dma_w1, n_w1)
            for k in range(2):
                for part in range(PARTS):
                    for v in range(2):
                        last = nc.gpsimd.tensor_scalar(
                            w_rows[:, k, part, v, :], wx_t[:, 2 + k * S:2 + (k + 1) * S],
                            half_mask[:, 64 * v:64 * v + 1], None, ALU.mult)
            link(last)
            link(nc.gpsimd.memset(less_1[:, :], -1.0))
            link(nc.gpsimd.memset(less_1[0:C, :], 0.0))
            link(nc.gpsimd.memset(less_2[:, :], 0.0))
            link(nc.gpsimd.memset(less_2[2 * C:3 * C, :], -1.0))
            nc.gpsimd.tensor_copy(pick_state[:, :, :, :],
                                  diag[0:BC, :].rearrange("p (v n) -> p n v", v=2).unsqueeze(3)
                                  .to_broadcast([BC, S, 2, 64])).then_inc(w_rows_sb, 1)

            for t in (w_km, r_bd):
                link(nc.gpsimd.memset(t[:, :, :], 0.0))
            nc.gpsimd.tensor_copy(ident_bf[:, :], ident[:, :]).then_inc(w2_zero, 1)
            link(nc.gpsimd.memset(win_mask[:, :], 0.0))
            for h in range(G):
                r = slice(C * h, C * h + C)
                link(nc.gpsimd.affine_select(out=win_mask[r, 0:C], in_=win_mask[r, 0:C], compare_op=ALU.is_gt,
                                             fill=-1e30, base=0, pattern=[[-1, C]], channel_multiplier=1))
                link(nc.gpsimd.affine_select(out=win_mask[r, C:2 * C], in_=win_mask[r, C:2 * C],
                                             compare_op=ALU.is_ge, fill=-1e30, base=0, pattern=[[1, C]],
                                             channel_multiplier=-1))
            pool.wait_ge(bd0_ready, 1)
            for t in (w_q3, w_k3, w_p3):
                link(nc.gpsimd.memset(t[:, :], 0.0))
            link(nc.gpsimd.memset(w_v3, 0.0))
            link(nc.gpsimd.memset(head_scale[:, :], float(C // H3) ** -0.5))
            for g in range(G):
                r = slice(C * g, C * g + C)
                link(nc.gpsimd.affine_select(out=head_scale[r, :], in_=head_scale[r, :],
                                             compare_op=ALU.is_ge, fill=0.0, base=0,
                                             pattern=[[-8, H3]], channel_multiplier=1))
                link(nc.gpsimd.affine_select(out=head_scale[r, :], in_=head_scale[r, :],
                                             compare_op=ALU.is_ge, fill=0.0, base=7,
                                             pattern=[[8, H3]], channel_multiplier=-1))
            nc.gpsimd.memset(b_v3[:, :], 0.0).then_inc(w3_zero, 1)
            pool.wait_ge(w3_zero, 1)
            for i in range(WT):
                nc.gpsimd.tensor_copy(mask_bf[:, i, :], win_mask[:, :])
            nc.gpsimd.iota(rank[:, :], pattern=[[-1, E2]], base=E2, channel_multiplier=0,
                           allow_small_or_imprecise_dtypes=True).then_inc(w2_mask, 1)

            pool.wait_ge(cols_sb, 1)
            for q in range(SLOTS // CHUNK):
                if q >= 2:
                    pool.wait_ge(hot_used, q - 1)
                weigh_planes(nc.gpsimd, q % 2, q).then_inc(hot_sb, 1)

            def gather(i, done=gathered):
                nc.gpsimd.indirect_dma_start(
                    out=hit[:, i // C, 0, i % C:i % C + 1], out_offset=None,
                    in_=a["L3_attn_edge_values"].rearrange("(e o) -> e o", o=1),
                    in_offset=bass.IndirectOffsetOnAxis(ap=tab_i[:, i:i + 1], axis=0)).then_inc(done, 16)

            for i in range(J * S):
                j, n = i // S, i % S
                if n == 0:
                    pool.wait_ge(dtu_sb, j + 1)
                pool.wait_ge(b_copied, i + 1)
                if i >= 2:
                    pool.wait_ge(scan_done, i - 1)
                nc.gpsimd.tensor_tensor(dBu[:, i % 2, :], dtu[:, j * NT:(j + 1) * NT], b_sb[:, i % 2, :],
                                        ALU.mult).then_inc(dbu_done, 1)
                if i == 1:
                    pool.wait_ge(tab_dve, 1)
                if i % 4 == 1:
                    gather(i // 4)
            for i in range(UNDER_SCAN, EARLY):
                gather(i)

            pool.wait_ge(x_new, 2)
            nc.gpsimd.memset(alone, 0.0).then_inc(alone_zero, 1)
            nc.gpsimd.memset(eb_bd, 0.0)
            nc.gpsimd.memset(e_bd, 0.0).then_inc(ex_zero, 1)

            pool.wait_ge(over_sb, 1)
            more = pool.value_load(over_i[0:1, 0:1], min_val=0, max_val=P)
            with pool.If(more > 0):
                pool.wait_ge(gathered, 16 * EARLY)
                with pool.Fori(0, EDGES // (P * GW)) as t:
                    for k, dst in ((0, g_row), (1, g_col)):
                        src = a["L3_attn_edge_index"][k, :].rearrange("(t p f) -> t p f", p=P, f=GW)
                        nc.gpsimd.dma_start(dst, src[bass.ds(t, 1), :, :].rearrange(
                            "o p f -> (o p) f")).then_inc(gen_in, 16)
                    pool.wait_ge(gen_done, t + 1)
                    pool.sem_inc(gen_passed, 1)
                pool.wait_ge(tab_dve, 2)
                for i in range(EARLY):
                    gather(i, gathered_again)
                pool.wait_ge(gathered_again, 16 * EARLY)
            for u in range(16):
                for i in range(EARLY + 2 * u, EARLY + 2 * u + 2):
                    gather(i)
                pool.wait_ge(s2_scale, u + 1)
                nc.gpsimd.tensor_tensor(
                    s2_buf[u % 2].rearrange("p (s k) -> p s k", k=2 * C),
                    s2_buf[u % 2].rearrange("p (s k) -> p s k", k=2 * C),
                    sm2[:, u % 2, :].unsqueeze(2).to_broadcast([P, 16, 2 * C]), ALU.mult).then_inc(s2_prob, 1)
            pool.wait_ge(gathered, 16 * 2 * C)
            nc.gpsimd.tensor_tensor(hit[:, :, 0, :], hit[:, :, 0, :], hit[:, :, 1, :],
                                    ALU.mult).then_inc(hit_sb, 1)
            pool.wait_ge(hit_sb, 1)
            for k in range(2):
                nc.gpsimd.dma_start(bias_dram[k, :].rearrange("(s p c) -> p s c", s=2, c=C),
                                    hit[:, :, k, :]).then_inc(bias_out, 16)
            pool.wait_ge(bias_out, 32)
            for h in range(H3):
                for k, dst in ((0, wgt), (1, msk)):
                    nc.gpsimd.dma_start(dst[C * h:C * h + C, :, 0:C],
                                        bias_dram[k, :].rearrange("(b q c) -> q b c", b=BL, c=C)
                                        ).then_inc(bias_in, 16)

            pool.wait_ge(x_new, 3)
            nc.gpsimd.memset(k3, 0.0).then_inc(k3_zero, 1)

        @block.scalar
        def _(act):
            act.wait_ge(proj0, 1)
            nc.scalar.activation(theta, bank(0, 2), ACT.Copy).then_inc(theta_sb, 1)
            act.wait_ge(vb_ps, 1)
            nc.scalar.activation(vb, bank(0, 2), ACT.Copy).then_inc(vb_sb, 1)
            act.wait_ge(shifted0, 1)
            nc.scalar.activation(att, att, ACT.Exp).then_inc(exp0, 1)
            act.wait_ge(attT_ps, 1)
            nc.scalar.activation(att_t, bank(0, 4), ACT.Copy).then_inc(attT_sb, 1)

            n_act = [0]

            def link(ins):
                n_act[0] += 1
                ins.then_inc(act_chain, 1)
                act.wait_ge(act_chain, n_act[0])

            def inverse_root(dst, src, eps):
                link(nc.scalar.activation(dst, src, ACT.Ln, bias=eps[:, :]))
                return nc.scalar.activation(dst, dst, ACT.Exp, scale=-0.5)

            def norm_steps(k, eps):
                act.wait_ge(centred, k)
                nc.scalar.activation(sq[:, :], bank(0, 2), ACT.Square).then_inc(squared, 1)
                act.wait_ge(variance, k)
                inverse_root(rstd[:, :], bank(2, 2), eps).then_inc(rstd_sb, 1)

            act.wait_ge(consts, 2)
            act.wait_ge(bn_sb, 1)
            inverse_root(rs4[:, :], bn2[:, :, 1], eps5).then_inc(rs4_sb, 1)

            act.wait_ge(dma_w1, n_w1)
            link(nc.scalar.activation(a_neg[:, :], a_log[:, :], ACT.Exp))
            link(nc.scalar.mul(a_neg[:, :], a_neg[:, :], -1.0))
            norm_steps(1, eps5)
            for i in range(8):
                g, jp = i // 2, i % 2
                act.wait_ge(xz_ps, 2 * i + 1)
                k = 4 * (i % 2)
                dst = xi_pad[:, g + 8 * jp:g + 8 * jp + 5:4, 3:259]
                nc.scalar.activation(dst, bank(k).rearrange("p (j n) -> p j n", n=N),
                                     ACT.Copy).then_inc(xi_used, 1)
                act.wait_ge(xz_ps, 2 * i + 2)
                nc.scalar.activation(z_act.rearrange("p (b n) -> p b n", n=N)
                                     [:, g + 8 * jp:g + 8 * jp + 5:4, :],
                                     bank(k + 1).rearrange("p (j n) -> p j n", n=N),
                                     ACT.Silu).then_inc(z_used, 1)
            act.wait_ge(conv0, 1)
            act.wait_ge(xi_used, 8)
            nc.scalar.activation(u_act.rearrange("p (b t) -> p b t", b=B), xi_pad[:, :, 0:N],
                                 ACT.Identity, bias=conv_b[:, :],
                                 scale=conv_w[:, 0:1]).then_inc(conv0, 1)
            for j in range(J):
                act.wait_ge(conv_done, j + 1)
                r = slice(j * NT, (j + 1) * NT)
                nc.scalar.activation(u_act[:, r], u_act[:, r], ACT.Silu).then_inc(u_sb, 1)
            def round_part(c, src, done):
                nc.scalar.activation(rounded[c % 2], src, ACT.Copy).then_inc(done, 1)

            for k in range(2):
                act.wait_ge(compact_ps, k + 1)
                round_part(k, ps[0:BC, 2 * k:2 * k + 2, :].rearrange("p a b -> p (a b)"), round_1)
            for k in range(2):
                act.wait_ge(rest_1, k + 1)
                round_part(k, rest[k], round_2)
            for j in range(J):
                r = slice(j * NT, (j + 1) * NT)
                act.wait_ge(dt_ps, j + 1)
                pre = bank(2 * (j % 2), 2)
                nc.scalar.activation(dt_act[:, r], pre, ACT.Abs, bias=b_dt[:, :])
                nc.scalar.activation(dtu[:, r], pre, ACT.Relu, bias=b_dt[:, :]).then_inc(dt_parts, 1)
            act.wait_ge(dt_parts, J)
            link(nc.scalar.activation(dt_act, dt_act, ACT.Exp, scale=-1.0))
            for j in range(J):
                r = slice(j * NT, (j + 1) * NT)
                nc.scalar.activation(dt_act[:, r], dt_act[:, r], ACT.Ln, bias=1.0).then_inc(dt_log, 1)
            for i in range(J * S):
                j, n = i // S, i % S
                act.wait_ge(b_ps, i + 1)
                if i >= 2:
                    act.wait_ge(dbu_done, i - 1)
                nc.scalar.activation(b_sb[:, i % 2, :], bank(0, 2), ACT.Copy).then_inc(b_copied, 1)
                if i >= 2:
                    act.wait_ge(scan_done, i - 1)
                if i == 0:
                    act.wait_ge(dA_zero, 1)
                if n == 0:
                    act.wait_ge(dt_sb, j + 1)
                src = dt_act[:, j * NT:(j + 1) * NT].rearrange("p (b t) -> p b t", t=N)
                dst = dA[:, i % 2, :].rearrange("p (b t) -> p b t", t=N)
                nc.scalar.activation(dst[:, :, 1:], src[:, :, 1:], ACT.Exp,
                                     scale=a_neg[:, n:n + 1]).then_inc(dA_sb, 1)
                for k in range(2):
                    c = 2 * (j + 1) + k
                    if j < J - 1 and n == SPLIT[k] + ROUND_1:
                        act.wait_ge(compact_ps, c + 1)
                        act.wait_ge(parts_sb, c - 1)
                        round_part(c, ps[0:BC, 4:6, :].rearrange("p a b -> p (a b)"), round_1)
                    if j < J - 1 and n == SPLIT[k] + ROUND_2:
                        act.wait_ge(rest_1, c + 1)
                        round_part(c, rest[k], round_2)
            norm_steps(2, eps5)

            act.wait_ge(w2_ps, 1)
            act.wait_ge(w2_zero, 1)
            for g in range(G):
                r = slice(C * g, C * g + C)
                nc.scalar.activation(w_km[r, :, r], bank(6)[r, 0:H2 * C].rearrange("p (h c) -> p h c", c=C),
                                     ACT.Copy, scale=float(C) ** -0.5)
            nc.scalar.activation(w_vu[:, :], bank(7)[:, 0:H2 * C], ACT.Copy).then_inc(w2_sb, 1)
            norm_steps(3, eps5)
            act.wait_ge(normed, 2)
            act.wait_ge(alone_zero, 1)
            for g in range(2):
                r = slice(C * g, C * g + C)
                nc.scalar.activation(alone[r, g, :], xn[r, :], ACT.Copy).then_inc(alone_sb, 1)
            for h in range(H2):
                act.wait_ge(km_ps, h + 1)
                nc.scalar.activation(km[:, :, h, :], bank(2 * (h % 4), 2).rearrange("p (t k) -> p t k", k=C),
                                     ACT.Copy).then_inc(km_sb, 1)
            for u in range(16):
                act.wait_ge(s2_shifted, u + 1)
                nc.scalar.activation(s2_buf[u % 2], s2_buf[u % 2], ACT.Exp).then_inc(s2_exp, 1)
            norm_steps(4, eps5)
            act.wait_ge(lg_shifted, 1)
            nc.scalar.activation(gate[:, :, :], gate[:, :, :], ACT.Exp).then_inc(lg_exp, 1)
            act.wait_ge(gate_ps, 1)
            nc.scalar.activation(gate_t, bank(0, 2)[0:G * E2, :], ACT.Copy).then_inc(gate_copied, 1)

            norm_steps(5, eps5)
            act.wait_ge(dma_w3, n_w3)
            link(nc.scalar.activation(b_qh[:, :], head_scale[:, :], ACT.Copy, scale=b_q3[:, :]))
            act.wait_ge(qkv3_ps, 1)
            for h in range(H3):
                last = nc.scalar.activation(q3[:, :, h, :], bank(4, 2).rearrange("p (s q) -> p s q", q=C),
                                            ACT.Identity, bias=b_qh[:, h:h + 1],
                                            scale=head_scale[:, h:h + 1])
            last.then_inc(q3_sb, 1)
            for jp in range(2):
                act.wait_ge(v3_ps, jp + 1)
                nc.scalar.activation(v3[jp].rearrange("p (g n) -> p g n", g=G),
                                     bank(4 * jp, 4).rearrange("p (g n) -> p g n", g=G),
                                     ACT.Identity, bias=b_v3[:, :]).then_inc(v3_sb, 1)
            for jp in range(2):
                for j in (2 * jp, 2 * jp + 1):
                    act.wait_ge(s3_shift, j + 1)
                    nc.scalar.activation(s3[j % 2], s3[j % 2], ACT.Exp).then_inc(s3_exp, 1)
                for j in (2 * jp, 2 * jp + 1):
                    act.wait_ge(o3_ps, j + 1)
                    nc.scalar.activation(o3[:, j * N:(j + 1) * N], bank(4 * (j % 2))[:, 0:N],
                                         ACT.Copy).then_inc(o3_sb, 1)

            norm_steps(6, eps5)
            active = act.alloc_register("act_active")
            hold(act, ctrl_ready, 1)
            act.reg_load(active, ctrl[0:1, 0:1])
            with act.Fori(0, ROUNDS) as outer:
                with act.If_ne(active, 0):
                    with act.Fori(0, ROUNDS) as inner:
                        i = outer * ROUNDS + inner
                        with act.If_ne(active, 0):
                            attends = act.value_load(ctrl[0:1, 1:2], min_val=0, max_val=1)
                            feeds = act.value_load(ctrl[0:1, 2:3], min_val=0, max_val=1)
                            with act.If(attends > 0):
                                hold(act, attn_pe, ATTN_PE * i + 1)
                                nc.scalar.activation(q4, bank(0, 2), ACT.Copy).then_inc(attn_act, 1)
                                hold(act, attn_pe, ATTN_PE * i + 2)
                                nc.scalar.activation(v4.rearrange("p (g t) -> p g t", g=G), ps[:, 4:8, 0:N],
                                                     ACT.Copy).then_inc(attn_act, 1)
                                for b in range(B):
                                    hold(act, attn_dve, ATTN_DVE * i + 2 + 3 * b)
                                    for h in range(2):
                                        last = nc.scalar.activation(p4[:, h * N:(h + 1) * N],
                                                                    bank(0)[:, h * N:(h + 1) * N], ACT.Exp,
                                                                    bias=nm4[:, h:h + 1], scale=float(C) ** -0.5,
                                                                    accum_out=sm4[:, h:h + 1])
                                    last.then_inc(attn_act, 1)
                                hold(act, attn_pe, ATTN_PE * i + 2 + 3 * B)
                                nc.scalar.activation(y4, bank(2, 2), ACT.Copy).then_inc(attn_act, 1)
                            with act.Else():
                                act.sem_inc(attn_act, ATTN_ACT)
                            with act.If(feeds > 0):
                                hold(act, dma_f, N_STEP * i + N_STEP)
                                for g in range(G):
                                    hold(act, ffn_pe, FFN_PE * i + g + 1)
                                    nc.scalar.activation(hid[:, g * NT:(g + 1) * NT], bank(2 * g, 2), ACT.Relu,
                                                         bias=b1_4).then_inc(ffn_act, 1)
                            with act.Else():
                                act.sem_inc(ffn_act, G)
                            hold(act, ctrl_ready, i + 2)
                            act.reg_load(active, ctrl[0:1, 0:1])

        @block.vector
        def _(dve):
            link = chained(dve, dve_chain)
            V = nc.vector

            EH = HALF

            def edges(first, end):
                for piece in range(first, end):
                    c, part = piece // (EC // EH), piece % (EC // EH)
                    if part == 0:
                        dve.wait_ge(dma_e[c % 2], 32 * (c // 2 + 1))
                    at = slice(part * EH, (part + 1) * EH)
                    r_, c_ = e_row[:, c % 2, at], e_col[:, c % 2, at]
                    x_, u_, key = e_x[:, at], e_u[:, at], e_key[:, at]
                    link(V.tensor_tensor(x_, r_, c_, ALU.bitwise_xor))
                    V.scalar_tensor_tensor(u_, x_, 8.0, r_, ALU.mult, ALU.max)
                    V.scalar_tensor_tensor(key, r_, float(C), x_, ALU.mult, ALU.add).then_inc(e_used, 1)
                    dve.wait_ge(e_used, piece + 1)
                    if piece == 0:
                        dve.wait_ge(place_sb, 1)
                    per = lambda t: t.rearrange("p (s f) -> p s f", f=SEG)
                    link(V.tensor_tensor(per(key), per(key),
                                         seg_place[:, :].unsqueeze(1).to_broadcast([P, EH // SEG, SEG]), ALU.add))
                    link(V.scalar_tensor_tensor(key, u_, float(N), key, ALU.is_lt, ALU.mult))
                    for q in range(EH // SEG):
                        to = 8 * (piece * (EH // SEG) + q)
                        last = V.max(cand[:, to:to + 8], key[:, q * SEG:(q + 1) * SEG])
                    link(last)

            edges(0, 2)
            dve.wait_ge(dma_w0, n_w0)
            link(V.memset(phi_bd, 0.0))
            link(V.memset(gp_bd, 0.0))
            V.transpose(bd0[:, :, :].rearrange("p a b -> p (a b)"),
                        nat0[:, :, :].rearrange("p a b -> p (a b)"))
            V.transpose(wo_bd[:, :], wo_nat[:, :]).then_inc(bd0_ready, 1)
            for k, dst in ((1, phi_bd), (2, gp_bd)):
                dve.wait_ge(proj0, k + 1)
                link(V.tensor_reduce(pool_w[:, 0:NT // 2],
                                     bank(2 * k, 2).rearrange("p (m b) -> p m b", b=2), AX_X, ALU.max))
                src = pool_w[:, 0:NT // 2].rearrange("p (m a w) -> p m w a", a=2, w=8)
                for g in range(G):
                    r = slice(C * g, C * g + C)
                    last = V.tensor_reduce(
                        dst[r, :, g, :].rearrange("p j (h w) -> p j h w", w=8),
                        pool_w[r, 0:NT // 2].rearrange("p (j h a w) -> p j h w a", j=J, a=2, w=8),
                        AX_X, ALU.max)
                last.then_inc(pooled, 1)
                dve.wait_ge(pooled, k)
            seg = lambda t: t.rearrange("p (s m) -> p s m", m=64)
            wide = lambda t: t[:, :].unsqueeze(2).to_broadcast([P, 32, 64])
            edges(2, 3)
            dve.wait_ge(logits0, 1)
            link(V.tensor_reduce(mx0[:, :], seg(bank(4, 4)), AX_X, ALU.max))
            V.tensor_tensor(seg(att), seg(bank(4, 4)), wide(mx0), ALU.subtract).then_inc(shifted0, 1)
            dve.wait_ge(exp0, 1)
            link(V.tensor_reduce(sm0[:, :], seg(att), AX_X, ALU.add))
            link(V.reciprocal(rs0[:, :], sm0[:, :]))
            V.tensor_tensor(seg(att), seg(att), wide(rs0), ALU.mult).then_inc(prob0, 1)
            edges(3, 5)
            dve.wait_ge(o0_ps, 1)
            dve.wait_ge(dma_x, 16)
            V.scalar_tensor_tensor(X[:, :], bank(4, 2), gamma0[:, :], X[:, :], ALU.mult,
                                   ALU.add).then_inc(x_new, 1)
            dve.wait_ge(x_new, 1)

            for j in range(J):
                last = V.bn_stats(bn6[:, j, :], X[:, j * N:(j + 1) * N])
            link(last)
            for j in range(J):
                last = V.bn_aggr(bn2[:, j, :], bn6[:, j, :])
            last.then_inc(bn_sb, 1)
            dve.wait_ge(rs4_sb, 1)
            for j in range(J):
                last = V.tensor_scalar(xn[:, j * N:(j + 1) * N], X[:, j * N:(j + 1) * N],
                                       bn2[:, j, 0:1], rs4[:, j:j + 1], ALU.subtract, ALU.mult)
            last.then_inc(norm_in, 1)

            def finish_norm(k, dst):
                dve.wait_ge(rstd_sb, k)
                link(V.tensor_tensor(dst, bank(0, 2), rstd[:, :], ALU.mult))

            dve.wait_ge(dma_w1, n_w1)
            V.transpose(win_t[:, :], win_nat[:, :, :].rearrange("p a b -> p (a b)"))
            V.transpose(wout_t[:, :], wout_nat[:, :])
            V.memset(xi_pad[:, :, 0:3], 0.0).then_inc(conv0, 1)
            dve.wait_ge(wdt_ps, 1)
            V.tensor_scalar(skip_diag[:, :], ident[:, :], d_skip[:, :], None, ALU.mult).then_inc(skip_sb, 1)
            dve.wait_ge(w_rows_sb, 1)
            V.tensor_tensor(w_dt[:, :], bank(7)[:, 0:P], half_mask[:, :], ALU.mult).then_inc(w1_dve, 1)
            edges(5, 7)
            finish_norm(1, xn[:, :])
            V.tensor_scalar(x1[:, :], xn[:, :], ln_g[:, :], ln_b[:, :], ALU.mult, ALU.add).then_inc(x1_sb, 1)
            dve.wait_ge(x2_ps, 1)
            V.tensor_scalar(x2[:, :], bank(4, 2), ln_g[:, :], ln_b[:, :], ALU.mult,
                            ALU.add).then_inc(x12, 1)
            edges(7, 16)
            link(V.tensor_scalar(k_a, cand, -1.0, None, ALU.add))
            link(V.tensor_scalar(k_b, k_a, CELLS - 1, 13, ALU.bitwise_and, ALU.logical_shift_left))
            link(V.tensor_scalar(k_a, k_a, 13, None, ALU.logical_shift_right))
            link(V.tensor_tensor(k_b, k_b, k_a, ALU.bitwise_or))
            link(V.tensor_tensor(k_b, k_b, seg_bits, ALU.bitwise_or))
            link(V.tensor_scalar(k_a, cand, 0.0, -1.0, ALU.is_gt, ALU.mult))
            link(V.tensor_tensor(k_key, k_b, k_a, ALU.bitwise_and))

            def sort_slots(keys, rounds, link):
                for q in range(rounds):
                    link(V.max(top48[:, 8 * q:8 * q + 8], keys))
                    link(V.match_replace(keys, top48[:, 8 * q:8 * q + 8], keys, 0.0))

            def slot_fields(slots, base, link):
                n = slice(0, slots)
                t = top48[:, n].bitcast(I32)
                link(V.tensor_scalar(d_a[:, n], t, 13, CELLS - 1, ALU.logical_shift_right, ALU.bitwise_and))
                link(V.tensor_scalar(d_b[:, n], t, 8191, None, ALU.bitwise_and))
                link(V.tensor_tensor(d_b[:, n], d_b[:, n], base.to_broadcast([P, slots]), ALU.bitwise_or))
                link(V.tensor_scalar(d_ok[:, n], top48[:, n], 0.0, weight[:, :].bitcast(F32), ALU.is_gt,
                                     ALU.mult))
                link(V.tensor_tensor(d_new[:, 1:slots], d_a[:, 1:slots], d_a[:, 0:slots - 1], ALU.not_equal))
                link(V.tensor_tensor(d_ok[:, 1:slots], d_ok[:, 1:slots], d_new[:, 1:slots], ALU.mult))
                link(V.tensor_copy(weighed[:, n, 0], d_ok[:, n]))
                for k in range(1, PLANES):
                    link(V.tensor_scalar(d_c[:, n], d_b[:, n], SYMBOL * (k - 1), (1 << SYMBOL) - 1,
                                         ALU.logical_shift_right, ALU.bitwise_and))
                    link(V.scalar_tensor_tensor(weighed[:, n, k], d_c[:, n], 1.0, d_ok[:, n], ALU.add, ALU.mult))
                link(V.tensor_scalar(d_row[:, n], d_a[:, n], 5, None, ALU.logical_shift_right))
                link(V.tensor_tensor(d_c[:, n], d_a[:, n], d_row[:, n], ALU.bitwise_xor))
                link(V.tensor_scalar(d_col[:, n], d_c[:, n], C - 1, None, ALU.bitwise_and))
                link(V.tensor_copy(d_at[:, n], d_row[:, n]))
                return V.tensor_tensor(col_hot[:, n, :],
                                       rows_at[:, 0:C].unsqueeze(1).to_broadcast([P, slots, C]),
                                       d_col[:, n].unsqueeze(2).to_broadcast([P, slots, C]), ALU.is_equal)

            def hot_rows(k, q):
                for s_ in range(CHUNK):
                    at = CHUNK * q + s_
                    last = V.tensor_scalar(row_hot[k][:, s_, :], rows_at[:, :], d_at[:, at:at + 1], None,
                                           ALU.is_equal)
                return last

            def table_indices(link):
                link(V.tensor_scalar(tab_i[:, :], tab[:, :], -1.0, 0.0, ALU.add, ALU.max))
                return V.tensor_scalar(hit[:, :, 1, :], tab[:, :].rearrange("p (s c) -> p s c", c=C), 0.0, None,
                                       ALU.is_gt)

            def planes_to_table(dst, base, link):
                weights = ps[:, 4:8, 0:2 * C]
                shares = ps[:, 4:8, 2 * C:2 * C * PLANES].rearrange("p g (k c) -> p g k c", c=2 * C)
                k3_ = PLANES - 1
                link(V.tensor_scalar(inv_i, weights.bitcast(I32), 23, None, ALU.logical_shift_right))
                link(V.tensor_scalar(inv_i, inv_i, -1, 254, ALU.mult, ALU.add))
                link(V.tensor_scalar(inv_i, inv_i, 23, None, ALU.logical_shift_left))
                link(V.tensor_tensor(symbols, shares, inv_i.bitcast(F32).unsqueeze(2)
                                     .to_broadcast([P, G, k3_, 2 * C]), ALU.mult))
                link(V.tensor_scalar(symbols, symbols, -0.25, float(1 << 23), ALU.add, ALU.add))
                link(V.tensor_scalar(symbols, symbols, -float(1 << 23), None, ALU.add))
                number = symbols[:, :, k3_ - 1, :]
                for k in range(k3_ - 2, -1, -1):
                    link(V.scalar_tensor_tensor(number, number, float(1 << SYMBOL), symbols[:, :, k, :],
                                                ALU.mult, ALU.add))
                link(V.tensor_tensor(number, number, base.unsqueeze(2).to_broadcast([P, G, 2 * C]), ALU.add))
                link(V.scalar_tensor_tensor(number, weights, 0.0, number, ALU.is_gt, ALU.mult))
                return V.tensor_reduce(dst, number.rearrange("p g c -> p c g"), AX_X, ALU.max)

            sort_slots(k_key.bitcast(F32), SLOTS // 8, link)
            link(V.tensor_reduce(over[:, 0:1], cand.rearrange("p (s e) -> p s e", e=8)[:, :, 7:8]
                                 .rearrange("p s e -> p (s e)"), AX_X, ALU.max))
            link(V.tensor_reduce(over[:, 1:2], k_key.bitcast(F32), AX_X, ALU.max))
            link(V.tensor_tensor(over[:, 0:1], over[:, 0:1], over[:, 1:2], ALU.max))
            link(V.tensor_scalar(over[:, 0:1], over[:, 0:1], 0.0, None, ALU.is_gt))
            link(V.tensor_scalar(weight[:, :], weight[:, :], 23, None, ALU.logical_shift_left))
            slot_fields(SLOTS, p_base[:, 0:1], link).then_inc(cols_sb, 1)
            dve.wait_ge(cols_sb, 1)
            for q in range(2):
                hot_rows(q, q).then_inc(rows_sb, 1)
            dve.wait_ge(conv0, 2)
            for j in range(J):
                r = slice(j * NT, (j + 1) * NT)
                uj = u_act[:, r].rearrange("p (b t) -> p b t", t=N)
                for k in range(1, 4):
                    ins = V.scalar_tensor_tensor(uj, xi_pad[:, 4 * j:4 * j + 4, k:k + N],
                                                 conv_w[:, k:k + 1], uj, ALU.mult, ALU.add)
                    if k < 3:
                        link(ins)
                ins.then_inc(conv_done, 1)
            dve.wait_ge(hot_used, 1)
            hot_rows(0, 2).then_inc(rows_sb, 1)

            def take_off_1(c, src):
                dve.wait_ge(round_1, c + 1)
                V.scalar_tensor_tensor(rest[c % 2], rounded[c % 2], less_1[:, :], src, ALU.mult,
                                       ALU.add).then_inc(rest_1, 1)

            def take_off_2(c):
                dve.wait_ge(round_2, c + 1)
                j = c // 2
                V.scalar_tensor_tensor(parts[:, c % 2, j * NT:(j + 1) * NT], rounded[c % 2], less_2[:, :],
                                       rest[c % 2], ALU.mult, ALU.add).then_inc(parts_sb, 1)

            for k in range(2):
                take_off_1(k, ps[0:BC, 2 * k:2 * k + 2, :].rearrange("p a b -> p (a b)"))
            for k in range(2):
                take_off_2(k)
            for j in range(J):
                r = slice(j * NT, (j + 1) * NT)
                dve.wait_ge(dt_log, j + 1)
                V.tensor_tensor(dt_act[:, r], dt_act[:, r], dtu[:, r], ALU.add).then_inc(dt_sb, 1)
                dve.wait_ge(dt_sb, j + 1)
                V.tensor_tensor(dtu[:, r], dt_act[:, r], u_act[:, r], ALU.mult).then_inc(dtu_sb, 1)
            dve.wait_ge(planes_ps, 1)
            V.tensor_copy(planes, ps[:, 4:8, 0:N]).then_inc(planes_sb, 1)
            dve.wait_ge(planes_t, 1)
            V.tensor_copy(over_i[:, :], bank(4)[0:1, HALF - 1:HALF]).then_inc(over_sb, 1)
            link(planes_to_table(tab[:, :], g_base[:, 0, :], link))
            table_indices(link).then_inc(tab_dve, 1)
            V.memset(dA[:, :, 0:NT:N], 0.0).then_inc(dA_zero, 1)
            def state_scan(i):
                k = i % 2
                dve.wait_ge(dbu_done, i + 1)
                dve.wait_ge(dA_sb, i + 1)
                if i >= 3:
                    dve.wait_ge(hc_done, i - 2)
                V.tensor_tensor_scan(h_buf[i % 3], dA[:, k, :], dBu[:, k, :], 0.0, ALU.mult,
                                     ALU.add).then_inc(scan_done, 1)

            def gate_group(j):
                r = slice(j * NT, (j + 1) * NT)
                dve.wait_ge(y_ps, S * (j + 1))
                V.tensor_tensor(z_act[:, r], z_act[:, r], bank(6, 2), ALU.mult).then_inc(gated, 1)

            state_scan(0)
            for i in range(J * S):
                j, n = i // S, i % S
                k = i % 2
                if i + 1 < J * S:
                    state_scan(i + 1)
                dve.wait_ge(scan_done, i + 1)
                dve.wait_ge(c_ps, i + 1)
                if i >= 2:
                    dve.wait_ge(y_ps, i - 1)
                V.tensor_tensor(hC[:, k, :], h_buf[i % 3], bank(2, 2), ALU.mult).then_inc(hc_done, 1)
                if n == 0 and j > 0:
                    gate_group(j - 1)
                for q in range(2):
                    if j < J - 1 and n == SPLIT[q] + REST_1:
                        take_off_1(2 * (j + 1) + q, ps[0:BC, 4:6, :].rearrange("p a b -> p (a b)"))
                    if j < J - 1 and n == SPLIT[q] + REST_2:
                        take_off_2(2 * (j + 1) + q)
            gate_group(J - 1)
            dve.wait_ge(dma_w2, n_w2)
            V.transpose(wu_t[:, :], wu_nat[:, :]).then_inc(wu_ready, 1)
            dve.wait_ge(mo_ps, 1)
            link(V.scalar_tensor_tensor(xn[:, :], x1[:, :], s1[:, :], bank(0, 2), ALU.mult, ALU.add))
            V.scalar_tensor_tensor(xn[:, :], x2[:, :], s2[:, :], xn[:, :], ALU.mult,
                                   ALU.add).then_inc(norm_in, 1)
            finish_norm(2, xn[:, :])
            V.tensor_scalar(xn[:, :], xn[:, :], ln_g[:, :], ln_b[:, :], ALU.mult, ALU.add).then_inc(normed, 1)
            dve.wait_ge(wp_ps, 1)
            V.scalar_tensor_tensor(X[:, :], bank(4, 2), b_p[:, :], X[:, :], ALU.add,
                                   ALU.add).then_inc(x_new, 1)

            more = dve.value_load(over_i[0:1, 0:1], min_val=0, max_val=P)
            with dve.If(more > 0):
                flink = chained(dve, gen_frame)
                dve.wait_ge(gathered, 16 * EARLY)
                flink(V.memset(tab[:, :], 0.0))
                GEN = 44
                with dve.Fori(0, EDGES // (P * GW)) as t:
                    inside = [0]

                    def glink(ins):
                        inside[0] += 1
                        ins.then_inc(gen_chain, 1)
                        dve.wait_ge(gen_chain, GEN * t + inside[0])
                        dve.sem_inc(gen_passed, 1)

                    dve.wait_ge(gen_in, 32 * t + 32)
                    glink(V.tensor_tensor(g_x, g_row, g_col, ALU.bitwise_xor))
                    glink(V.scalar_tensor_tensor(g_u, g_x, 8.0, g_row, ALU.mult, ALU.max))
                    glink(V.scalar_tensor_tensor(k_b[:, 0:GW], g_row, float(C), g_x, ALU.mult, ALU.add))
                    glink(V.tensor_scalar(k_b[:, 0:GW], k_b[:, 0:GW], CELLS - 1, 13, ALU.bitwise_and,
                                          ALU.logical_shift_left))
                    glink(V.tensor_copy(k_a[:, 0:GW], rows_at[:, 0:GW]))
                    glink(V.tensor_tensor(k_b[:, 0:GW], k_b[:, 0:GW], k_a[:, 0:GW], ALU.bitwise_or))
                    glink(V.tensor_scalar(k_a[:, 0:GW], g_u, float(N), -1.0, ALU.is_lt, ALU.mult))
                    glink(V.tensor_scalar(k_b[:, 0:GW], k_b[:, 0:GW], 1 << 30, None, ALU.bitwise_or))
                    glink(V.tensor_tensor(k_key[:, 0:GW], k_b[:, 0:GW], k_a[:, 0:GW], ALU.bitwise_and))
                    sort_slots(k_key[:, 0:GW].bitcast(F32), GW // 8, glink)
                    glink(slot_fields(GW, p_base[:, 1:2], glink))
                    hot_rows(0, 0)
                    weigh_planes(V, 0, 0).then_inc(gen_slots, 1)
                    dve.wait_ge(gen_ps, t + 1)
                    V.tensor_copy(planes, ps[:, 4:8, 0:N]).then_inc(gen_sb, 1)
                    dve.wait_ge(gen_t, t + 1)
                    glink(planes_to_table(tab_new[:, :], g_base[:, 1, :], glink))
                    glink(V.tensor_tensor(tab[:, :], tab[:, :], tab_new[:, :], ALU.max))
                    glink(V.tensor_scalar(g_base[:, 1, :], g_base[:, 1, :], float(P * GW), None, ALU.add))
                    dve.sem_inc(gen_done, 1)
                    assert inside[0] == GEN, inside[0]
                table_indices(flink).then_inc(tab_dve, 1)


            def norm(k):
                dve.wait_ge(rstd_sb, k)
                V.tensor_tensor(xn[:, :], bank(0, 2), rstd[:, :], ALU.mult).then_inc(normed, 1)

            norm(3)
            dve.wait_ge(normed, 2)
            dve.wait_ge(alone_zero, 1)
            for g in range(2, G):
                r = slice(C * g, C * g + C)
                V.tensor_copy(alone[r, g, :], xn[r, :]).then_inc(alone_sb, 1)

            def window_scores(u):
                k = u % 2
                s = s2_buf[k]
                seg = s.rearrange("p (s k) -> p s k", k=2 * C)
                dve.wait_ge(s2_ps, u + 1)
                if u >= 2:
                    dve.wait_ge(p2_sb, u - 1)
                V.transpose(s, bank(2 * k, 2)).then_inc(s2_read, 1)
                dve.wait_ge(s2_read, u + 1)
                link(V.tensor_reduce(mx2[:, k, :], seg, AX_X, ALU.max))
                V.tensor_tensor(seg, seg, mx2[:, k, :].unsqueeze(2).to_broadcast([P, 16, 2 * C]),
                                ALU.subtract).then_inc(s2_shifted, 1)
                dve.wait_ge(v2_ps, u + 1)
                if u >= 2:
                    dve.wait_ge(o2_ps, u - 1)
                V.transpose(vm_buf[k], bank(4 + k)).then_inc(v2_sb, 1)

            def window_sums(u):
                k = u % 2
                dve.wait_ge(s2_exp, u + 1)
                link(V.tensor_reduce(sm2[:, k, :], s2_buf[k].rearrange("p (s k) -> p s k", k=2 * C),
                                     AX_X, ALU.add))
                V.reciprocal(sm2[:, k, :], sm2[:, k, :]).then_inc(s2_scale, 1)

            def window_probs(u):
                k = u % 2
                dve.wait_ge(s2_prob, u + 1)
                if u >= 2:
                    dve.wait_ge(o2_ps, u - 1)
                V.transpose(pt_buf[k], s2_buf[k]).then_inc(p2_sb, 1)

            window_scores(0)
            for u in range(1, 16):
                window_sums(u - 1)
                if u >= 2:
                    window_probs(u - 2)
                window_scores(u)
            window_sums(15)
            window_probs(14)
            window_probs(15)
            dve.wait_ge(o2_ps, 16)
            V.scalar_tensor_tensor(X[:, :], bank(6, 2), b_u[:, :], X[:, :], ALU.add,
                                   ALU.add).then_inc(x_new, 1)

            flat3 = lambda t: t[:, :, :].rearrange("p b k -> p (b k)")

            def bias_and_gates():
                dve.wait_ge(bias_in, 16 * 2 * H3)
                dg = diag[:, :].unsqueeze(1).to_broadcast([P, BL, C])
                link(V.memset(wgt[:, :, C:KN], 1.0))
                link(V.memset(msk[:, :, C:KN], 1.0))
                link(V.tensor_tensor(gate3[:, :, :], wgt[:, :, 0:C], dg, ALU.mult))
                link(V.tensor_tensor(wgt[:, :, 0:C], wgt[:, :, 0:C], gate3[:, :, :], ALU.subtract))
                link(V.tensor_tensor(wgt[:, :, 0:C], wgt[:, :, 0:C], dg, ALU.add))
                link(V.tensor_tensor(msk[:, :, 0:C], msk[:, :, 0:C], dg, ALU.max))
                dve.wait_ge(dma_w3, n_w3)
                link(V.tensor_scalar(gate3[:, :, :], wgt[:, :, 0:C], gate_w3[:, :], gate_b3[:, :], ALU.mult,
                                     ALU.add))
                link(V.tensor_tensor(gate3[:, :, :], gate3[:, :, :], msk[:, :, 0:C], ALU.mult))
                link(V.tensor_tensor(node_gate[:, 0:1], gate_w3[:, :], gate_b3[:, :], ALU.add))
                link(V.tensor_scalar(node_gate[:, 0:1], node_gate[:, 0:1], 1.0 / C, None, ALU.mult))
                link(V.tensor_scalar(gate3[:, :, :], gate3[:, :, :], node_gate[:, 0:1], None, ALU.add))
                link(V.tensor_scalar(flat3(msk), flat3(msk), -1.0, 1e30, ALU.add, ALU.mult))
                spread_g = lambda t: t[:, :, :].unsqueeze(2).to_broadcast([P, BL, G, KN])
                link(V.tensor_tensor(added, spread_g(msk), spread_g(wgt), ALU.add))

            norm(4)
            wide8 = lambda t: t[:, :].unsqueeze(2).to_broadcast([P, TT * G, E2])
            ranks = rank[:, :].unsqueeze(1).to_broadcast([P, TT * G, E2])
            dve.wait_ge(lg_ps, 1)
            dve.wait_ge(w2_mask, 1)
            lps = bank(4)[:, 0:TT * G * E2].rearrange("p (t e) -> p t e", e=E2)
            link(V.tensor_copy(lg[:, :, :], lps))

            def pick(sel, values, top):
                link(V.tensor_reduce(top[:, :], values, AX_X, ALU.max))
                link(V.tensor_tensor(sel[:, :, :], values, wide8(top), ALU.is_equal))
                link(V.tensor_tensor(sel[:, :, :], sel[:, :, :], ranks, ALU.mult))
                link(V.tensor_reduce(top2[:, :], sel[:, :, :], AX_X, ALU.max))
                link(V.tensor_tensor(sel[:, :, :], sel[:, :, :], wide8(top2), ALU.is_equal))

            pick(sel_a, lg[:, :, :], top1)
            V.tensor_tensor(gate[:, :, :], lg[:, :, :], wide8(top1), ALU.subtract).then_inc(lg_shifted, 1)
            dve.wait_ge(lg_exp, 1)
            link(V.scalar_tensor_tensor(lg[:, :, :], sel_a[:, :, :], -3e38, lg[:, :, :], ALU.mult, ALU.add))
            pick(sel_b, lg[:, :, :], top1)
            link(V.tensor_tensor(sel_a[:, :, :], sel_a[:, :, :], sel_b[:, :, :], ALU.add))
            link(V.tensor_tensor(gate[:, :, :], gate[:, :, :], sel_a[:, :, :], ALU.mult))
            link(V.tensor_reduce(top1[:, :], gate[:, :, :], AX_X, ALU.add))
            link(V.reciprocal(top1[:, :], top1[:, :]))
            V.tensor_tensor(gate[:, :, :], gate[:, :, :], wide8(top1), ALU.mult).then_inc(gate_sb, 1)
            dve.wait_ge(gate_sb, 1)
            for t in range(TT):
                if t == 4:
                    bias_and_gates()
                dve.wait_ge(ex_ps, t + 1)
                if t >= 2:
                    dve.wait_ge(y2_part, t - 1)
                w = gate[:, G * t:G * t + G, :].unsqueeze(3)
                V.tensor_tensor(mix[t % 2].rearrange("p (e g c) -> p g e c", e=E2, g=G),
                                bank(4 + 2 * (t % 2), 2).rearrange("p (g e c) -> p g e c", g=G, c=C),
                                w.to_broadcast([P, G, E2, C]), ALU.mult).then_inc(ex_sb, 1)
            dve.wait_ge(y2_part, TT)
            V.tensor_tensor(X[:, :], X[:, :], bank(2, 2), ALU.add).then_inc(x_new, 1)

            norm(5)
            dve.wait_ge(qkv3_ps, 1)
            dve.wait_ge(k3_zero, 1)
            keys_ps = bank(6, 2).rearrange("p (s k) -> p s k", k=C)
            link(V.tensor_reduce(mx3[:, 0, :], keys_ps, AX_X, ALU.add))
            for g in range(G):
                r = slice(C * g, C * g + C)
                V.tensor_scalar(k3[r, :, g, 0:C], keys_ps[r, :, :], b_k3[r, :], None, ALU.add)
                last = V.tensor_scalar(k3[r, :, g, C:KN].rearrange("p s k -> p (s k)"), mx3[r, 0, :], 1.0 / C,
                                       b_k3[r, :], ALU.mult, ALU.add)
            last.then_inc(k3_node, 1)
            for jp in range(2):
                dve.wait_ge(v3_sb, jp + 1)
                V.transpose(vm3[jp], v3[jp]).then_inc(vm3_sb, 1)

            def block_scores(j):
                k = j % 2
                two = lambda t: t.rearrange("p (a t) -> p a t", a=4)
                keys = s3[k].rearrange("p (s k) -> p s k", k=KN)
                dve.wait_ge(s3_ps, j + 1)
                V.tensor_tensor(two(s3[k]), ps[:, 4 * k:4 * k + 4, 0:2 * G * KN],
                                two(added.rearrange("p b g k -> p (b g k)")), ALU.add).then_inc(s3_read, 1)
                dve.wait_ge(s3_read, j + 1)
                link(V.tensor_reduce(mx3[:, k, :], keys, AX_X, ALU.max))
                V.tensor_tensor(keys, keys, mx3[:, k, :].unsqueeze(2).to_broadcast([P, G * BL, KN]),
                                ALU.subtract).then_inc(s3_shift, 1)

            def block_probs(j):
                k = j % 2
                keys = s3[k].rearrange("p (s k) -> p s k", k=KN)
                a_ = a3[k].rearrange("p (s k) -> p s k", k=C)
                dve.wait_ge(s3_exp, j + 1)
                link(V.tensor_reduce(sm3[:, k, :], keys, AX_X, ALU.add))
                link(V.reciprocal(sm3[:, k, :], sm3[:, k, :]))
                link(V.tensor_scalar(mx3[:, k, :], keys[:, :, C:KN].rearrange("p s k -> p (s k)"), 1.0 / C, None,
                                     ALU.mult))
                link(V.tensor_tensor(a_, keys[:, :, 0:C], mx3[:, k, :].unsqueeze(2)
                                     .to_broadcast([P, G * BL, C]), ALU.add))
                link(V.tensor_tensor(a_, a_, sm3[:, k, :].unsqueeze(2).to_broadcast([P, G * BL, C]), ALU.mult))
                four = a3[k].rearrange("p (b g k) -> p b g k", g=G, k=C)
                link(V.tensor_tensor(four, four, gate3[:, :, :].unsqueeze(2).to_broadcast([P, BL, G, C]),
                                     ALU.add))
                if j >= 2:
                    dve.wait_ge(o3_ps, j - 1)
                V.transpose(at3[k], a3[k]).then_inc(at3_sb, 1)

            for jp in range(2):
                for j in (2 * jp, 2 * jp + 1):
                    block_scores(j)
                for j in (2 * jp, 2 * jp + 1):
                    block_probs(j)
            dve.wait_ge(p3_ps, 1)
            V.scalar_tensor_tensor(X[:, :], bank(2, 2), b_p3[:, :], X[:, :], ALU.add,
                                   ALU.add).then_inc(x_new, 1)

            dve.wait_ge(rstd_sb, 6)
            link(V.tensor_tensor(h4, bank(0, 2), rstd[:, :], ALU.mult))
            dve.wait_ge(dma_m, 32)
            link(V.tensor_copy(steps_f.rearrange("p t o -> p (t o)"), steps_u8))

            def find_step(link):
                link(V.transpose(h_t, h4[0:C, 0:C]))
                link(V.max(best8[:, :], h_t[0:1, 0:NOPS]))
                link(V.max_index(best8_i[:, :], best8[:, :], h_t[0:1, 0:NOPS]))
                link(V.tensor_copy(op_f[:, :], best8_i[:, 0:1]))
                link(V.tensor_scalar(one_hot[:, :], ops_at[:, :], op_f[:, :], None, ALU.is_equal))
                link(V.tensor_tensor(picked, steps_f, one_hot[:, 0:NOPS].unsqueeze(1)
                                     .to_broadcast([1, 2 * NB, NOPS]), ALU.mult))
                link(V.tensor_reduce(flags[:, :, :].rearrange("p k b -> p (k b)"), picked, AX_X, ALU.max))
                link(V.tensor_tensor(open_[:, :], flags[:, 0, :], flags[:, 1, :], ALU.max))
                link(V.tensor_scalar(one_hot[:, :], ops_at[:, :], from_block[:, :], None, ALU.is_ge))
                link(V.tensor_tensor(open_[:, :], open_[:, :], one_hot[:, :], ALU.mult))
                link(V.tensor_tensor(open_[:, :], open_[:, :], ops_back[:, :], ALU.mult))
                link(V.tensor_reduce(found[:, :], open_[:, :], AX_X, ALU.max))
                link(V.tensor_scalar(next_block[:, :], found[:, :], -1.0, float(NONE), ALU.mult, ALU.add))
                link(V.tensor_scalar(one_hot[:, :], ops_at[:, :], next_block[:, :], None, ALU.is_equal))
                link(V.tensor_tensor(flags[:, :, :], flags[:, :, :], one_hot[:, :].unsqueeze(1)
                                     .to_broadcast([1, 2, NB]), ALU.mult))
                link(V.tensor_reduce(ctrl_f[:, 1:3], flags[:, :, :], AX_X, ALU.max))
                link(V.tensor_scalar(ctrl_f[:, 0:1], found[:, :], 0.0, None, ALU.is_gt))
                link(V.scalar_tensor_tensor(ctrl_f[:, 3:4], next_block[:, :], float(NOPS), op_f[:, :],
                                            ALU.mult, ALU.add))
                link(V.tensor_scalar(ctrl_f[:, 3:4], ctrl_f[:, 3:4], float(STEPS - 1), None, ALU.min))
                link(V.tensor_scalar(from_block[:, :], next_block[:, :], 1.0, None, ALU.add))
                return V.tensor_copy(ctrl[:, :], ctrl_f[:, :])

            FIND = 20
            find_step(link).then_inc(ctrl_ready, 1)

            def counted(chain, base, done):
                def link_(ins):
                    done[0] += 1
                    ins.then_inc(chain, 1)
                    hold(dve, chain, base + done[0])
                return link_

            active = dve.alloc_register("dve_active")
            hold(dve, ctrl_ready, 1)
            dve.reg_load(active, ctrl[0:1, 0:1])
            with dve.Fori(0, ROUNDS) as outer:
                with dve.If_ne(active, 0):
                    with dve.Fori(0, ROUNDS) as inner:
                        i = outer * ROUNDS + inner
                        with dve.If_ne(active, 0):
                            attends = dve.value_load(ctrl[0:1, 1:2], min_val=0, max_val=1)
                            feeds = dve.value_load(ctrl[0:1, 2:3], min_val=0, max_val=1)
                            ATTN_LINKS = 3 * B + 1
                            with dve.If(attends > 0):
                                done = [0]
                                alink = counted(attn_chain, ATTN_LINKS * i, done)
                                hold(dve, attn_pe, ATTN_PE * i + 1)
                                V.tensor_copy(k4, bank(2, 2)).then_inc(attn_dve, 1)
                                for b in range(B):
                                    hold(dve, attn_pe, ATTN_PE * i + 3 + 3 * b)
                                    alink(V.tensor_reduce(mx4, bank(0).rearrange("p (h k) -> p h k", h=2), AX_X,
                                                          ALU.max))
                                    V.tensor_scalar(nm4, mx4, -float(C) ** -0.5, None, ALU.mult).then_inc(attn_dve, 1)
                                    hold(dve, attn_act, ATTN_ACT * i + 3 + b)
                                    alink(V.reciprocal(mx4, sm4))
                                    V.tensor_tensor(p4.rearrange("p (h k) -> p h k", h=2),
                                                    p4.rearrange("p (h k) -> p h k", h=2),
                                                    mx4.unsqueeze(2).to_broadcast([P, 2, N]),
                                                    ALU.mult).then_inc(attn_dve, 1)
                                    hold(dve, attn_pe, ATTN_PE * i + 4 + 3 * b)
                                    alink(V.tensor_copy(pt4, bank(1)))
                                    dve.sem_inc(attn_dve, 1)
                                hold(dve, attn_pe, ATTN_PE * i + 3 + 3 * B)
                                V.tensor_copy(h4, bank(0, 2)).then_inc(attn_dve, 1)
                                hold(dve, attn_dve, ATTN_DVE * i + 2 + 3 * B)
                                V.tensor_copy(mx4, nm4).then_inc(attn_chain, 1)
                                assert done[0] + 1 == ATTN_LINKS
                            with dve.Else():
                                dve.sem_inc(attn_dve, ATTN_DVE)
                                dve.sem_inc(attn_chain, ATTN_LINKS)
                            done = [1]
                            slink = counted(step_chain, (FIND + 1) * i, done)
                            with dve.If(feeds > 0):
                                hold(dve, dma_f, N_STEP * i + N_STEP)
                                hold(dve, ffn_pe, FFN_PE * i + G + 1)
                                V.tensor_scalar(h4, bank(0, 2), b2_4, None, ALU.add).then_inc(step_chain, 1)
                            with dve.Else():
                                dve.sem_inc(step_chain, 1)
                            hold(dve, step_chain, (FIND + 1) * i + 1)
                            find_step(slink).then_inc(ctrl_ready, 1)
                            assert done[0] == FIND + 1, done[0]
                            hold(dve, ctrl_ready, i + 2)
                            dve.reg_load(active, ctrl[0:1, 0:1])
            V.tensor_tensor(X[:, :], X[:, :], h4, ALU.add).then_inc(x_new, 1)

        @block.tensor
        def _(pe):
            T = nc.tensor

            def keep_warm(count, k):
                for _ in range(count):
                    T.matmul(bank(k), zero_bf[:, :], mask_bf[:, :, :].rearrange("p i t -> p (i t)"),
                             start=True, stop=True, skip_group_check=True)

            def both_halves(k, weight, src):
                for h in range(2):
                    last = T.matmul(bank(k + h), weight, src[:, h * HALF:(h + 1) * HALF],
                                    start=True, stop=True)
                return last

            pe.wait_ge(bd0_ready, 1)
            pe.wait_ge(dma_x, 16)
            for k in range(3):
                both_halves(2 * k, bd0[:, k, :], X).then_inc(proj0, 1)
            pe.wait_ge(theta_sb, 1)
            pe.wait_ge(pooled, 2)
            for j in range(J):
                for h in range(2):
                    t = 2 * j + h
                    last = T.matmul(bank(4 + t // 2)[:, N * (t % 2):N * (t % 2) + N],
                                    theta[:, j * N + h * P:j * N + h * P + P],
                                    phi_bd[:, j, :, :].rearrange("p g m -> p (g m)"), start=True, stop=True)
            last.then_inc(logits0, 1)
            for j in range(J):
                for q in range(2):
                    t = 2 * j + q
                    last = T.matmul(bank(t // 4)[:, P * (t % 4):P * (t % 4) + P],
                                    gp_bd[:, j, 2 * q:2 * q + 2, :].rearrange("p g m -> p (g m)"),
                                    wo_bd[:, :], start=True, stop=True)
            last.then_inc(vb_ps, 1)
            pe.wait_ge(prob0, 1)
            pe.wait_ge(vb_sb, 1)
            pe.wait_ge(consts, 2)
            for j in range(J):
                for h in range(2):
                    for q in range(2):
                        at = (2 * j + h) * N + q * P
                        last = T.transpose(bank(j)[:, q * N + h * P:q * N + h * P + P], att[:, at:at + P],
                                           ident[:, :])
            last.then_inc(attT_ps, 1)
            pe.wait_ge(attT_sb, 1)
            for j in range(J):
                for q in range(2):
                    last = T.matmul(bank(4 + j // 2)[:, N * (j % 2):N * (j % 2) + N],
                                    vb[:, (2 * j + q) * P:(2 * j + q + 1) * P],
                                    att_t[:, (2 * j + q) * N:(2 * j + q + 1) * N],
                                    start=(q == 0), stop=(q == 1))
            last.then_inc(o0_ps, 1)

            def channel_norm(k, src):
                pe.wait_ge(norm_in, k)
                both_halves(0, centerer[:, :], src).then_inc(centred, 1)
                pe.wait_ge(squared, k)
                both_halves(2, averager[:, :], sq).then_inc(variance, 1)

            pe.wait_ge(dma_w1, n_w1)
            flat = lambda t: t[:, :, :].rearrange("p a b -> p (a b)")
            T.matmul(bank(7)[:, 0:P], flat(wx_rows), flat(wdt_t), start=True, stop=True).then_inc(wdt_ps, 1)
            channel_norm(1, xn)
            pe.wait_ge(x1_sb, 1)
            both_halves(4, permuter[:, :], xn).then_inc(x2_ps, 1)
            pe.wait_ge(x12, 1)
            pe.wait_ge(w1_dve, 1)
            for i in range(8):
                g, jp = i // 2, i % 2
                k = 4 * (i % 2)
                r = slice(C * g, C * g + C)
                if i >= 2:
                    pe.wait_ge(xi_used, i - 1)
                    pe.wait_ge(z_used, i - 1)
                for part in range(2):
                    for v, src in ((0, x1), (1, x2)):
                        last = T.matmul(bank(k + part)[64 * v:64 * v + 64, :],
                                        win_t[r, 64 * part:64 * part + 64],
                                        src[r, jp * HALF:(jp + 1) * HALF], start=True, stop=True)
                    last.then_inc(xz_ps, 1)

            def clear_planes():
                for g in range(G):
                    r = slice(C * g, C * g + C)
                    last = T.matmul(bank(4 + g)[:, 0:2 * P], zero_bf[r, :],
                                    zero_bf[r, :].unsqueeze(1).to_broadcast([C, 2, P]), start=True,
                                    stop=False, skip_group_check=True)
                return last

            def put_chunk(k, ends):
                for s_ in range(CHUNK):
                    for g in range(G):
                        r = slice(C * g, C * g + C)
                        last = T.matmul(bank(4 + g)[:, 0:N], plane_hot[k][r, s_, :, :].rearrange("p k c -> p (k c)"),
                                        row_hot[k][r, s_, :], start=False, stop=(ends and s_ == CHUNK - 1),
                                        skip_group_check=True)
                return last

            def turn_planes():
                for g in range(G):
                    for h in range(2):
                        last = T.transpose(
                            bank(4 + g)[:, 0:2 * P].rearrange("p (k h c) -> p k h c", h=2, c=C)[:, :, h, :],
                            planes[:, g, h * P:(h + 1) * P], ident[:, :])
                return last

            pe.wait_ge(xi_used, 8)
            pe.wait_ge(z_used, 8)
            pe.wait_ge(consts, 2)
            clear_planes()
            pe.wait_ge(cols_sb, 1)
            T.matmul(bank(4)[0:1, HALF - 1:HALF], over[:, 0:1], one_col[:, :], start=True, stop=True,
                     skip_group_check=True)
            def take_chunk(q):
                pe.wait_ge(rows_sb, q + 1)
                pe.wait_ge(hot_sb, q + 1)
                ends = q == SLOTS // CHUNK - 1
                put_chunk(q % 2, ends).then_inc(planes_ps if ends else hot_used, 1)

            def compact(k, j, to):
                for h in range(2):
                    last = T.matmul(bank(to + h)[0:BC, :],
                                    w_rows[:, k, :, :, :].rearrange("p a v n -> p (a v n)"),
                                    u_act[:, j * NT + h * HALF:j * NT + (h + 1) * HALF], start=True, stop=True)
                last.then_inc(compact_ps, 1)

            for q in range(SLOTS // CHUNK - 1):
                take_chunk(q)
            pe.wait_ge(u_sb, J)
            for k in range(2):
                compact(k, 0, 2 * k)
            for j in range(J):
                if j < 2:
                    pe.wait_ge(rest_1, j + 1)
                else:
                    pe.wait_ge(dt_parts, j - 1)
                both_halves(2 * (j % 2), w_dt[:, :], u_act[:, j * NT:(j + 1) * NT]).then_inc(dt_ps, 1)
            take_chunk(SLOTS // CHUNK - 1)
            pe.wait_ge(planes_sb, 1)
            turn_planes().then_inc(planes_t, 1)
            pe.wait_ge(dt_parts, J)

            def spread(k, i, to):
                j, n = i // S, i % S
                pe.wait_ge(parts_sb, 2 * j + k + 1)
                for h in range(2):
                    last = T.matmul(bank(to + h), pick_state[:, n, :, :].rearrange("p v i -> p (v i)"),
                                    parts[:, k, j * NT + h * HALF:j * NT + (h + 1) * HALF],
                                    start=True, stop=True)
                return last

            def add_state(i):
                j, n = i // S, i % S
                if i == 0:
                    pe.wait_ge(tab_dve, 1)
                if n == 0:
                    if j > 0:
                        pe.wait_ge(gated, j)
                    for h in range(2):
                        T.matmul(bank(6 + h), skip_diag[:, :],
                                 u_act[:, j * NT + h * HALF:j * NT + (h + 1) * HALF], start=True, stop=False)
                pe.wait_ge(hc_done, i + 1)
                for h in range(2):
                    last = T.matmul(bank(6 + h), ident[:, :], hC[:, i % 2, h * HALF:(h + 1) * HALF],
                                    start=False, stop=(n == S - 1))
                last.then_inc(y_ps, 1)

            AHEAD = 3
            for i in range(-AHEAD, J * S):
                j, n = i // S, i % S
                if i + AHEAD < J * S:
                    if i + AHEAD > 0:
                        pe.wait_ge(b_copied, i + AHEAD)
                    spread(0, i + AHEAD, 0).then_inc(b_ps, 1)
                if i < 0:
                    continue
                if i >= 1:
                    pe.wait_ge(hc_done, i)
                spread(1, i, 2).then_inc(c_ps, 1)
                if i >= 1:
                    add_state(i - 1)
                for k in range(2):
                    if j < J - 1 and n == SPLIT[k]:
                        if j + k > 0:
                            pe.wait_ge(rest_1, 2 * (j + 1) + k)
                        compact(k, j + 1, 4)
            add_state(J * S - 1)
            pe.wait_ge(gated, J)
            for b in range(B):
                j, g = b // G, b % G
                last = T.matmul(bank(j // 2)[C * g:C * g + C, N * (j % 2):N * (j % 2) + N], wout_t[:, :],
                                z_act[:, b * N:(b + 1) * N], start=True, stop=True)
            last.then_inc(mo_ps, 1)
            channel_norm(2, xn)
            pe.wait_ge(dma_w2, n_w2)
            pe.wait_ge(wu_ready, 1)
            for h in range(H2):
                for g in range(G):
                    r = slice(C * g, C * g + C)
                    T.matmul(bank(6)[r, C * h:C * h + C], wk2[:, h, :], wq2[:, h, :], start=True, stop=True)
                    last = T.matmul(bank(7)[r, C * h:C * h + C], wv2[:, h, :], wu_t[:, C * h:C * h + C],
                                    start=True, stop=True)
            last.then_inc(w2_ps, 1)
            pe.wait_ge(normed, 1)
            both_halves(4, bd0[:, 3, :], xn).then_inc(wp_ps, 1)

            def stream_norm(k, news, free):
                pe.wait_ge(x_new, news)
                both_halves(0, centerer[:, :], X).then_inc(centred, 1)
                keep_warm(4, free)
                pe.wait_ge(squared, k)
                both_halves(2, averager[:, :], sq).then_inc(variance, 1)
                keep_warm(12, free)

            pe.wait_ge(over_sb, 1)
            more = pe.value_load(over_i[0:1, 0:1], min_val=0, max_val=P)
            with pe.If(more > 0):
                pe.wait_ge(w2_sb, 1)
                with pe.Fori(0, EDGES // (P * GW)) as t:
                    pe.wait_ge(gen_slots, t + 1)
                    pe.sem_inc(gen_passed, 1)
                    clear_planes()
                    put_chunk(0, True).then_inc(gen_ps, 1)
                    pe.wait_ge(gen_sb, t + 1)
                    turn_planes().then_inc(gen_t, 1)
                pe.wait_ge(gen_done, EDGES // (P * GW))
            pe.wait_ge(w2_mask, 1)
            stream_norm(3, 2, 4)
            pe.wait_ge(normed, 2)
            pe.wait_ge(w2_sb, 1)
            for h in range(H2):
                if h >= 4:
                    pe.wait_ge(km_sb, h - 3)
                both_halves(2 * (h % 4), w_km[:, h, :], xn).then_inc(km_ps, 1)
            pe.wait_ge(km_sb, H2)
            pe.wait_ge(w2_mask, 1)
            pe.wait_ge(alone_sb, G)
            for k in range(2):
                T.matmul(bank(6 + k), zero_bf[:, :], mask_bf[:, :, :].rearrange("p i t -> p (i t)"),
                         start=True, stop=False, skip_group_check=True)

            def unit(u):
                return u // 4, u // 2 % 2, u % 2

            def unit_scores(u):
                g, jp, hg = unit(u)
                k = u % 2
                if u >= 2:
                    pe.wait_ge(s2_read, u - 1)
                for d in range(2):
                    j = 2 * jp + d
                    sb_ = bank(2 * k + d)
                    keep_warm(3, 2 * k + d)
                    T.matmul(sb_, ident_bf[:, :], mask_bf[:, :, :].rearrange("p i t -> p (i t)"),
                             start=True, stop=False, skip_group_check=True)
                    for m in range(WT):
                        width = 2 * C if m < WT - 1 else C
                        q0 = j * N + m * C
                        last = T.matmul(sb_[:, 2 * C * m + C:2 * C * m + C + width],
                                        km[:, j * WT + m, 4 * hg:4 * hg + 4, :].rearrange("p h k -> p (h k)"),
                                        alone[:, g, q0:q0 + width],
                                        start=False, stop=(m == WT - 1), skip_group_check=True)
                last.then_inc(s2_ps, 1)
                if u >= 2:
                    pe.wait_ge(v2_sb, u - 1)
                T.matmul(bank(4 + k), w_vu[:, 4 * hg * C:4 * (hg + 1) * C],
                         alone[:, g, jp * HALF:(jp + 1) * HALF], start=True, stop=True).then_inc(v2_ps, 1)

            def unit_output(u):
                g, jp, hg = unit(u)
                r = slice(C * g, C * g + C)
                k = u % 2
                pe.wait_ge(p2_sb, u + 1)
                pe.wait_ge(v2_sb, u + 1)
                for d in range(2):
                    for m in range(WT):
                        width = 2 * C if m < WT - 1 else C
                        q0 = d * N + m * C
                        p0 = d * HALF + 2 * C * m + C
                        last = T.matmul(bank(6 + jp)[r, q0:q0 + width],
                                        vm_buf[k][:, d * N + m * C:d * N + m * C + C],
                                        pt_buf[k][:, p0:p0 + width], start=False,
                                        stop=(u == 15 and m == WT - 1), skip_group_check=True)
                last.then_inc(o2_ps, 1)

            for u in range(16):
                unit_scores(u)
                if u >= 2:
                    unit_output(u - 2)
            unit_output(14)
            unit_output(15)

            stream_norm(4, 3, 4)
            pe.wait_ge(normed, 3)
            rb = rb_row[:, :, :].rearrange("p g e -> p (g e)")
            pe.wait_ge(dma_ex, n_ex)
            ebd = e_bd[:, :, :].rearrange("p g e -> p (g e)")
            for t in range(TT):
                o = bank(4)[:, t * G * E2:(t + 1) * G * E2]
                T.matmul(o, one_row[:, :], rb, start=True, stop=False)
                last = T.matmul(o, xn[:, t * P:t * P + P], r_bd[:, :, :].rearrange("p g e -> p (g e)"),
                                start=False, stop=True)
            last.then_inc(lg_ps, 1)

            def combine(t):
                o = bank(2 + t // 4)[:, P * (t % 4):P * (t % 4) + P]
                T.matmul(o, eb_bd, gate_t[:, t * P:t * P + P], start=True, stop=False)
                pe.wait_ge(ex_sb, t + 1)
                for e in range(E2):
                    last = T.matmul(o, mix[t % 2][:, P * e:P * e + P], ident[:, :], start=False,
                                    stop=(e == E2 - 1))
                last.then_inc(y2_part, 1)

            for t in range(TT):
                if t == 0:
                    pe.wait_ge(lg_shifted, 1)
                if t >= 2:
                    pe.wait_ge(ex_sb, t - 1)
                for k in range(2):
                    o = bank(4 + 2 * (t % 2) + k)
                    last = T.matmul(o, xn[:, t * P:t * P + P], ebd[:, k * HALF:(k + 1) * HALF], start=True,
                                    stop=True)
                last.then_inc(ex_ps, 1)
                if t == 1:
                    pe.wait_ge(gate_sb, 1)
                    for q in range(TT):
                        last = T.transpose(bank(q // 4)[0:G * E2, P * (q % 4):P * (q % 4) + P],
                                           gate[:, G * q:G * q + G, :].rearrange("p g e -> p (g e)"), ident[:, :])
                    last.then_inc(gate_ps, 1)
                    pe.wait_ge(gate_copied, 1)
                if t >= 1:
                    combine(t - 1)
            combine(TT - 1)

            stream_norm(5, 4, 7)
            pe.wait_ge(normed, 4)
            pe.wait_ge(dma_w3, n_w3)
            both_halves(4, w_q3[:, :], xn)
            both_halves(6, w_k3[:, :], xn).then_inc(qkv3_ps, 1)
            for jp in range(2):
                if jp == 1:
                    pe.wait_ge(q3_sb, 1)
                    pe.wait_ge(k3_node, 1)
                for g in range(G):
                    last = T.matmul(bank(4 * jp + g), w_v3[C * g:C * g + C, :, :].rearrange("p h c -> p (h c)"),
                                    xn[C * g:C * g + C, jp * HALF:(jp + 1) * HALF], start=True, stop=True)
                last.then_inc(v3_ps, 1)

            def block_scores(j):
                k = j % 2
                for b in range(BL):
                    at = b % 2 * G * KN
                    last = T.matmul(bank(4 * k + b // 2)[:, at:at + G * KN],
                                    q3[:, j * BL + b, :, :].rearrange("p h q -> p (h q)"),
                                    k3[:, j * BL + b, :, :].rearrange("p g k -> p (g k)"), start=True,
                                    stop=True)
                last.then_inc(s3_ps, 1)

            def block_output(j):
                k = j % 2
                pe.wait_ge(at3_sb, j + 1)
                for g in range(G):
                    for b in range(BL):
                        v0 = (2 * g + j % 2) * N + b * C
                        last = T.matmul(bank(4 * k)[C * g:C * g + C, b * C:b * C + C],
                                        vm3[j // 2][:, v0:v0 + C],
                                        at3[k][:, (b * G + g) * C:(b * G + g + 1) * C],
                                        start=True, stop=True)
                last.then_inc(o3_ps, 1)

            pe.wait_ge(k3_node, 1)
            for j in range(J):
                if j < 2:
                    pe.wait_ge(v3_sb, j + 1)
                if j >= 2:
                    pe.wait_ge(o3_sb, j - 1)
                block_scores(j)
                if j % 2 == 0:
                    pe.wait_ge(vm3_sb, j // 2 + 1)
                if j >= 1:
                    block_output(j - 1)
            block_output(J - 1)
            pe.wait_ge(o3_sb, J)
            both_halves(2, w_p3[:, :], o3).then_inc(p3_ps, 1)

            stream_norm(6, 5, 7)

            def per_batch(k, weight, src):
                for g in range(G):
                    r = slice(C * g, C * g + C)
                    for h in range(2):
                        last = T.matmul(bank(k + h)[r, :], weight[r, :], src[r, h * HALF:(h + 1) * HALF],
                                        start=True, stop=True)
                return last

            active = pe.alloc_register("pe_active")
            hold(pe, ctrl_ready, 1)
            pe.reg_load(active, ctrl[0:1, 0:1])
            with pe.Fori(0, ROUNDS) as outer:
                with pe.If_ne(active, 0):
                    with pe.Fori(0, ROUNDS) as inner:
                        i = outer * ROUNDS + inner
                        with pe.If_ne(active, 0):
                            attends = pe.value_load(ctrl[0:1, 1:2], min_val=0, max_val=1)
                            feeds = pe.value_load(ctrl[0:1, 2:3], min_val=0, max_val=1)
                            with pe.If(attends > 0):
                                hold(pe, dma_fa, N_STEP * i + N_STEP)
                                per_batch(0, w4[:, 0, :], h4)
                                per_batch(2, w4[:, 1, :], h4).then_inc(attn_pe, 1)
                                for g in range(G):
                                    r = slice(C * g, C * g + C)
                                    for t in range(TT):
                                        last = T.matmul(bank(4 + g)[:, t * C:(t + 1) * C], h4[r, t * P:(t + 1) * P],
                                                        w4[r, 2, :], start=True, stop=True)
                                last.then_inc(attn_pe, 1)
                                hold(pe, attn_act, ATTN_ACT * i + 2)
                                hold(pe, attn_dve, ATTN_DVE * i + 1)
                                for b in range(B):
                                    g, j = b // J, b % J
                                    r = slice(C * g, C * g + C)
                                    for h in range(2):
                                        q0 = j * N + h * P
                                        last = T.matmul(bank(0)[:, h * N:(h + 1) * N], q4[r, q0:q0 + P],
                                                        k4[r, j * N:(j + 1) * N], start=True, stop=True)
                                    last.then_inc(attn_pe, 1)
                                    hold(pe, attn_dve, ATTN_DVE * i + 3 + 3 * b)
                                    for kh in range(2):
                                        for qh in range(2):
                                            last = T.transpose(bank(1)[:, kh * N + qh * P:kh * N + qh * P + P],
                                                               p4[:, qh * N + kh * P:qh * N + kh * P + P],
                                                               ident[:, :])
                                    last.then_inc(attn_pe, 1)
                                    hold(pe, attn_dve, ATTN_DVE * i + 4 + 3 * b)
                                    for kh in range(2):
                                        v0 = ((g * J + j) * 2 + kh) * C
                                        last = T.matmul(bank(2 + j // 2)[r, (j % 2) * N:(j % 2) * N + N],
                                                        v4[:, v0:v0 + C], pt4[:, kh * N:(kh + 1) * N],
                                                        start=(kh == 0), stop=(kh == 1))
                                    last.then_inc(attn_pe, 1)
                                hold(pe, attn_act, ATTN_ACT * i + 3 + B)
                                per_batch(0, w4[:, 3, :], y4).then_inc(attn_pe, 1)
                            with pe.Else():
                                pe.sem_inc(attn_pe, ATTN_PE)
                            with pe.If(feeds > 0):
                                keep_warm(14, 7)
                                hold(pe, dma_f, N_STEP * i + N_STEP)
                                hold(pe, attn_dve, ATTN_DVE * i + ATTN_DVE)
                                for g in range(G):
                                    r = slice(C * g, C * g + C)
                                    for h in range(2):
                                        last = T.matmul(bank(2 * g + h), w1_4[r, :], h4[r, h * HALF:(h + 1) * HALF],
                                                        start=True, stop=True)
                                    last.then_inc(ffn_pe, 1)
                                for g in range(G):
                                    hold(pe, ffn_act, G * i + g + 1)
                                    for h in range(2):
                                        last = T.matmul(bank(h)[C * g:C * g + C, :], w2_4,
                                                        hid[:, g * NT + h * HALF:g * NT + (h + 1) * HALF],
                                                        start=True, stop=True)
                                last.then_inc(ffn_pe, 1)
                            with pe.Else():
                                pe.sem_inc(ffn_pe, FFN_PE)
                            hold(pe, ctrl_ready, i + 2)
                            pe.reg_load(active, ctrl[0:1, 0:1])


_INS = [
    'x', 'L0_conv_w_theta', 'L0_conv_w_phi', 'L0_conv_w_g',
    'L0_conv_w_o', 'L0_conv_gamma', 'L1_conv_gamma', 'L1_conv_beta',
    'L1_conv_W_in', 'L1_conv_conv_w', 'L1_conv_conv_b', 'L1_conv_W_x',
    'L1_conv_W_dt', 'L1_conv_b_dt', 'L1_conv_A_log', 'L1_conv_D_skip',
    'L1_conv_W_out', 'L1_conv_W_p', 'L1_conv_b_p', 'L1_conv_s1',
    'L1_conv_s2', 'L2_attn_Wq', 'L2_attn_Wk', 'L2_attn_Wv',
    'L2_attn_Wu', 'L2_attn_bu', 'L2_ffn_router_w', 'L2_ffn_router_b',
    'L2_ffn_expert_w', 'L2_ffn_expert_b', 'L3_attn_edge_index', 'L3_attn_edge_values',
    'L3_attn_qkv_w', 'L3_attn_qkv_b', 'L3_attn_proj_w', 'L3_attn_proj_b',
    'L3_attn_gate_w', 'L3_attn_gate_b', 'L3_ffn_ffn_w1', 'L3_ffn_ffn_b1',
    'L3_ffn_ffn_w2', 'L3_ffn_ffn_b2', 'L3_ffn_wq', 'L3_ffn_wk',
    'L3_ffn_wv', 'L3_ffn_wo', 'L3_ffn_attn_mask', 'L3_ffn_ffn_mask']
_OUT = (16, 32, 16, 16)


def kernel(**inputs):
    import numpy as _np
    import concourse.bacc as _bacc
    from concourse import mybir as _mybir
    from concourse.bass_utils import run_bass_kernel_spmd as _run

    nc = _bacc.Bacc("TRN2", target_bir_lowering=False, num_devices=1)
    arrays, aps = {}, {}
    for name in _INS:
        a = _np.ascontiguousarray(inputs[name])
        arrays[f"in_{name}"] = a
        aps[name] = nc.dram_tensor(f"in_{name}", a.shape, _mybir.dt.from_np(a.dtype), kind="ExternalInput").ap()
    out = nc.dram_tensor("out_0", _OUT, _mybir.dt.float32, kind="ExternalOutput").ap()
    hybrid_kernel(nc, aps, out)
    r = _run(nc, [arrays], core_ids=[0])
    return r.results[0]["out_0"]
```
